# Optimizing a Trainium2 kernel written in Bass

```python
import numpy as np
import jax
import jax.numpy as jnp

def _softmax(x, axis=-1):
    return jax.nn.softmax(x, axis=axis)

def _gelu(x):
    return jax.nn.gelu(x, approximate=True)

def _silu(x):
    return jax.nn.silu(x)

def _sigmoid(x):
    return jax.nn.sigmoid(x)

def _layernorm(x, axis=-1, eps=1e-05):
    m = jnp.mean(x, axis=axis, keepdims=True)
    v = jnp.var(x, axis=axis, keepdims=True)
    return (x - m) / jnp.sqrt(v + eps)

def _scatter_add(tgt, idx, src, axis=0):
    return tgt.at[idx].add(src)

def _segment_sum(src, seg, n):
    return jax.ops.segment_sum(src, seg, n)
kernel_name = 'mk_vit_tower_d2_tok_img1024_r4_29be0b'

def setup_inputs(seed: int=0):
    np.random.seed(seed)
    _w = jnp.asarray

    def _rec_inputs():
        import jax
        import jax.numpy as jnp
        _rk = jax.random.key(seed)
        x = -0.000125008 + 0.999885 * jax.random.normal(jax.random.fold_in(_rk, 1), (4, 512, 256, 4), jnp.float32)
        return x
    x = _rec_inputs()

    def _L0_tok_setup():
        import jax, jax.numpy as jnp
        import numpy as np
        key = jax.random.key(seed)
        k1, k2, k3 = jax.random.split(key, 3)
        B, H, I, O, Dp1 = (4, 512, 256, 256, 4)
        x = jax.random.normal(k1, (B, H, I, Dp1), dtype=jnp.float32)
        weight = 0.1 * jax.random.normal(k2, (O, Dp1), dtype=jnp.float32)
        weighted_sum = 0.1 * jax.random.normal(k3, (O, I), dtype=jnp.float32)
        return {'x': x, 'weight': weight, 'weighted_sum': weighted_sum}
    _L0_tok_all = _L0_tok_setup()
    _L0_tok_in = {k: v for k, v in _L0_tok_all.items() if k in ('weight', 'weighted_sum')}
    del _L0_tok_all

    def _L0_attn_setup():
        import jax, jax.numpy as jnp
        import numpy as np
        B, S, H, NH = (1, 1024, 256, 16)
        DH = H // NH

        def _split_heads(x):
            b, s, h = x.shape
            return jnp.transpose(x.reshape(b, s, NH, DH), (0, 2, 1, 3))
        key = jax.random.key(seed)
        ks = jax.random.split(key, 9)
        sc = 0.02
        return {'queries': jax.random.normal(ks[0], (B, S, H), jnp.float32), 'keys': jax.random.normal(ks[1], (B, S, H), jnp.float32), 'values': jax.random.normal(ks[2], (B, S, H), jnp.float32), 'Wq_w': jax.random.normal(ks[3], (H, H), jnp.float32) * sc, 'Wq_b': jax.random.normal(ks[4], (H,), jnp.float32) * sc, 'Wk_w': jax.random.normal(ks[5], (H, H), jnp.float32) * sc, 'Wk_b': jax.random.normal(ks[6], (H,), jnp.float32) * sc, 'Wv_w': jax.random.normal(ks[7], (H, H), jnp.float32) * sc, 'Wv_b': jax.random.normal(ks[8], (H,), jnp.float32) * sc}
    _L0_attn_all = _L0_attn_setup()
    _L0_attn_in = {k: v for k, v in _L0_attn_all.items() if k in ('keys', 'values', 'Wq_w', 'Wq_b', 'Wk_w', 'Wk_b', 'Wv_w', 'Wv_b')}
    del _L0_attn_all

    def _L0_ffn_setup():
        import jax, jax.numpy as jnp
        import numpy as np

        def _binarize(w):
            alpha = jax.lax.stop_gradient(jnp.mean(jnp.abs(w), axis=1, keepdims=True))
            bw = alpha * jnp.sign(w)
            return w + jax.lax.stop_gradient(bw - w)
        key = jax.random.key(seed)
        k1, k2, k3, k4, k5 = jax.random.split(key, 5)
        D, H = (256, 1024)
        x = jax.random.normal(k1, (64, 196, D), dtype=jnp.float32)
        w1 = jax.random.normal(k2, (H, D), dtype=jnp.float32) * 0.02
        b1 = jax.random.normal(k3, (H,), dtype=jnp.float32) * 0.02
        w2 = jax.random.normal(k4, (D, H), dtype=jnp.float32) * 0.02
        b2 = jax.random.normal(k5, (D,), dtype=jnp.float32) * 0.02
        return {'x': x, 'w1': w1, 'b1': b1, 'w2': w2, 'b2': b2}
    _L0_ffn_all = _L0_ffn_setup()
    _L0_ffn_in = {k: v for k, v in _L0_ffn_all.items() if k in ('w1', 'b1', 'w2', 'b2')}
    del _L0_ffn_all

    def _L1_attn_setup():
        import math
        import jax, jax.numpy as jnp
        import numpy as np
        E = 256
        H = 16
        D = E // H

        def _l2norm(t, eps=1e-12):
            n = jnp.sqrt(jnp.sum(t * t, axis=-1, keepdims=True))
            return t / jnp.maximum(n, eps)
        key = jax.random.key(seed)
        ks = jax.random.split(key, 10)
        s = 0.02
        x = jax.random.normal(ks[0], (2, 1024, E), dtype=jnp.float32)
        Wq = jax.random.normal(ks[1], (E, E), dtype=jnp.float32) * s
        Wk = jax.random.normal(ks[2], (E, E), dtype=jnp.float32) * s
        Wv = jax.random.normal(ks[3], (E, E), dtype=jnp.float32) * s
        Walpha = jax.random.normal(ks[4], (E, H), dtype=jnp.float32) * s
        Wbeta = jax.random.normal(ks[5], (E, H), dtype=jnp.float32) * s
        A_log = jnp.linspace(0.0, math.log(16.0), H).astype(jnp.float32)
        dt_bias = jnp.zeros((H,), dtype=jnp.float32)
        Wgate = jax.random.normal(ks[6], (E, E), dtype=jnp.float32) * s
        Wout = jax.random.normal(ks[7], (E, E), dtype=jnp.float32) * s
        rms_w = jnp.ones((D,), dtype=jnp.float32)
        return {'x': x, 'Wq': Wq, 'Wk': Wk, 'Wv': Wv, 'Walpha': Walpha, 'Wbeta': Wbeta, 'A_log': A_log, 'dt_bias': dt_bias, 'Wgate': Wgate, 'Wout': Wout, 'rms_w': rms_w}
    _L1_attn_all = _L1_attn_setup()
    _L1_attn_in = {k: v for k, v in _L1_attn_all.items() if k in ('Wq', 'Wk', 'Wv', 'Walpha', 'Wbeta', 'A_log', 'dt_bias', 'Wgate', 'Wout', 'rms_w')}
    del _L1_attn_all

    def _L1_ffn_setup():
        import jax, jax.numpy as jnp
        import numpy as np
        B, S, DIM, FFN, E = (4, 512, 256, 1024, 8)
        key = jax.random.key(seed)
        k0, k1, k2, k3 = jax.random.split(key, 4)
        scale = 0.02
        return {'hidden_states': jax.random.normal(k0, (B, S, DIM), jnp.float32), 'router_w': jax.random.normal(k1, (DIM, E), jnp.float32) * scale, 'router_b': jnp.zeros((E,), jnp.float32), 'w1': jax.random.normal(k2, (E, DIM, 2 * FFN), jnp.float32) * scale, 'w2': jax.random.normal(k3, (E, FFN, DIM), jnp.float32) * scale}
    _L1_ffn_all = _L1_ffn_setup()
    _L1_ffn_in = {k: v for k, v in _L1_ffn_all.items() if k in ('router_w', 'router_b', 'w1', 'w2')}
    del _L1_ffn_all
    return {'x': x, 'L0_tok_weight': _L0_tok_in['weight'], 'L0_tok_weighted_sum': _L0_tok_in['weighted_sum'], 'L0_attn_keys': _L0_attn_in['keys'], 'L0_attn_values': _L0_attn_in['values'], 'L0_attn_Wq_w': _L0_attn_in['Wq_w'], 'L0_attn_Wq_b': _L0_attn_in['Wq_b'], 'L0_attn_Wk_w': _L0_attn_in['Wk_w'], 'L0_attn_Wk_b': _L0_attn_in['Wk_b'], 'L0_attn_Wv_w': _L0_attn_in['Wv_w'], 'L0_attn_Wv_b': _L0_attn_in['Wv_b'], 'L0_ffn_w1': _L0_ffn_in['w1'], 'L0_ffn_b1': _L0_ffn_in['b1'], 'L0_ffn_w2': _L0_ffn_in['w2'], 'L0_ffn_b2': _L0_ffn_in['b2'], 'L1_attn_Wq': _L1_attn_in['Wq'], 'L1_attn_Wk': _L1_attn_in['Wk'], 'L1_attn_Wv': _L1_attn_in['Wv'], 'L1_attn_Walpha': _L1_attn_in['Walpha'], 'L1_attn_Wbeta': _L1_attn_in['Wbeta'], 'L1_attn_A_log': _L1_attn_in['A_log'], 'L1_attn_dt_bias': _L1_attn_in['dt_bias'], 'L1_attn_Wgate': _L1_attn_in['Wgate'], 'L1_attn_Wout': _L1_attn_in['Wout'], 'L1_attn_rms_w': _L1_attn_in['rms_w'], 'L1_ffn_router_w': _L1_ffn_in['router_w'], 'L1_ffn_router_b': _L1_ffn_in['router_b'], 'L1_ffn_w1': _L1_ffn_in['w1'], 'L1_ffn_w2': _L1_ffn_in['w2']}

def reference(x, L0_tok_weight, L0_tok_weighted_sum, L0_attn_keys, L0_attn_values, L0_attn_Wq_w, L0_attn_Wq_b, L0_attn_Wk_w, L0_attn_Wk_b, L0_attn_Wv_w, L0_attn_Wv_b, L0_ffn_w1, L0_ffn_b1, L0_ffn_w2, L0_ffn_b2, L1_attn_Wq, L1_attn_Wk, L1_attn_Wv, L1_attn_Walpha, L1_attn_Wbeta, L1_attn_A_log, L1_attn_dt_bias, L1_attn_Wgate, L1_attn_Wout, L1_attn_rms_w, L1_ffn_router_w, L1_ffn_router_b, L1_ffn_w1, L1_ffn_w2):
    import jax
    import jax.numpy as jnp

    def _L0_tok_ref(x, weight, weighted_sum):
        import jax, jax.numpy as jnp
        import numpy as np
        return jnp.einsum('bhid,oi,od->bho', x, weighted_sum, weight)

    def _L0_attn_ref(queries, keys, values, Wq_w, Wq_b, Wk_w, Wk_b, Wv_w, Wv_b):
        import jax, jax.numpy as jnp
        import numpy as np
        B, S, H, NH = (1, 1024, 256, 16)
        DH = H // NH

        def _split_heads(x):
            b, s, h = x.shape
            return jnp.transpose(x.reshape(b, s, NH, DH), (0, 2, 1, 3))
        q = jax.nn.relu(queries @ Wq_w.T + Wq_b)
        k = jax.nn.relu(keys @ Wk_w.T + Wk_b)
        v = jax.nn.relu(values @ Wv_w.T + Wv_b)
        qh, kh, vh = (_split_heads(q), _split_heads(k), _split_heads(v))
        score = jnp.einsum('bhsd,bhtd->bhst', qh, kh) / jnp.sqrt(jnp.float32(DH))
        attn = jax.nn.softmax(score, axis=-1)
        a = jnp.einsum('bhst,bhtd->bhsd', attn, vh)
        a = jnp.transpose(a, (0, 1, 3, 2)).reshape(q.shape[0], q.shape[1], q.shape[2])
        return a + queries

    def _L0_ffn_ref(x, w1, b1, w2, b2):
        import jax, jax.numpy as jnp
        import numpy as np

        def _binarize(w):
            alpha = jax.lax.stop_gradient(jnp.mean(jnp.abs(w), axis=1, keepdims=True))
            bw = alpha * jnp.sign(w)
            return w + jax.lax.stop_gradient(bw - w)
        bw1 = _binarize(w1)
        h = jnp.einsum('bsd,hd->bsh', x, bw1) + b1
        h = jax.nn.gelu(h, approximate=False)
        bw2 = _binarize(w2)
        out = jnp.einsum('bsh,dh->bsd', h, bw2) + b2
        return out

    def _L1_attn_ref(x, Wq, Wk, Wv, Walpha, Wbeta, A_log, dt_bias, Wgate, Wout, rms_w):
        import math
        import jax, jax.numpy as jnp
        import numpy as np
        E = 256
        H = 16
        D = E // H

        def _l2norm(t, eps=1e-12):
            n = jnp.sqrt(jnp.sum(t * t, axis=-1, keepdims=True))
            return t / jnp.maximum(n, eps)
        b, s, _ = x.shape
        q = (x @ Wq).reshape(b, s, H, D)
        k = (x @ Wk).reshape(b, s, H, D)
        v = (x @ Wv).reshape(b, s, H, D)
        q = _l2norm(q) / math.sqrt(D)
        k = _l2norm(k)
        dt = jax.nn.softplus(x @ Walpha + dt_bias)
        alpha = jnp.exp(-jnp.exp(A_log) * dt)
        beta = jax.nn.sigmoid(x @ Wbeta)
        qT = jnp.moveaxis(q, 1, 0)
        kT = jnp.moveaxis(k, 1, 0)
        vT = jnp.moveaxis(v, 1, 0)
        aT = jnp.moveaxis(alpha, 1, 0)
        bT = jnp.moveaxis(beta, 1, 0)
        state0 = jnp.zeros((b, H, D, D), dtype=x.dtype)

        def step(state, inp):
            q_t, k_t, v_t, a_t, b_t = inp
            state = a_t[..., None, None] * state
            stored = jnp.einsum('bhij,bhj->bhi', state, k_t)
            delta = b_t[..., None] * (v_t - stored)
            state = state + jnp.einsum('bhi,bhj->bhij', delta, k_t)
            o_t = jnp.einsum('bhij,bhj->bhi', state, q_t)
            return (state, o_t)
        qs = jnp.swapaxes(qT, 1, 2).swapaxes(1, 1)
        _, outs = jax.lax.scan(step, state0, (qT, kT, vT, aT, bT))
        out = jnp.moveaxis(outs, 0, 1)
        var = jnp.mean(out * out, axis=-1, keepdims=True)
        out = out * jax.lax.rsqrt(var + 1e-06) * rms_w
        out = out.reshape(b, s, E)
        gate = jax.nn.silu(x @ Wgate)
        return out * gate @ Wout

    def _L1_ffn_ref(hidden_states, router_w, router_b, w1, w2):
        import jax, jax.numpy as jnp
        import numpy as np
        B, S, DIM, FFN, E = (4, 512, 256, 1024, 8)
        b, s, d = hidden_states.shape
        x = hidden_states.reshape(-1, d)
        logits = x @ router_w + router_b
        route = jax.nn.softmax(logits, axis=1)
        max_prob = jnp.max(route, axis=1, keepdims=True)
        max_ind = jnp.argmax(route, axis=1)
        out = jnp.zeros_like(x)
        num_experts = w1.shape[0]
        for e in range(num_experts):
            h = x @ w1[e]
            a, g = jnp.split(h, 2, axis=1)
            y = jax.nn.silu(a) * g @ w2[e]
            out = jnp.where((max_ind == e)[:, None], y, out)
        out = out * max_prob
        return out.reshape(b, s, d)
    h = _L0_tok_ref(x, L0_tok_weight, L0_tok_weighted_sum)
    h = h + _L0_attn_ref(_layernorm(h, axis=-1), L0_attn_keys, L0_attn_values, L0_attn_Wq_w, L0_attn_Wq_b, L0_attn_Wk_w, L0_attn_Wk_b, L0_attn_Wv_w, L0_attn_Wv_b)
    h = h + _L0_ffn_ref(_layernorm(h, axis=-1), L0_ffn_w1, L0_ffn_b1, L0_ffn_w2, L0_ffn_b2)
    h = h + _L1_attn_ref(_layernorm(h, axis=-1), L1_attn_Wq, L1_attn_Wk, L1_attn_Wv, L1_attn_Walpha, L1_attn_Wbeta, L1_attn_A_log, L1_attn_dt_bias, L1_attn_Wgate, L1_attn_Wout, L1_attn_rms_w)
    h = h + _L1_ffn_ref(_layernorm(h, axis=-1), L1_ffn_router_w, L1_ffn_router_b, L1_ffn_w1, L1_ffn_w2)
    return h

_drawn_inputs = setup_inputs


def setup_inputs(seed=0):
    import zlib

    import numpy as np

    out = dict(_drawn_inputs(seed))
    spreads = {'L1_attn_dt_bias': (0.0, 2.0), 'L1_attn_rms_w': (1.0, 0.6), 'L1_ffn_router_b': (0.0, 0.8)}
    factors = {'L0_attn_keys': 8.0,
     'L0_attn_values': 8.0,
     'L0_attn_Wq_w': 8.0,
     'L0_attn_Wq_b': 8.0,
     'L0_attn_Wk_w': 8.0,
     'L0_attn_Wk_b': 8.0,
     'L0_attn_Wv_w': 8.0,
     'L0_attn_Wv_b': 7.854,
     'L0_ffn_b1': 8.0,
     'L0_ffn_b2': 3.874,
     'L1_attn_Walpha': 64.0,
     'L1_attn_Wbeta': 41.955,
     'L1_attn_A_log': 19.256,
     'L1_ffn_router_w': 8.0,
     'L1_ffn_w1': 8.0,
     'L1_ffn_w2': 8.0}
    for name, (base, spread) in spreads.items():
        noise = np.random.default_rng([zlib.crc32(name.encode()), seed]).standard_normal(out[name].shape)
        drawn = base * np.exp(spread * noise) if base else spread * noise
        out[name] = jnp.asarray(drawn.astype(out[name].dtype))
    for name, factor in factors.items():
        out[name] = (out[name] * factor).astype(out[name].dtype)
    return out
```

```python
from contextlib import ExitStack

import numpy as np
from concourse import mybir
from concourse.bass import IndirectOffsetOnAxis, ds

F32 = mybir.dt.float32
BF16 = mybir.dt.bfloat16
I32 = mybir.dt.int32
U32 = mybir.dt.uint32
ALU = mybir.AluOpType
ACT = mybir.ActivationFunctionType
AX = mybir.AxisListType

P = 128
B, S, D = 4, 512, 256
NT = B * S // P
FC = D // P
TOK_D = 4
NK, NH, DH = 1024, 16, 16
KC = NK // P
QT = S // P
HC = 8
NE = 8
ET = 256
NET = (B * S + NE * (ET - 1)) // ET
CAT = 4 * D + 2 * NH
NPART = 96
HID = 1024
LN_EPS = 1e-5


STOP = 4


def build(nc, a, out, stop):
    with ExitStack() as ctx:
        def sb(name, shape, dt=F32):
            return ctx.enter_context(nc.sbuf_tensor(name, shape, dt))

        def sem(name):
            return ctx.enter_context(nc.semaphore(name))

        ps = ctx.enter_context(nc.psum_tensor("ps", [P, 8, 512], F32))
        h_res = sb("h_res", [P, NT, D])
        xn = sb("xn", [P, NT, D])
        ident = sb("ident", [P, P])
        ident_b = sb("ident_b", [P, P], BF16)
        bn = sb("bn", [P, 2, 6])
        mv = sb("mv", [P, NT, 2])
        var_eps = sb("var_eps", [P, NT])
        rstd = sb("rstd", [P, NT])
        ones = sb("ones", [P, P])
        minus_half = sb("minus_half", [P, NT * 32])
        arena = sb("arena", [P, 44000])

        def view(at, shape, dt=F32):
            n = int(np.prod(shape))
            words = n if dt in (F32, I32, U32) else n // 2
            v = arena[:, at:at + words]
            if dt != F32:
                v = v.bitcast(dt)
            names = " ".join(f"d{i}" for i in range(len(shape)))
            if len(shape) > 1:
                v = v.rearrange(f"p ({names}) -> p {names}", **{f"d{i}": s for i, s in enumerate(shape)})
            return v, at + words

        at = 0
        xnt, at = view(at, [FC, NT * P])
        kstk, at = view(at, [NH, NK], BF16)
        at_q1 = at + NH * S // 2
        qstk, at = view(at, [2, NH, S], BF16)
        vaug, at = view(at, [KC, NH, 32])
        at_att = at
        x_t = []
        for b in range(B - 1):
            v, at = view(at, [8, S])
            x_t.append(v)
        x_t.append(view(at_q1 - NH * S // 2, [8, S])[0])
        w_tok, at = view(at, [8, D])
        ws_t, w_at = view(0, [FC, D])
        w_bc, _ = view(w_at, [TOK_D, D])
        at_tok = at
        at = at_att
        prob, at = view(at, [2, 4, S])
        att, at = view(at, [2, S])
        rden, at = view(at, [S])
        spread, at = view(at, [P])
        gather, at = view(at, [2, P])
        mx, at = view(at, [2, QT, NH])
        mx1, at = view(at, [QT, NH])
        mlo, at = view(at, [QT, NH])
        mpad, at = view(at, [QT, P], BF16)
        mrow, at = view(at, [S], BF16)
        at_free = at
        assert at <= at_tok
        at = at_tok
        keys_t, k_at = view(at_q1, [FC, NK])
        vals_t, _ = view(k_at, [FC, NK])
        wq_t, at = view(at, [FC, D])
        wk_t, at = view(at, [FC, D])
        wv_t, at = view(at, [FC, D])
        bias_qk, at = view(at, [2, FC])
        bias_v, at = view(at, [D])
        sel, at = view(at, [NH])
        proj, at = view(at, [2, S])
        part, at = view(at, [2, 3, S], BF16)
        vtmp, at = view(at, [2, D])
        assert at <= 44000, at
        at = at_free
        w1, at = view(at, [FC, HID])
        w2, at = view(at, [HC, D])
        w_abs, at = view(at, [HC * D])
        w_mean, at = view(at, [HC * D])
        w_sign, at = view(at, [HC * D])
        bias_1, at = view(at, [HC])
        bias_2, at = view(at, [D])
        assert at <= 44000, at
        hid, _ = view(FC * NT * P, [2, HC, S])
        ffn_sum, _ = view(FC * NT * P + 2 * HC * S, [2, D])

        at = FC * NT * P
        v_rec, _ = view(0, [S, 8])
        w_cat, at = view(at, [FC, CAT])
        w_out, at = view(at, [FC, D])
        at_qkv = at
        kq_src, at = view(at, [2, 4, B, D])
        v_src, at = view(at, [4, 2, B, NH, 8])
        ab, at = view(at, [NT, 2 * NH])
        kq_rec, at = view(at, [S, 2, DH])
        sc_rec, at = view(at, [S, 3])
        r_rec, r_at = view(at_qkv, [S, 2, 8])
        d_rec, _ = view(r_at, [S, 8])
        state, at = view(at, [8, DH])
        prod, at = view(at, [2, 8, DH])
        outer, at = view(at, [8, DH])
        sq, at = view(at, [2, 2 * D])
        ssum, at = view(at, [NT, 2 * NH])
        rnorm, at = view(at, [NT, 2 * NH])
        small = []
        for _ in range(8):
            v, at = view(at, [NT, NH])
            small.append(v)
        kqdot, at = view(at, [NT, NH])
        dt_bias, at = view(at, [NH])
        a_exp, at = view(at, [NH])
        rms_w, at = view(at, [DH])
        assert at <= 44000, at
        o_tok, o_at = view(at_qkv + NT * 3 * D + NT * 2 * NH, [NT, D])
        o_t, _ = view(o_at, [2, FC, P])
        assert at <= 43744
        zero_row, _ = view(43744, [D])
        at = FC * NT * P
        rw, at = view(at, [FC, NE])
        rb, at = view(at, [NE])
        tri, at = view(at, [P])
        em8, at = view(at, [NE])
        thr, at = view(at, [NE])
        tile_no, at = view(at, [NET])
        lg, at = view(at, [NT, NE])
        lmax, at = view(at, [NT])
        eq, at = view(at, [NT, NE])
        onehot, at = view(at, [NT, NE])
        lexp, at = view(at, [NT, NE])
        pmax, at = view(at, [NT])
        cnt, at = view(at, [3, NT, NE])
        cmp_, at = view(at, [NET, NE])
        ends, at = view(at, [3, NE])
        base, at = view(at, [NE])
        pos, at = view(at, [NT])
        pos_i, at = view(at, [NT], U32)
        te, at = view(at, [NET + 1])
        te_i, at = view(at, [NET + 1], U32)
        ew1, at = view(at, [2, FC, 2 * HID])
        ew2, at = view(at, [2, HC, D])
        xs, at = view(at, [2, 2, D])
        xst, at = view(at, [2, FC, ET])
        silu, at = view(at, [2, ET])
        eu, at = view(at, [2, HC, ET])
        ys, at = view(at, [2, 2, D])
        yg, at = view(at, [NT, D])
        assert at <= 43744, at
        xs_dram = nc.dram_tensor("xs_dram", [NET * ET, D], F32, kind="Internal").ap()
        ys_dram = nc.dram_tensor("ys_dram", [NET * ET, D], F32, kind="Internal").ap()
        gate = xn[:, :, :]
        qk_parts = nc.dram_tensor("qk_parts", [3, D, NK + B * S], BF16, kind="Internal").ap()

        d_small = sem("d_small")
        d_kv = sem("d_kv")
        d_x = [sem(f"d_x{b}") for b in range(B)]
        consts = sem("consts")
        ident_ok = sem("ident_ok")
        wtok_ok = sem("wtok_ok")
        mm_tok = sem("mm_tok")
        tok_out = sem("tok_out")
        dve_step = sem("dve_step")
        pool_step = sem("pool_step")
        ln_var = sem("ln_var")
        ln_rstd = sem("ln_rstd")
        ln_out = sem("ln_out")
        tp_mm = sem("tp_mm")
        tp_out = sem("tp_out")
        pj_mm = sem("pj_mm")
        pj_out = sem("pj_out")
        pj_split = sem("pj_split")
        d_part = [sem("d_part0"), sem("d_part1")]
        d_kstk = sem("d_kstk")
        d_qstk = [sem(f"d_qstk{b}") for b in range(B)]
        sel_ok = sem("sel_ok")
        v_mm = sem("v_mm")
        v_out = sem("v_out")
        st_mm = sem("st_mm")
        exp_out = sem("exp_out")
        sm_mm = sem("sm_mm")
        max_out = sem("max_out")
        av_mm = sem("av_mm")
        av_out = sem("av_out")
        mx_pad = sem("mx_pad")
        mx_mm = sem("mx_mm")
        mx_row = sem("mx_row")
        d_mrow = sem("d_mrow")
        at_mm = sem("at_mm")
        at_add = sem("at_add")
        rd_ok = sem("rd_ok")
        sum_mm = sem("sum_mm")
        att_ok = sem("att_ok")
        h_pre = sem("h_pre")
        d_out = sem("d_out")
        zero_ok = sem("zero_ok")
        d_zero = sem("d_zero")
        d_rt = sem("d_rt")
        lg_mm = sem("lg_mm")
        lg_out = sem("lg_out")
        hot_ok = sem("hot_ok")
        sh_ok = sem("sh_ok")
        lexp_ok = sem("lexp_ok")
        cnt_mm = sem("cnt_mm")
        pos_ok = sem("pos_ok")
        d_disp = sem("d_disp")
        d_ew = [sem("d_ew0"), sem("d_ew1")]
        et_mm = sem("et_mm")
        et_out = sem("et_out")
        e1_mm = sem("e1_mm")
        e_silu = sem("e_silu")
        e1_out = sem("e1_out")
        e2_mm = sem("e2_mm")
        e2_out = sem("e2_out")
        d_ys = [sem("d_ys0"), sem("d_ys1")]
        d_yg = sem("d_yg")
        fin = sem("fin")
        d_w = sem("d_w")
        abs_ok = sem("abs_ok")
        mean_mm = sem("mean_mm")
        mean_ok = sem("mean_ok")
        w_ok = sem("w_ok")
        f1_mm = sem("f1_mm")
        f1_out = sem("f1_out")
        f2_mm = sem("f2_mm")
        f2_out = sem("f2_out")
        ffn_add = sem("ffn_add")
        d_w3 = sem("d_w3")
        c_mm = sem("c_mm")
        c_out = sem("c_out")
        c_ab = sem("c_ab")
        ss_ok = sem("ss_ok")
        nrm_ok = sem("nrm_ok")
        act_ab = sem("act_ab")
        dve_ab = sem("dve_ab")
        gate_ok = sem("gate_ok")
        rec_src = sem("rec_src")
        rt_mm = sem("rt_mm")
        rt_out = [sem("rt_out_act"), sem("rt_out_dve")]
        rec = sem("rec")
        o_ok = sem("o_ok")
        ot_mm = sem("ot_mm")
        ot_out = sem("ot_out")
        rms_ss = sem("rms_ss")
        rms_rt = sem("rms_rt")
        og_ok = sem("og_ok")
        og_mm = sem("og_mm")
        og_out = sem("og_out")
        wo_mm = sem("wo_mm")
        attn_add = sem("attn_add")

        rec_comps = ([("kq", w, c) for w in range(2) for c in range(DH)] + [("v", 0, i) for i in range(8)]
                     + [("sc", 0, i) for i in range(3)])
        NBANK = 4 * 11

        def rec_bank(n):
            return n // 11, rec_comps[4 * (n % 11):4 * (n % 11) + 4]

        def take_turned(eng, n):
            ftu, comps = rec_bank(n)
            ft, u = divmod(ftu, 2)
            kind, which, c0 = comps[0]
            dst = {"kq": kq_rec[:, :, which, :] if kind == "kq" else None, "v": v_rec, "sc": sc_rec}[kind]
            dst = dst.rearrange("p (f s u) c -> p f u s c", f=2, u=2)[:, ft, u, :, c0:c0 + len(comps)]
            src = ps[:, n % 4, 0:len(comps) * P].rearrange("p (c s) -> p s c", s=P)
            eng.wait_ge(rt_mm, n + 1)
            copy = eng.copy if n % 2 == 0 else eng.tensor_copy
            if kind == "v":
                copy(dst, src).then_inc(rt_out[n % 2], 2)
            else:
                copy(dst[0:64], src[0:64]).then_inc(rt_out[n % 2], 1)
                copy(dst[64:P], src[0:64]).then_inc(rt_out[n % 2], 1)

        def expert_tiles(eng, tile):
            tile(0, 0, True)
            tile(1, 1, True)
            with eng.Fori(1, NET // 2) as i:
                tile(i * 2, 0, False)
                tile(i * 2 + 1, 1, False)
            if NET % 2:
                tile(NET - 1, 0, False)

        def tile_at(j):
            return (j % 4) * B + j // 4

        block = ctx.enter_context(nc.Block())
        NU = 4 + 2 * B

        def turn_bank(stage, j):
            return ((2, 3), (2, 3), (3, 7), (3, 7))[stage][j % 2]

        def unit_cols(u):
            return (u // 2) * S

        @block.sync
        def _(sp):
            sp.dma_start(ws_t, a["tok_ws_t"].rearrange("(c p) n -> p c n", p=P)).then_inc(d_small, 16)
            sp.dma_start(w_bc, a["tok_w_t"].rearrange("(a d) n -> a d n", a=1).broadcast_to([P, TOK_D, D])).then_inc(d_small, 16)
            sp.dma_start(bias_qk, a["bias_qk"]).then_inc(d_small, 16)
            sp.dma_start(bias_v, a["bias_v"].broadcast_to([P, D])).then_inc(d_small, 16)
            for dst, name in ((keys_t, "keys_t"), (wk_t, "wk_t"), (vals_t, "vals_t"), (wv_t, "wv_t"), (wq_t, "wq_t")):
                sp.dma_start(dst, a[name].rearrange("(c p) n -> p c n", p=P)).then_inc(d_kv, 16)
            order_k, order_q = (0, 1, 0, 1, 2, 0), (0, 0, 1, 1, 0, 2)
            for u in range(NU):
                sp.wait_ge(pj_split, u + 1)
                m = u % 2
                sp.dma_start(qk_parts[:, m * P:(m + 1) * P, unit_cols(u):unit_cols(u) + S].rearrange("t p n -> p t n"),
                             part[:, u % 2]).then_inc(d_part[u % 2], 16)
                if u == 3:
                    sp.wait_ge(d_part[0], 32)
                    sp.wait_ge(d_part[1], 32)
                    for r, t in enumerate(order_k):
                        sp.dma_start(kstk[r * DH:(r + 1) * DH], qk_parts[t, :, 0:NK].rearrange("(h d) n -> d h n", d=DH)
                                     ).then_inc(d_kstk, 16)
                if u >= NU - 3 and u % 2:
                    b = (u - (NU - 3)) // 2
                    sp.wait_ge(d_part[0], 16 * (b + 3))
                    sp.wait_ge(d_part[1], 16 * (b + 3))
                    sp.wait_ge(mm_tok, NT)
                    for r, t in enumerate(order_q):
                        sp.dma_start(qstk[r * DH:(r + 1) * DH, b],
                                     qk_parts[t, :, NK + b * S:NK + (b + 1) * S].rearrange("(h d) n -> d h n", d=DH)
                                     ).then_inc(d_qstk[b], 16)
            for m in range(2):
                sp.wait_ge(d_part[m], 16 * (NU // 2))
            sp.wait_ge(pj_mm, NU)
            sp.wait_ge(v_out, KC)
            for dst, src in ((w1, a["w1_t"].rearrange("(c p) n -> p c n", p=P)), (w2, a["w2_t"].rearrange("(c p) n -> p c n", p=P)),
                             (bias_1, a["b1"]), (bias_2, a["b2"].broadcast_to([P, D]))):
                sp.dma_start(dst, src).then_inc(d_w, 16)
            for b in range(B):
                sp.wait_ge(mx_row, b + 1)
                sp.dma_start(qstk[NPART:P, b % 2], mrow[NPART:P].unsqueeze(1).broadcast_to([P - NPART, NH, S])).then_inc(d_mrow, 16)
                if 1 <= b < B - 1:
                    sp.wait_ge(st_mm, 64 * b)
                    for r, t in enumerate(order_q):
                        sp.dma_start(qstk[r * DH:(r + 1) * DH, (b + 1) % 2],
                                     qk_parts[t, :, NK + (b + 1) * S:NK + (b + 2) * S].rearrange("(h d) n -> d h n", d=DH)
                                     ).then_inc(d_qstk[b + 1], 16)
            if stop == 1:
                sp.wait_ge(at_add, 2 * B)
            if stop >= 2:
                sp.wait_ge(ffn_add, NT)
            if stop >= 3:
                for dst, src in ((w_cat, a["w_cat"].rearrange("(c p) n -> p c n", p=P)),
                                 (w_out, a["w_out"].rearrange("(c p) n -> p c n", p=P)),
                                 (dt_bias, a["dt_bias"].broadcast_to([P, NH])), (a_exp, a["a_log"].broadcast_to([P, NH])),
                                 (rms_w, a["rms_w"].broadcast_to([P, DH]))):
                    sp.dma_start(dst, src).then_inc(d_w3, 16)
                sp.wait_ge(attn_add, NT)
            if stop < 4:
                sp.dma_start(out.rearrange("(n p u) c -> p n u c", p=P, u=2),
                             h_res[:, :, :].rearrange("p (n u) c -> p n u c", u=2)).then_inc(d_out, 16)
            if stop == 4:
                for dst, src in ((rw, a["router_w"].rearrange("(c p) n -> p c n", p=P)), (rb, a["router_b"].broadcast_to([P, NE])),
                                 (tri, a["tri"]), (em8, a["em8"].broadcast_to([P, NE])), (thr, a["thr"].broadcast_to([P, NE])),
                                 (tile_no, a["tile_no"].broadcast_to([P, NET]))):
                    sp.dma_start(dst, src).then_inc(d_rt, 16)
                sp.wait_ge(pos_ok, 1)
                sp.wait_ge(d_disp, 16 * NT)

                def load(t, slot, first):
                    if not first:
                        sp.wait_ge(e2_mm, t - 1)
                    e = sp.value_load(te_i[0:1, ds(t, 1)], min_val=0, max_val=NE - 1)
                    sp.dma_start(xs[:, slot], xs_dram.rearrange("(t r p) n -> p t r n", p=P, r=2)[:, ds(t, 1)].rearrange("p o r n -> p (o r) n")
                                 ).then_inc(d_ew[slot], 16)
                    sp.dma_start(ew1[:, slot], a["ew1"].rearrange("e (c p) n -> p e c n", p=P)[:, ds(e, 1)].rearrange("p o c n -> p (o c) n")
                                 ).then_inc(d_ew[slot], 16)
                    sp.dma_start(ew2[:, slot], a["ew2"].rearrange("e (c p) n -> p e c n", p=P)[:, ds(e, 1)].rearrange("p o c n -> p (o c) n")
                                 ).then_inc(d_ew[slot], 16)

                expert_tiles(sp, load)
                for b in range(B):
                    sp.wait_ge(fin, 4 * b + 4)
                    sp.dma_start(out.rearrange("(b f p u) c -> p b f u c", b=B, f=2, u=2)[:, b],
                                 h_res[:, 4 * b:4 * b + 4, :].rearrange("p (f u) c -> p f u c", u=2)).then_inc(d_out, 16)
            sp.wait_ge(d_out, 16 * B if stop == 4 else 16)

        @block.gpsimd
        def _(pool):
            pool.memset(ident[:, :], 0.0).then_inc(pool_step, 1)
            pool.memset(minus_half[:, :], -0.5).then_inc(consts, 1)
            pool.wait_ge(pool_step, 1)
            pool.affine_select(out=ident[:, :], in_=ident[:, :], compare_op=ALU.not_equal, fill=1.0, base=0,
                               pattern=[[-1, P]], channel_multiplier=1).then_inc(ident_ok, 1)
            pool.wait_ge(ident_ok, 1)
            pool.memset(sel[NPART:P], 0.0).then_inc(pool_step, 1)
            for i, base in enumerate((0, -NH)):
                pool.wait_ge(pool_step, 2 + i)
                pool.affine_select(out=sel[NPART:P], in_=sel[NPART:P], compare_op=ALU.not_equal, fill=-1.0, base=base,
                                   pattern=[[-1, NH]], channel_multiplier=1).then_inc(pool_step, 1)
            pool.wait_ge(pool_step, 4)
            pool.tensor_copy(kstk[NPART:P], sel[NPART:P].unsqueeze(2).broadcast_to([P - NPART, NH, NK])).then_inc(sel_ok, 1)

            def rstd_of(stage, j):
                pool.wait_ge(ln_var, stage * NT + j + 1)
                pool.tensor_tensor(rstd[:, j:j + 1], var_eps[:, j:j + 1], minus_half[:, 0:1], ALU.pow).then_inc(ln_rstd, 1)

            pool.wait_ge(consts, 1)
            pool.wait_ge(sel_ok, 1)
            for j in range(NT):
                rstd_of(0, j)
            pool.wait_ge(mm_tok, NT)
            pool.memset(spread, 0.0).then_inc(pool_step, 1)
            pool.memset(gather, 0.0).then_inc(pool_step, 1)
            pool.wait_ge(pool_step, 6)
            pool.affine_select(out=spread.rearrange("p (c d) -> p c d", c=4), in_=spread.rearrange("p (c d) -> p c d", c=4),
                               compare_op=ALU.not_equal, fill=1.0, base=-DH, pattern=[[-32, 4], [0, 32]],
                               channel_multiplier=1).then_inc(pool_step, 1)
            for i in range(2):
                pool.wait_ge(pool_step, 7 + i)
                g = gather[:, i, 64 * i:64 * i + 64].rearrange("p (c d) -> p c d", c=4)
                pool.affine_select(out=g, in_=g, compare_op=ALU.not_equal, fill=1.0, base=0, pattern=[[-32, 4], [-1, DH]],
                                   channel_multiplier=1).then_inc(pool_step, 1)
            pool.wait_ge(pool_step, 9)
            pool.memset(ones[:, :], 1.0).then_inc(consts, 4)

            psteps = [9]

            def pstep(ins):
                psteps[0] += 1
                ins.then_inc(pool_step, 1)
                pool.wait_ge(pool_step, psteps[0])

            pool.wait_ge(d_w, 64)
            for i, w in enumerate((w1, w2)):
                w = w.rearrange("p c n -> p (c n)")
                pstep(pool.tensor_scalar(w_sign, w, 0.0, None, ALU.is_gt))
                pool.wait_ge(mean_mm, i + 1)
                pstep(pool.tensor_scalar(w_abs, w, 0.0, None, ALU.is_lt))
                pstep(pool.tensor_tensor(w_sign, w_sign, w_abs, ALU.subtract))
                pool.wait_ge(mean_ok, i + 1)
                pstep(pool.tensor_tensor(w_sign, w_sign, w_mean, ALU.mult))
                pstep(pool.tensor_tensor(w_sign, w_sign, w, ALU.subtract))
                pool.tensor_tensor(w, w, w_sign, ALU.add).then_inc(w_ok, 1)
                pool.wait_ge(w_ok, i + 1)
            if stop >= 2:
                for j in range(NT):
                    rstd_of(1, j)
            if stop >= 4:
                pool.memset(zero_row, 0.0).then_inc(zero_ok, 1)
                pool.wait_ge(zero_ok, 1)
                pool.dma_start(xs_dram.rearrange("(t p) n -> p t n", p=P), zero_row.unsqueeze(1).broadcast_to([P, 2 * NET, D])
                               ).then_inc(d_zero, 16)
            if stop >= 3:
                for j in range(NT):
                    rstd_of(2, j)
                pool.wait_ge(d_w3, 80)
                pool.wait_ge(c_out, NT)
                g = gate.rearrange("p j (h d) -> p (j h) d", d=DH)
                pool.tensor_tensor(g, g, rms_w.unsqueeze(1).broadcast_to([P, NT * NH, DH]), ALU.mult).then_inc(gate_ok, 1)
            if stop >= 4:
                for j in range(NT):
                    rstd_of(3, j)
                pool.wait_ge(pos_ok, 1)
                pool.wait_ge(d_zero, 16)
                for j in range(NT):
                    pool.indirect_dma_start(out=xs_dram, out_offset=IndirectOffsetOnAxis(ap=pos_i[:, j:j + 1], axis=0),
                                            in_=xn[:, j, :], in_offset=None).then_inc(d_disp, 16)
                pool.wait_ge(d_ys[0], 16 * ((NET + 1) // 2))
                pool.wait_ge(d_ys[1], 16 * (NET // 2))
                for j in range(NT):
                    pool.indirect_dma_start(out=yg[:, j, :], out_offset=None, in_=ys_dram,
                                            in_offset=IndirectOffsetOnAxis(ap=pos_i[:, j:j + 1], axis=0)).then_inc(d_yg, 16)

        @block.scalar
        def _(act):
            for b in range(B):
                act.dma_start(x_t[b],
                              a["x_t"].rearrange("(c p) n -> p c n", p=P)[:, :, b * S:(b + 1) * S]).then_inc(d_x[b], 16)

            def project_out(u):
                act.wait_ge(pj_mm, u + 1)
                if u >= 2:
                    act.wait_ge(pj_split, u - 1)
                which = 0 if u >= 4 else 1
                act.activation(proj[:, u % 2], ps[:, 4 + u % 2, :], ACT.Relu,
                               bias=bias_qk[:, which, u % 2:u % 2 + 1]).then_inc(pj_out, 1)

            def turn_out(stage, j):
                n = stage * NT + j
                act.wait_ge(tp_mm, n + 1)
                act.copy(xnt[:, :, j * P:(j + 1) * P],
                         ps[:, turn_bank(stage, j), 0:FC * P].rearrange("p (c n) -> p c n", c=FC)).then_inc(tp_out, 1)

            act.wait_ge(d_small, 64)
            for u in range(4):
                project_out(u)
            for b in range(B):
                for j in range(4 * b, 4 * b + 4):
                    turn_out(0, j)
                for m in range(2):
                    project_out(4 + 2 * b + m)

            def unit(n, e):
                for g in range(2):
                    act.wait_ge(st_mm, 2 * n + g + 1)
                    if g == 0 and not (isinstance(n, int) and n < 2):
                        act.wait_ge(av_mm, n - 1)
                    act.activation(prob[:, e, 2 * g:2 * g + 2, :], ps[:, 2 * g:2 * g + 2, :], ACT.Exp,
                                   scale=DH ** -0.5).then_inc(exp_out, 1)

            def quad(b, q, m, parity):
                for e in range(8):
                    unit(8 * m + e, e % 2)
                    if e == 1 and not (isinstance(q, int) and q == 0):
                        quad_out_slot(8 * m, m - 1, 1 - parity)

            def quad_out_slot(n, m, slot):
                act.wait_ge(av_mm, n)
                if not (isinstance(m, int) and m < 2):
                    act.wait_ge(at_mm, m - 1)
                act.copy(att[:, slot], ps[:, 6, :]).then_inc(av_out, 1)

            act.wait_ge(d_w, 64)
            for i, w in enumerate((w1, w2)):
                if i:
                    act.wait_ge(w_ok, i)
                act.activation(w_abs, w.rearrange("p c n -> p (c n)"), ACT.Abs).then_inc(abs_ok, 1)
                act.wait_ge(mean_mm, i + 1)
                if i == 0:
                    act.mul(w_mean.rearrange("p (c a n) -> p c a n", c=FC, a=2)[:, 0], ps[:, 6:8, :], 1.0 / D)
                    act.mul(w_mean.rearrange("p (c a n) -> p c a n", c=FC, a=2)[:, 1], ps[:, 6:8, :], 1.0 / D).then_inc(mean_ok, 1)
                else:
                    for c in range(HC):
                        ins = act.mul(w_mean.rearrange("p (c n) -> p c n", c=HC)[:, c], ps[:, 6, 0:D], 1.0 / HID)
                    ins.then_inc(mean_ok, 1)

            for b in range(B):
                act.wait_ge(mx_mm, b + 1)
                if b:
                    act.wait_ge(d_mrow, 16 * b)
                act.copy(mrow[NPART:P], ps[NPART:P, 7, 0:S // 2].bitcast(BF16)).then_inc(mx_row, 1)
                quad(b, 0, 4 * b, 0)
                quad(b, 1, 4 * b + 1, 1)
                with act.Fori(1, 2) as qp:
                    for e in range(2):
                        quad(b, None, qp * 2 + (4 * b + e), e)
                quad_out_slot(32 * b + 32, 4 * b + 3, 1)

            if stop >= 2:
                for b in range(B):
                    for j in range(4 * b, 4 * b + 4):
                        turn_out(1, j)
                    for m in range(HC):
                        act.wait_ge(f1_mm, b * HC + m + 1)
                        if b >= 2 and m == 0:
                            act.wait_ge(f2_mm, 4 * (b - 1))
                        act.activation(hid[:, b % 2, m, :], ps[:, 4 + m % 2, :], ACT.Gelu, bias=bias_1[:, m:m + 1]).then_inc(f1_out, 1)
            if stop >= 3:
                act.wait_ge(d_w3, 80)

                def take_cat(j):
                    act.wait_ge(c_mm, j + 1)
                    s0 = 4 * (j % 2)
                    act.copy(kq_src[:, :, j % 4, j // 4, :], ps[:, s0, :].rearrange("p (w n) -> p w n", w=2))
                    act.copy(v_src[:, j % 4, :, j // 4], ps[:, s0 + 1, 0:D].rearrange("p (h a c) -> p a h c", a=2, c=8))
                    act.activation(gate[:, j, :], ps[:, s0 + 1, D:2 * D], ACT.Silu).then_inc(c_out, 1)

                for j in range(NT):
                    turn_out(2, j)
                    if j:
                        take_cat(j - 1)
                take_cat(NT - 1)
                act.wait_ge(ss_ok, NT)
                act.activation(rnorm, ssum, ACT.Sqrt).then_inc(nrm_ok, 1)
                z, u, ga, be = small[0], small[1], small[2], small[3]
                act.wait_ge(dve_ab, 1)
                act.activation(a_exp, a_exp, ACT.Exp).then_inc(act_ab, 1)
                act.activation(u, z, ACT.Abs).then_inc(act_ab, 1)
                act.wait_ge(act_ab, 2)
                act.activation(u, u, ACT.Exp, scale=-1.0).then_inc(act_ab, 1)
                act.activation(be, ab[:, :, NH:2 * NH], ACT.Exp, scale=-1.0).then_inc(act_ab, 1)
                act.wait_ge(dve_ab, 2)
                act.activation(ga, ga, ACT.Exp, scale=-1.0).then_inc(act_ab, 1)
                for n in range(0, NBANK, 2):
                    take_turned(act, n)
                act.wait_ge(rms_ss, 1)
                act.activation(small[0], small[0], ACT.Sqrt).then_inc(rms_rt, 1)
                for j in range(NT):
                    act.wait_ge(og_mm, j + 1)
                    if j >= 2:
                        act.wait_ge(wo_mm, j - 1)
                    act.copy(o_t[:, j % 2], ps[:, 2 + j % 2, 0:FC * P].rearrange("p (c n) -> p c n", c=FC)).then_inc(og_out, 1)

            if stop >= 4:
                for j in range(NT):
                    turn_out(3, j)
                act.wait_ge(sh_ok, 1)
                act.activation(lexp, lexp, ACT.Exp).then_inc(lexp_ok, 1)

                def expert(t, slot, first):
                    act.wait_ge(et_mm, t + 1)
                    if not first:
                        act.wait_ge(e1_mm, (t - 1) * HC)
                    act.copy(xst[:, slot], ps[:, 6, :].rearrange("p (c n) -> p c n", c=FC)).then_inc(et_out, 1)
                    for m in range(HC):
                        act.wait_ge(e1_mm, t * HC + m + 1)
                        if not (first and t == 0 and m < 2):
                            act.wait_ge(e1_out, t * HC + m - 1)
                        act.activation(silu[:, m % 2], ps[:, m % 4, 0:ET], ACT.Silu).then_inc(e_silu, 1)
                    act.wait_ge(e2_out, t + 1)
                    act.dma_start(ys_dram.rearrange("(t r p) n -> p t r n", p=P, r=2)[:, ds(t, 1)].rearrange("p o r n -> p (o r) n"),
                                  ys[:, slot]).then_inc(d_ys[slot], 16)

                expert_tiles(act, expert)

        @block.tensor
        def _(pe):
            pe.wait_ge(d_kv, 80)
            for u in range(4):
                kh, m = divmod(u, 2)
                if u >= 2:
                    pe.wait_ge(pj_out, u - 1)
                for c in range(FC):
                    mm = pe.matmul(ps[:, 4 + u % 2, :], wk_t[:, c, m * P:(m + 1) * P], keys_t[:, c, kh * S:(kh + 1) * S],
                                   start=(c == 0), stop=(c == FC - 1))
                mm.then_inc(pj_mm, 1)
            for kc in range(KC):
                if kc >= 2:
                    pe.wait_ge(v_out, kc - 1)
                for c in range(FC):
                    mm = pe.matmul(ps[:, 6 + kc % 2, 0:D], vals_t[:, c, kc * P:(kc + 1) * P], wv_t[:, c, :],
                                   start=(c == 0), stop=(c == FC - 1))
                mm.then_inc(v_mm, 1)

            def turn(stage, j):
                n = stage * NT + j
                pe.wait_ge(ln_out, n + 1)
                if n >= 2:
                    pe.wait_ge(tp_out, n - 1)
                for c in range(FC):
                    mm = pe.transpose(ps[:, turn_bank(stage, j), c * P:(c + 1) * P], xn[:, j, c * P:(c + 1) * P], ident[:, :])
                mm.then_inc(tp_mm, 1)

            pe.wait_ge(ident_ok, 1)
            for b in range(B + 1):
                if b < B:
                    pe.wait_ge(d_x[b], 16)
                    for j in range(4 * b, 4 * b + 4):
                        if j >= 2:
                            pe.wait_ge(tok_out, j - 1)
                        for c in range(8):
                            if b == 0 and j == 0:
                                pe.wait_ge(wtok_ok, c + 1)
                            mm = pe.matmul(ps[:, j % 2, 0:D], x_t[b][:, c, (j % 4) * P:(j % 4 + 1) * P], w_tok[:, c, :],
                                           start=(c == 0), stop=(c == 7))
                        mm.then_inc(mm_tok, 1)
                if b >= 1:
                    for j in range(4 * b - 4, 4 * b):
                        turn(0, j)
                    pe.wait_ge(tp_out, 4 * b)
                    for m in range(2):
                        u = 4 + 2 * (b - 1) + m
                        pe.wait_ge(pj_out, u - 1)
                        for c in range(FC):
                            mm = pe.matmul(ps[:, 4 + u % 2, :], wq_t[:, c, m * P:(m + 1) * P],
                                           xnt[:, c, (b - 1) * S:b * S], start=(c == 0), stop=(c == FC - 1))
                        mm.then_inc(pj_mm, 1)

            def unit(q, kc, n, slot, nmax, mslot):
                for g in range(2):
                    if n is not None:
                        if n:
                            pe.wait_ge(exp_out, 2 * n + g - 1)
                        for i in range(2):
                            h = 4 * q + 2 * g + i
                            mm = pe.matmul(ps[:, 2 * g + i, :], kstk[:, h, kc * P:(kc + 1) * P], qstk[:, slot, h, :],
                                           start=True, stop=True)
                        mm.then_inc(st_mm, 1)
                    if nmax is not None:
                        h, part_of = divmod(8 * q + kc, 2)
                        qt = 2 * part_of + g
                        for half in range(2):
                            if nmax or g:
                                pe.wait_ge(max_out, 4 * nmax + 2 * g + half - 1)
                            pe.matmul(ps[:, 4 + half, :], qstk[0:NPART, mslot, h, qt * P:(qt + 1) * P],
                                      kstk[0:NPART, h, half * S:(half + 1) * S], start=True, stop=True).then_inc(sm_mm, 1)

            def attend(n):
                m, kc = divmod(n, KC)
                pe.wait_ge(exp_out, 2 * n + 2)
                if kc == 0 and m:
                    pe.wait_ge(av_out, m)
                for c in range(4):
                    mm = pe.matmul(ps[32 * c:32 * c + 32, 6, :], vaug[:, kc, 4 * (m % 4) + c, :], prob[:, n % 2, c, :],
                                   start=(kc == 0), stop=(kc == KC - 1), skip_group_check=True)
                mm.then_inc(av_mm, 1)

            def spread_sums(m):
                pe.wait_ge(av_out, m + 1)
                if m >= 2 and m % 2 == 0:
                    pe.wait_ge(at_add, m // 2)
                if m % 4 == 0:
                    pe.wait_ge(mx_row, m // 4 + 1)
                if m % 2:
                    pe.wait_ge(rd_ok, m)
                pe.matmul(ps[:, 7, :], spread, att[:, m % 2], start=True, stop=True).then_inc(sum_mm, 1)

            def compact(m):
                pe.wait_ge(att_ok, m + 1)
                for i in range(2):
                    mm = pe.matmul(ps[:, 7, :], gather[:, i], att[:, i], start=(i == 0), stop=(i == 1))
                mm.then_inc(at_mm, 2)

            pe.wait_ge(consts, 5)
            for i in range(2):
                pe.wait_ge(abs_ok, i + 1)
                if i:
                    pe.wait_ge(mean_ok, i)
                if i == 0:
                    for half in range(2):
                        for c in range(FC):
                            mm = pe.matmul(ps[:, 6 + half, :], ones[:, :], w_abs[:, c * HID + half * S:c * HID + (half + 1) * S],
                                           start=(c == 0), stop=(c == FC - 1))
                else:
                    for c in range(HC):
                        mm = pe.matmul(ps[:, 6, 0:D], ones[:, :], w_abs[:, c * D:(c + 1) * D], start=(c == 0), stop=(c == HC - 1))
                mm.then_inc(mean_mm, 1)
            pe.wait_ge(mean_ok, 2)
            pe.wait_ge(d_kstk, 96)
            pe.wait_ge(sel_ok, 1)
            pe.wait_ge(v_out, KC)
            pe.wait_ge(pj_out, NU)
            for b in range(-1, B):
                if b + 1 < B:
                    pe.wait_ge(d_qstk[b + 1], 96)
                if b >= 0:
                    pe.wait_ge(d_mrow, 16 * (b + 1))
                for q in range(4):
                    for kc in range(KC):
                        n = 32 * b + 8 * q + kc
                        unit(q, kc, n if b >= 0 else None, b % 2, n + 32 if b + 1 < B else None, (b + 1) % 2)
                        if b >= 0 and n > 32 * b:
                            attend(n - 1)
                        if b >= 0 and kc == 3 and q:
                            spread_sums(4 * b + q - 1)
                        if b >= 0 and kc == 6 and q == 2:
                            compact(4 * b + 1)
                if b >= 0:
                    attend(32 * b + 31)
                    spread_sums(4 * b + 3)
                    compact(4 * b + 3)
                if b + 1 < B:
                    pe.wait_ge(mx_pad, b + 2)
                    if b >= 0:
                        pe.wait_ge(at_add, 2 * b + 2)
                    for qt in range(QT):
                        mm = pe.transpose(ps[:, 7, qt * (P // 2):(qt + 1) * (P // 2)].bitcast(BF16), mpad[:, qt, :], ident_b[:, :])
                    mm.then_inc(mx_mm, 1)

            if stop >= 2:
                pe.wait_ge(w_ok, 2)
                pe.wait_ge(at_add, 2 * B)
                pe.wait_ge(exp_out, 256)

                def hidden(b):
                    for m in range(HC):
                        n = b * HC + m
                        if n >= 2:
                            pe.wait_ge(f1_out, n - 1)
                        for c in range(FC):
                            mm = pe.matmul(ps[:, 4 + m % 2, :], w1[:, c, m * P:(m + 1) * P], xnt[:, c, b * S:(b + 1) * S],
                                           start=(c == 0), stop=(c == FC - 1))
                        mm.then_inc(f1_mm, 1)

                def ffn_out(b):
                    pe.wait_ge(f1_out, HC * (b + 1))
                    for i in range(4):
                        j = 4 * b + i
                        if j >= 2:
                            pe.wait_ge(f2_out, j - 1)
                        for m in range(HC):
                            mm = pe.matmul(ps[:, 6 + j % 2, 0:D], hid[:, b % 2, m, i * P:(i + 1) * P], w2[:, m, :],
                                           start=(m == 0), stop=(m == HC - 1))
                        mm.then_inc(f2_mm, 1)

                for b in range(B + 1):
                    if b < B:
                        for j in range(4 * b, 4 * b + 4):
                            turn(1, j)
                        pe.wait_ge(tp_out, NT + 4 * b + 4)
                        hidden(b)
                    if b:
                        ffn_out(b - 1)
            if stop >= 3:
                pe.wait_ge(d_w3, 80)
                pe.wait_ge(f2_out, NT)

                def project(j):
                    pe.wait_ge(tp_out, 2 * NT + j + 1)
                    if j >= 2:
                        pe.wait_ge(c_out, j - 1)
                        pe.wait_ge(c_ab, j - 1)
                    s0 = 4 * (j % 2)
                    for i, (lo, n) in enumerate(((0, 512), (512, 512), (1024, 2 * NH))):
                        for c in range(FC):
                            mm = pe.matmul(ps[:, s0 + i, 0:n], xnt[:, c, j * P:(j + 1) * P], w_cat[:, c, lo:lo + n],
                                           start=(c == 0), stop=(c == FC - 1))
                    mm.then_inc(c_mm, 1)

                for j in range(NT):
                    turn(2, j)
                    if j:
                        project(j - 1)
                project(NT - 1)
                pe.wait_ge(rec_src, 1)
                pe.wait_ge(c_ab, NT)
                for n in range(NBANK):
                    ftu, comps = rec_bank(n)
                    if n >= 4:
                        pe.wait_ge(rt_out[n % 2], 2 * (n // 2 - 1))
                    for i, (kind, which, c) in enumerate(comps):
                        if kind == "sc":
                            src = (small[2], small[4], kqdot)[c][:, B * ftu:B * (ftu + 1), :].rearrange("p b h -> p (b h)")
                        elif kind == "v":
                            src = v_src[:, ftu].rearrange("p a b h c -> p (a b h) c")[:, :, c]
                        else:
                            src = kq_src[:, which, ftu].rearrange("p b (h c) -> p (b h) c", c=DH)[:, :, c]
                        mm = pe.transpose(ps[0:src.shape[1], n % 4, i * P:(i + 1) * P], src, ident[:, :])
                    mm.then_inc(rt_mm, 1)
                pe.wait_ge(o_ok, 1)
                for n in range(8):
                    ftu, ih = divmod(n, 2)
                    ft, u = divmod(ftu, 2)
                    if n >= 2:
                        pe.wait_ge(ot_out, n - 1)
                    for i in range(4):
                        src = d_rec.rearrange("p (f s u) c -> p f u s c", f=2, u=2)[:, ft, u, :, 4 * ih + i]
                        mm = pe.transpose(ps[:, n % 2, i * P:(i + 1) * P], src, ident[:, :])
                    mm.then_inc(ot_mm, 1)
                for j in range(NT + 1):
                    if j < NT:
                        pe.wait_ge(og_ok, j + 1)
                        if j >= 2:
                            pe.wait_ge(og_out, j - 1)
                        for c in range(FC):
                            mm = pe.transpose(ps[:, 2 + j % 2, c * P:(c + 1) * P], o_tok[:, j, c * P:(c + 1) * P], ident[:, :])
                        mm.then_inc(og_mm, 1)
                    if j:
                        i = j - 1
                        pe.wait_ge(og_out, i + 1)
                        if i >= 2:
                            pe.wait_ge(attn_add, i - 1)
                        for c in range(FC):
                            mm = pe.matmul(ps[:, 4 + i % 2, 0:D], o_t[:, i % 2, c, :], w_out[:, c, :], start=(c == 0), stop=(c == FC - 1))
                        mm.then_inc(wo_mm, 1)

            if stop >= 4:
                pe.wait_ge(d_rt, 96)
                for j in range(NT):
                    if j == 0:
                        pe.wait_ge(attn_add, NT)
                    turn(3, j)
                    pe.wait_ge(tp_out, 3 * NT + j + 1)
                    for c in range(FC):
                        mm = pe.matmul(ps[:, 0, j * NE:(j + 1) * NE], xnt[:, c, j * P:(j + 1) * P], rw[:, c, :],
                                       start=(c == 0), stop=(c == FC - 1))
                mm.then_inc(lg_mm, 1)
                pe.wait_ge(hot_ok, 1)
                hot = onehot.rearrange("p j e -> p (j e)")
                pe.matmul(ps[:, 1, 0:NT * NE], tri, hot, start=True, stop=True)
                pe.matmul(ps[:, 2, 0:NT * NE], ones[:, :], hot, start=True, stop=True).then_inc(cnt_mm, 1)
                pe.wait_ge(pos_ok, 1)

                def turn_tokens(t, slot, first):
                    pe.wait_ge(d_ew[slot], (t // 2 + 1) * 48 if isinstance(t, int) else t * 24 + (48 if slot == 0 else 24))
                    if not (first and t == 0):
                        pe.wait_ge(et_out, t)
                    for c in range(FC):
                        for r in range(2):
                            mm = pe.transpose(ps[:, 6, c * ET + r * P:c * ET + (r + 1) * P], xs[:, slot, r, c * P:(c + 1) * P], ident[:, :])
                    mm.then_inc(et_mm, 1)

                def expert(t, slot, first):
                    pe.wait_ge(et_out, t + 1)
                    for m in range(HC):
                        if not (first and t == 0 and m < 4):
                            pe.wait_ge(e1_out, t * HC + m - 3)
                        for half in range(2):
                            for c in range(FC):
                                mm = pe.matmul(ps[:, m % 4, half * ET:(half + 1) * ET],
                                               ew1[:, slot, c, half * HID + m * P:half * HID + (m + 1) * P], xst[:, slot, c, :],
                                               start=(c == 0), stop=(c == FC - 1))
                        mm.then_inc(e1_mm, 1)
                    if not (isinstance(t, int) and t == NET - 1):
                        turn_tokens(t + 1, 1 - slot, first)
                    pe.wait_ge(e1_out, t * HC + HC)
                    if not (first and t == 0):
                        pe.wait_ge(e2_out, t)
                    for r in range(2):
                        for m in range(HC):
                            mm = pe.matmul(ps[:, 4 + r, 0:D], eu[:, slot, m, r * P:(r + 1) * P], ew2[:, slot, m, :],
                                           start=(m == 0), stop=(m == HC - 1))
                    mm.then_inc(e2_mm, 1)

                turn_tokens(0, 0, True)
                expert_tiles(pe, expert)

        @block.vector
        def _(dve):
            steps = [0]

            def step(ins):
                steps[0] += 1
                ins.then_inc(dve_step, 1)
                dve.wait_ge(dve_step, steps[0])

            dve.wait_ge(ident_ok, 1)
            dve.tensor_copy(ident_b[:, :], ident[:, :])
            dve.wait_ge(d_small, 64)
            for c in range(8):
                d, ic = divmod(c, FC)
                dve.tensor_tensor(w_tok[:, c, :], ws_t[:, ic, :], w_bc[:, d, :], ALU.mult).then_inc(wtok_ok, 1)
            step(dve.memset(vaug[:, :, :, DH:32], 0.0))
            dve.memset(vaug[:, :, :, DH:DH + 1], 1.0)

            def split(u):
                dve.wait_ge(pj_out, u + 1)
                if u >= 2:
                    dve.wait_ge(d_part[u % 2], 16 * (u // 2))
                f = proj[:, u % 2]
                step(dve.tensor_copy(part[:, u % 2, 0], f))
                step(dve.tensor_tensor(f, f, part[:, u % 2, 0], ALU.subtract))
                step(dve.tensor_copy(part[:, u % 2, 1], f))
                step(dve.tensor_tensor(f, f, part[:, u % 2, 1], ALU.subtract))
                dve.tensor_copy(part[:, u % 2, 2], f).then_inc(pj_split, 1)

            for u in range(4):
                split(u)
            for kc in range(KC):
                dve.wait_ge(v_mm, kc + 1)
                dve.tensor_tensor(vtmp[:, kc % 2], ps[:, 6 + kc % 2, 0:D], bias_v, ALU.add).then_inc(v_out, 1)
                dve.wait_ge(v_out, kc + 1)
                dve.tensor_scalar(vaug[:, kc, :, 0:DH], vtmp[:, kc % 2].rearrange("p (h d) -> p h d", h=NH), 0.0, None,
                                  ALU.max)

            def ln_stats(j):
                step(dve.bn_stats(bn[:, j % 2, :], h_res[:, j, :]))
                step(dve.bn_aggr(mv[:, j, :], bn[:, j % 2, :]))
                dve.tensor_scalar(var_eps[:, j:j + 1], mv[:, j, 1:2], LN_EPS, None, ALU.add).then_inc(ln_var, 1)

            def ln_apply(stage, j):
                dve.wait_ge(ln_rstd, stage * NT + j + 1)
                dve.tensor_scalar(xn[:, j, :], h_res[:, j, :], mv[:, j, 0:1], rstd[:, j:j + 1], ALU.subtract,
                                  ALU.mult).then_inc(ln_out, 1)

            for b in range(B + 1):
                if b < B:
                    for j in range(4 * b, 4 * b + 4):
                        dve.wait_ge(mm_tok, j + 1)
                        dve.tensor_copy(h_res[:, j, :], ps[:, j % 2, 0:D]).then_inc(tok_out, 1)
                        dve.wait_ge(tok_out, j + 1)
                        ln_stats(j)
                        if j >= 1:
                            ln_apply(0, j - 1)
                else:
                    ln_apply(0, NT - 1)
                if b >= 2:
                    for m in range(2):
                        split(4 + 2 * (b - 2) + m)
            for m in range(2):
                split(4 + 2 * (B - 1) + m)
            dve.wait_ge(mm_tok, NT)
            dve.wait_ge(ln_out, NT)
            step(dve.tensor_tensor(h_res[:, :, :], h_res[:, :, :], xn[:, :, :], ALU.add))
            step(dve.memset(mpad, 0.0))

            def maxima(h, nmax):
                for qt in range(QT):
                    for half in range(2):
                        dve.wait_ge(sm_mm, 8 * nmax + 2 * qt + half + 1)
                        dve.tensor_reduce(mx[:, half, qt, ds(h, 1)], ps[:, 4 + half, :], AX.X, ALU.max).then_inc(max_out, 1)

            def normalise(m, slot):
                dve.wait_ge(sum_mm, m + 1)
                if m:
                    dve.wait_ge(att_ok, m)
                dve.reciprocal(rden, ps[:, 7, :]).then_inc(rd_ok, 1)
                dve.wait_ge(rd_ok, m + 1)
                dve.tensor_tensor(att[:, slot], att[:, slot], rden, ALU.mult).then_inc(att_ok, 1)

            def add_attention(b, c):
                dve.wait_ge(at_mm, 4 * b + 2 * c + 2)
                row = h_res[:, 4 * b + 2 * c:4 * b + 2 * c + 2, :].rearrange("p f (s u) -> p f u s", u=2)
                dve.tensor_tensor(row, ps[:, 7, :].rearrange("p (f u s) -> p f u s", f=2, u=2), row, ALU.add
                                  ).then_inc(at_add, 1)

            dve.wait_ge(consts, 5)
            for b in range(-1, B):
                for q in range(4):
                    for i in range(4):
                        if b + 1 < B:
                            maxima(4 * q + i, (b + 1) * NH + 4 * q + i)
                        if b >= 0 and q and i == 2:
                            normalise(4 * b + q - 1, (q - 1) % 2)
                        if b >= 0 and q == 2 and i == 3:
                            add_attention(b, 0)
                if b >= 0:
                    normalise(4 * b + 3, 1)
                    add_attention(b, 1)
                if b + 1 < B:
                    dve.wait_ge(max_out, 8 * NH * (b + 2))
                    step(dve.tensor_tensor(mx1, mx[:, 0], mx[:, 1], ALU.max))
                    if b >= 0:
                        dve.wait_ge(mx_mm, b + 1)
                    step(dve.tensor_copy(mpad[:, :, NPART:NPART + NH], mx1))
                    step(dve.tensor_tensor(mlo, mx1, mpad[:, :, NPART:NPART + NH], ALU.subtract))
                    dve.tensor_copy(mpad[:, :, NPART + NH:P], mlo).then_inc(mx_pad, 1)

            if stop >= 2:
                for j in range(NT + 1):
                    if j < NT:
                        if j == 0:
                            dve.wait_ge(at_add, 2 * B)
                        ln_stats(j)
                    if j:
                        ln_apply(1, j - 1)
                for j in range(NT):
                    dve.wait_ge(f2_mm, j + 1)
                    if j >= 2:
                        dve.wait_ge(ffn_add, j - 1)
                    dve.tensor_tensor(ffn_sum[:, j % 2], ps[:, 6 + j % 2, 0:D], bias_2, ALU.add).then_inc(f2_out, 1)
                    dve.wait_ge(f2_out, j + 1)
                    dve.tensor_tensor(h_res[:, j, :], h_res[:, j, :], ffn_sum[:, j % 2], ALU.add).then_inc(ffn_add, 1)
            if stop >= 3:
                dve.wait_ge(ffn_add, NT)

                def squares(j):
                    dve.wait_ge(c_out, j + 1)
                    dve.tensor_copy(ab[:, tile_at(j), :], ps[:, 4 * (j % 2) + 2, 0:2 * NH]).then_inc(c_ab, 1)
                    kq = kq_src[:, :, j % 4, j // 4, :]
                    step(dve.tensor_tensor(sq[:, 0].rearrange("p (w n) -> p w n", w=2), kq, kq, ALU.mult))
                    dve.tensor_reduce(ssum[:, tile_at(j), :], sq[:, 0].rearrange("p (h d) -> p h d", d=DH), AX.X, ALU.add).then_inc(ss_ok, 1)
                    dve.wait_ge(ss_ok, j + 1)

                for j in range(NT + 2):
                    if j < NT:
                        ln_stats(j)
                    if 1 <= j <= NT:
                        ln_apply(2, j - 1)
                    if j >= 2:
                        squares(j - 2)
                z, u, ga, be, nab, s1, s2, q1 = small
                dve.wait_ge(d_w3, 80)
                dve.wait_ge(c_ab, NT)
                dve.tensor_tensor(z, ab[:, :, 0:NH], dt_bias.unsqueeze(1).broadcast_to([P, NT, NH]), ALU.add).then_inc(dve_ab, 1)
                dve.wait_ge(act_ab, 4)
                step(dve.tensor_scalar(s1, u, 2.0, None, ALU.add))
                step(dve.reciprocal(s2, s1))
                step(dve.tensor_tensor(s1, u, s2, ALU.mult))
                step(dve.tensor_tensor(s2, s1, s1, ALU.mult))
                step(dve.tensor_scalar(q1, s2, 1.0 / 15, None, ALU.mult))
                for m in (13, 11, 9, 7, 5, 3):
                    step(dve.scalar_tensor_tensor(out=q1, in0=q1, scalar=1.0 / m, in1=s2, op0=ALU.add, op1=ALU.mult))
                step(dve.scalar_tensor_tensor(out=q1, in0=q1, scalar=1.0, in1=s1, op0=ALU.add, op1=ALU.mult))
                step(dve.tensor_scalar(z, z, 0.0, None, ALU.max))
                step(dve.scalar_tensor_tensor(out=z, in0=q1, scalar=2.0, in1=z, op0=ALU.mult, op1=ALU.add))
                dve.tensor_tensor(ga, z, a_exp.unsqueeze(1).broadcast_to([P, NT, NH]), ALU.mult).then_inc(dve_ab, 1)
                step(dve.tensor_scalar(be, be, 1.0, None, ALU.add))
                step(dve.reciprocal(s1, be))
                dve.wait_ge(nrm_ok, 1)
                step(dve.tensor_scalar(rnorm, rnorm, 1e-12, None, ALU.max))
                step(dve.reciprocal(ssum, rnorm))
                step(dve.tensor_scalar(ssum[:, :, NH:], ssum[:, :, NH:], DH ** -0.5, None, ALU.mult))
                for j in range(NT):
                    kq = kq_src[:, :, j // B, j % B, :].rearrange("p w (h d) -> p w h d", d=DH)
                    for w in range(2):
                        dve.tensor_tensor(kq[:, w], kq[:, w], ssum[:, j, w * NH:(w + 1) * NH].unsqueeze(2).broadcast_to([P, NH, DH]),
                                          ALU.mult)
                    v = v_src[:, j // B, :, j % B]
                    ins = dve.tensor_tensor(v, v, s1[:, j, :].unsqueeze(1).unsqueeze(3).broadcast_to([P, 2, NH, 8]), ALU.mult)
                step(ins)
                for j in range(NT):
                    kq = kq_src[:, :, j // B, j % B, :]
                    step(dve.tensor_tensor(sq[:, 0, 0:D], kq[:, 0], kq[:, 1], ALU.mult))
                    step(dve.tensor_reduce(kqdot[:, j, :], sq[:, 0, 0:D].rearrange("p (h d) -> p h d", d=DH), AX.X, ALU.add))
                dve.wait_ge(act_ab, 5)
                dve.scalar_tensor_tensor(out=nab, in0=ga, scalar=-1.0, in1=s1, op0=ALU.mult, op1=ALU.mult).then_inc(rec_src, 1)
                for n in range(1, NBANK, 2):
                    take_turned(dve, n)
                step(dve.memset(state, 0.0))
                dve.wait_ge(rt_out[0], NBANK)
                dve.wait_ge(rt_out[1], NBANK)

                def rec_step(t, first):
                    n = 5 * t
                    if not first:
                        dve.wait_ge(rec, n)
                    dve.tensor_tensor(prod, state.unsqueeze(1).broadcast_to([P, 2, 8, DH]),
                                      kq_rec[:, ds(t, 1)].rearrange("p o w d -> p (o w) d").unsqueeze(2).broadcast_to([P, 2, 8, DH]),
                                      ALU.mult).then_inc(rec, 1)
                    dve.wait_ge(rec, n + 1)
                    r = r_rec[:, ds(t, 1)].rearrange("p o w i -> p (o w) i")
                    dve.tensor_reduce(r, prod, AX.X, ALU.add).then_inc(rec, 1)
                    dve.wait_ge(rec, n + 2)
                    delta = d_rec[:, ds(t, 1)].rearrange("p o i -> p (o i)")
                    dve.scalar_tensor_tensor(out=delta, in0=r[:, 0], scalar=sc_rec[:, ds(t, 1), 1], in1=v_rec[:, ds(t, 1)].rearrange("p o i -> p (o i)"),
                                             op0=ALU.mult, op1=ALU.add).then_inc(rec, 1)
                    dve.wait_ge(rec, n + 3)
                    key = kq_rec[:, ds(t, 1), 0]
                    dve.tensor_tensor(outer, delta.unsqueeze(2).broadcast_to([P, 8, DH]), key.broadcast_to([P, 8, DH]), ALU.mult
                                      ).then_inc(rec, 1)
                    dve.wait_ge(rec, n + 4)
                    dve.scalar_tensor_tensor(out=state, in0=state, scalar=sc_rec[:, ds(t, 1), 0], in1=outer,
                                             op0=ALU.mult, op1=ALU.add).then_inc(rec, 1)

                for t in range(4):
                    rec_step(t, t == 0)
                with dve.Fori(1, S // 4) as t4:
                    for i in range(4):
                        rec_step(t4 * 4 + i, False)
                dve.wait_ge(rec, 5 * S)
                step(dve.tensor_tensor(r_rec[:, :, 1, :], r_rec[:, :, 1, :], sc_rec[:, :, 0:1].broadcast_to([P, S, 8]), ALU.mult))
                step(dve.tensor_tensor(d_rec, d_rec, sc_rec[:, :, 2:3].broadcast_to([P, S, 8]), ALU.mult))
                dve.tensor_tensor(d_rec, d_rec, r_rec[:, :, 1, :], ALU.add).then_inc(o_ok, 1)
                for n in range(8):
                    ftu, ih = divmod(n, 2)
                    dve.wait_ge(ot_mm, n + 1)
                    for half in range(2):
                        dst = o_tok.rearrange("p (b f) (h a c) -> p b f h a c", f=4, a=2, c=8)[:, :, ftu, :, half, 4 * ih:4 * ih + 4]
                        src = ps[:, n % 2, :].rearrange("p (c a b h) -> p a b h c", c=4, a=2, b=B)[:, half]
                        ins = dve.tensor_copy(dst, src)
                    ins.then_inc(ot_out, 1)
                dve.wait_ge(ot_out, 8)
                ms = small[0]
                for j in range(NT):
                    step(dve.tensor_tensor(sq[:, 0, 0:D], o_tok[:, j, :], o_tok[:, j, :], ALU.mult))
                    step(dve.tensor_reduce(ms[:, j, :], sq[:, 0, 0:D].rearrange("p (h d) -> p h d", d=DH), AX.X, ALU.add))
                dve.tensor_scalar(ms, ms, 1.0 / DH, 1e-6, ALU.mult, ALU.add).then_inc(rms_ss, 1)
                dve.wait_ge(rms_rt, 1)
                step(dve.reciprocal(s1, ms))
                dve.wait_ge(gate_ok, 1)
                for j in range(NT):
                    o = o_tok[:, j, :].rearrange("p (h d) -> p h d", d=DH)
                    step(dve.tensor_tensor(o, o, s1[:, j, :].unsqueeze(2).broadcast_to([P, NH, DH]), ALU.mult))
                    dve.tensor_tensor(o_tok[:, j, :], o_tok[:, j, :], gate[:, j, :], ALU.mult).then_inc(og_ok, 1)
                for j in range(NT):
                    dve.wait_ge(wo_mm, j + 1)
                    dve.tensor_tensor(h_res[:, j, :], ps[:, 4 + j % 2, 0:D], h_res[:, j, :], ALU.add).then_inc(attn_add, 1)
            if stop >= 4:
                dve.wait_ge(attn_add, NT)
                for j in range(NT + 1):
                    if j < NT:
                        ln_stats(j)
                    if j:
                        ln_apply(3, j - 1)

                def over(v, n=NE):
                    return v.unsqueeze(2).broadcast_to([P, NT, n])

                def each(v, n=NT):
                    return v.unsqueeze(1).broadcast_to([P, n, NE])

                dve.wait_ge(lg_mm, 1)
                step(dve.tensor_tensor(lg, ps[:, 0, 0:NT * NE].rearrange("p (j e) -> p j e", e=NE), each(rb), ALU.add))
                step(dve.tensor_reduce(lmax, lg, AX.X, ALU.max))
                dve.tensor_tensor(lexp, lg, over(lmax), ALU.subtract).then_inc(sh_ok, 1)
                step(dve.tensor_tensor(eq, lg, over(lmax), ALU.is_ge))
                step(dve.tensor_tensor(eq, eq, each(em8), ALU.mult))
                step(dve.tensor_reduce(pos, eq, AX.X, ALU.min))
                dve.tensor_tensor(onehot, each(em8), over(pos), ALU.is_equal).then_inc(hot_ok, 1)
                dve.wait_ge(lexp_ok, 1)
                step(dve.tensor_reduce(pmax, lexp, AX.X, ALU.add))
                step(dve.reciprocal(pmax, pmax))
                dve.wait_ge(cnt_mm, 1)
                totals = ps[:, 2, 0:NT * NE].rearrange("p (j e) -> p j e", e=NE)
                step(dve.tensor_copy(cnt[:, 0], totals))
                src, w = 0, 1
                while w < NT:
                    step(dve.tensor_copy(cnt[:, 1 - src, 0:w], cnt[:, src, 0:w]))
                    step(dve.tensor_tensor(cnt[:, 1 - src, w:NT], cnt[:, src, w:NT], cnt[:, src, 0:NT - w], ALU.add))
                    src, w = 1 - src, 2 * w
                step(dve.tensor_tensor(cmp_[:, 0:NE], cnt[:, src, NT - 1].unsqueeze(2).broadcast_to([P, NE, NE]), each(thr, NE), ALU.is_gt))
                step(dve.tensor_reduce(ends[:, 0], cmp_[:, 0:NE], AX.X, ALU.add))
                step(dve.tensor_copy(ends[:, 2], ends[:, 0]))
                at_, w = 0, 1
                while w < NE:
                    step(dve.tensor_copy(ends[:, 1 - at_, 0:w], ends[:, at_, 0:w]))
                    step(dve.tensor_tensor(ends[:, 1 - at_, w:NE], ends[:, at_, w:NE], ends[:, at_, 0:NE - w], ALU.add))
                    at_, w = 1 - at_, 2 * w
                step(dve.tensor_tensor(base, ends[:, at_], ends[:, 2], ALU.subtract))
                step(dve.tensor_scalar(base, base, float(ET), None, ALU.mult))
                step(dve.tensor_tensor(cmp_, each(ends[:, at_], NET), tile_no.unsqueeze(2).broadcast_to([P, NET, NE]), ALU.is_le))
                step(dve.tensor_reduce(te[:, 0:NET], cmp_, AX.X, ALU.add))
                step(dve.tensor_scalar(te_i[:, 0:NET], te[:, 0:NET], float(NE - 1), None, ALU.min))
                step(dve.tensor_tensor(cnt[:, 2], cnt[:, src], totals, ALU.subtract))
                step(dve.tensor_tensor(cnt[:, 2], ps[:, 1, 0:NT * NE].rearrange("p (j e) -> p j e", e=NE), cnt[:, 2], ALU.add))
                step(dve.tensor_tensor(cnt[:, 2], cnt[:, 2], each(base), ALU.add))
                step(dve.tensor_tensor(cnt[:, 2], cnt[:, 2], onehot, ALU.mult))
                step(dve.tensor_reduce(pos, cnt[:, 2], AX.X, ALU.add))
                dve.tensor_copy(pos_i, pos).then_inc(pos_ok, 1)

                def expert(t, slot, first):
                    for m in range(HC):
                        dve.wait_ge(e_silu, t * HC + m + 1)
                        if m == 0 and not first:
                            dve.wait_ge(e2_mm, t - 1)
                        dve.tensor_tensor(eu[:, slot, m, :], ps[:, m % 4, ET:2 * ET], silu[:, m % 2], ALU.mult).then_inc(e1_out, 1)
                    dve.wait_ge(e2_mm, t + 1)
                    if not first:
                        dve.wait_ge(d_ys[slot], t * 8 if slot == 0 else t * 8 - 8)
                    dve.tensor_copy(ys[:, slot], ps[:, 4:6, 0:D]).then_inc(e2_out, 1)

                expert_tiles(dve, expert)
                dve.wait_ge(d_yg, 16 * NT)
                for j in range(NT):
                    dve.scalar_tensor_tensor(out=h_res[:, j, :], in0=yg[:, j, :], scalar=pmax[:, j:j + 1], in1=h_res[:, j, :],
                                             op0=ALU.mult, op1=ALU.add).then_inc(fin, 1)


def kernel(**inputs):
    import concourse.bacc as bacc
    from concourse import mybir as _mybir
    from concourse.bass_utils import run_bass_kernel_spmd

    n = {name: np.asarray(v) for name, v in inputs.items()}
    x = n["x"].reshape(B, 2, P, 2, D, TOK_D)
    arrays = {
        "x_t": x.transpose(5, 4, 0, 1, 3, 2).reshape(TOK_D * D, B * S),
        "tok_ws_t": n["L0_tok_weighted_sum"].T,
        "tok_w_t": n["L0_tok_weight"].T,
        "keys_t": n["L0_attn_keys"][0].T,
        "vals_t": n["L0_attn_values"][0].T,
        "wq_t": n["L0_attn_Wq_w"].T,
        "wk_t": n["L0_attn_Wk_w"].T,
        "wv_t": n["L0_attn_Wv_w"].T,
        "bias_qk": np.stack([n["L0_attn_Wq_b"], n["L0_attn_Wk_b"]]).reshape(2, FC, P).transpose(2, 0, 1),
        "bias_v": n["L0_attn_Wv_b"][None],
        "w1_t": n["L0_ffn_w1"].T,
        "w2_t": n["L0_ffn_w2"].T,
        "b1": n["L0_ffn_b1"].reshape(HC, P).T,
        "b2": n["L0_ffn_b2"][None],
        "w_cat": np.concatenate([n["L1_attn_" + w] for w in ("Wk", "Wq", "Wv", "Wgate", "Walpha", "Wbeta")], axis=1),
        "w_out": n["L1_attn_Wout"],
        "dt_bias": n["L1_attn_dt_bias"][None],
        "a_log": n["L1_attn_A_log"][None],
        "rms_w": n["L1_attn_rms_w"][None],
        "router_w": n["L1_ffn_router_w"],
        "router_b": n["L1_ffn_router_b"][None],
        "ew1": n["L1_ffn_w1"],
        "ew2": n["L1_ffn_w2"],
        "tri": np.triu(np.ones((P, P), np.float32), 1),
        "em8": np.arange(-NE, 0, dtype=np.float32)[None],
        "thr": np.arange(0, NE * ET, ET, dtype=np.float32)[None],
        "tile_no": np.arange(NET, dtype=np.float32)[None],
    }
    arrays = {f"in_{name}": np.ascontiguousarray(v) for name, v in arrays.items()}
    nc = bacc.Bacc("TRN2", target_bir_lowering=False, num_devices=1)
    aps = {name[3:]: nc.dram_tensor(name, v.shape, _mybir.dt.from_np(v.dtype), kind="ExternalInput").ap()
           for name, v in arrays.items()}
    out = nc.dram_tensor("out", [B * S, D], F32, kind="ExternalOutput").ap()
    build(nc, aps, out, STOP)
    r = run_bass_kernel_spmd(nc, [arrays], core_ids=[0])
    return r.results[0]["out"].reshape(B, S, D)
```

```python
from contextlib import ExitStack

import numpy as np
from concourse import mybir
from concourse.bass import IndirectOffsetOnAxis, ds

F32 = mybir.dt.float32
BF16 = mybir.dt.bfloat16
I32 = mybir.dt.int32
U32 = mybir.dt.uint32
ALU = mybir.AluOpType
ACT = mybir.ActivationFunctionType
AX = mybir.AxisListType

P = 128
B, S, D = 4, 512, 256
NT = B * S // P
FC = D // P
TOK_D = 4
NK, NH, DH = 1024, 16, 16
KC = NK // P
QT = S // P
HC = 8
NE = 8
ET = 256
NET = (B * S + NE * (ET - 1)) // ET
CAT = 4 * D + 2 * NH
NPART = 96
HID = 1024
LN_EPS = 1e-5


STOP = 4


def build(nc, a, out, stop):
    with ExitStack() as ctx:
        def sb(name, shape, dt=F32):
            return ctx.enter_context(nc.sbuf_tensor(name, shape, dt))

        def sem(name):
            return ctx.enter_context(nc.semaphore(name))

        ps = ctx.enter_context(nc.psum_tensor("ps", [P, 8, 512], F32))
        h_res = sb("h_res", [P, NT, D])
        xn = sb("xn", [P, NT, D])
        ident = sb("ident", [P, P])
        ident_b = sb("ident_b", [P, P], BF16)
        bn = sb("bn", [P, 2, 6])
        mv = sb("mv", [P, NT, 2])
        var_eps = sb("var_eps", [P, NT])
        rstd = sb("rstd", [P, NT])
        ones = sb("ones", [P, P])
        minus_half = sb("minus_half", [P, NT * 32])
        arena = sb("arena", [P, 44000])

        def view(at, shape, dt=F32):
            n = int(np.prod(shape))
            words = n if dt in (F32, I32, U32) else n // 2
            v = arena[:, at:at + words]
            if dt != F32:
                v = v.bitcast(dt)
            names = " ".join(f"d{i}" for i in range(len(shape)))
            if len(shape) > 1:
                v = v.rearrange(f"p ({names}) -> p {names}", **{f"d{i}": s for i, s in enumerate(shape)})
            return v, at + words

        at = 0
        xnt, at = view(at, [FC, NT * P])
        kstk, at = view(at, [NH, NK], BF16)
        at_q1 = at + NH * S // 2
        qstk, at = view(at, [2, NH, S], BF16)
        vaug, at = view(at, [KC, NH, 32])
        at_att = at
        x_t = []
        for b in range(B - 1):
            v, at = view(at, [8, S])
            x_t.append(v)
        x_t.append(view(at_q1 - NH * S // 2, [8, S])[0])
        w_tok, at = view(at, [8, D])
        ws_t, w_at = view(0, [FC, D])
        w_bc, _ = view(w_at, [TOK_D, D])
        at_tok = at
        at = at_att
        prob, at = view(at, [2, 4, S])
        att, at = view(at, [2, S])
        rden, at = view(at, [S])
        spread, at = view(at, [P])
        gather, at = view(at, [2, P])
        mx, at = view(at, [2, QT, NH])
        mx1, at = view(at, [QT, NH])
        mlo, at = view(at, [QT, NH])
        mpad, at = view(at, [QT, P], BF16)
        mrow, at = view(at, [S], BF16)
        at_free = at
        assert at <= at_tok
        at = at_tok
        keys_t, k_at = view(at_q1, [FC, NK])
        vals_t, _ = view(k_at, [FC, NK])
        wq_t, at = view(at, [FC, D])
        wk_t, at = view(at, [FC, D])
        wv_t, at = view(at, [FC, D])
        bias_qk, at = view(at, [2, FC])
        bias_v, at = view(at, [D])
        sel, at = view(at, [NH])
        proj, at = view(at, [2, S])
        part, at = view(at, [2, 3, S], BF16)
        vtmp, at = view(at, [2, D])
        assert at <= 44000, at
        at = at_free
        w1, at = view(at, [FC, HID])
        w2, at = view(at, [HC, D])
        w_abs, at = view(at, [HC * D])
        w_mean, at = view(at, [HC * D])
        w_sign, at = view(at, [HC * D])
        bias_1, at = view(at, [HC])
        bias_2, at = view(at, [D])
        assert at <= 44000, at
        hid, _ = view(FC * NT * P, [2, HC, S])
        ffn_sum, _ = view(FC * NT * P + 2 * HC * S, [2, D])

        R = NT * D
        kq_tok, _ = view(0, [2, NT, D])
        v_tok, _ = view(2 * R, [NT, D])
        gp, _ = view(3 * R, [NT, NH, 2, DH])
        a_u, _ = view(6 * R, [DH, 16, DH])
        gk, _ = view(4 * R, [NT * NH, DH])
        comb_qs, _ = view(4 * R, [NT, D])
        t_u, _ = view(3 * R, [DH, 16, DH])
        u_tok, _ = view(3 * R, [NT, D])
        vgk, _ = view(2 * R, [2, 2 * R])
        decay, _ = view(5 * R, [DH, 16, DH])
        t_prod, _ = view(4 * R, [R])
        k_one, at = view(6 * R, [2, 2, 2, P])
        kq_f, at = view(at, [2, 2, 2, P])
        sq, at = view(at, [2 * D])
        pick_dve, at = view(at, [4, 8, DH])
        pick_act, at = view(at, [2, 4, 8, DH])
        t_blk, _ = view(5 * R, [NT * NH, 2, DH])
        wq_t5, _ = view(5 * R, [NT, 2, 2, B, 32])
        o_tok, _ = view(5 * R, [NT, D])
        o_f, _ = view(6 * R, [FC, B, S])
        p_blk, _ = view(7 * R, [NT * NH, 2, DH])
        xnt4, at = view(7 * R, [FC, NT * P])
        w_cat, at = view(at, [FC, CAT])
        k_even, k_odd = kq_tok[:, 0], v_tok
        at = R
        xo, at = view(at, [4, D])
        comb_a, at = view(at, [2, 2, D])
        w_out, at = view(9 * R, [FC, D])
        small = []
        for _ in range(8):
            v, at = view(at, [NT, NH])
            small.append(v)
        w_neg, _ = view(at, [2, D])
        ab, at = view(at, [NT, 2 * NH])
        ssum, at = view(at, [NT, 2 * NH])
        rnorm, at = view(at, [NT, 2 * NH])
        state, s_at = view(at - NT * 4 * NH, [B, 2, 2, DH])
        s_dec, s_at = view(s_at, [B, 2, 2, DH])
        dt_bias, at = view(at, [NH])
        a_exp, at = view(at, [NH])
        rms_w, at = view(at, [DH])
        ab_u, at = view(at, [2, 16, DH])
        gam_u, at = view(at, [16, DH])
        gd, at = view(at, [2, NT * NH])
        gf, at = view(at, [2, 8, 16])
        gam_m, at = view(at, [8, 16])
        at_dconst = at
        half_mask, at = view(at, [2])
        eye16, at = view(at, [DH * DH])
        head_mask, at = view(at, [32])
        swap, at = view(at, [P])
        head_sel, at = view(at, [2, P])
        tile_mask, at = view(at, [8])
        dconst, at = view(at_dconst, [at - at_dconst])
        assert at <= 43744, at
        zero_row, _ = view(43744, [D])
        at = FC * NT * P
        rw, at = view(at, [FC, NE])
        rb, at = view(at, [NE])
        tri, at = view(at, [P])
        em8, at = view(at, [NE])
        thr, at = view(at, [NE])
        tile_no, at = view(at, [NET])
        lg, at = view(at, [NT, NE])
        lmax, at = view(at, [NT])
        eq, at = view(at, [NT, NE])
        onehot, at = view(at, [NT, NE])
        lexp, at = view(at, [NT, NE])
        pmax, at = view(at, [NT])
        cnt, at = view(at, [3, NT, NE])
        cmp_, at = view(at, [NET, NE])
        ends, at = view(at, [3, NE])
        base, at = view(at, [NE])
        pos, at = view(at, [NT])
        pos_i, at = view(at, [NT], U32)
        te, at = view(at, [NET + 1])
        te_i, at = view(at, [NET + 1], U32)
        ew1, at = view(at, [2, FC, 2 * HID])
        ew2, at = view(at, [2, HC, D])
        xs, at = view(at, [2, 2, D])
        xst, at = view(at, [2, FC, ET])
        silu, at = view(at, [2, ET])
        eu, at = view(at, [2, HC, ET])
        ys, at = view(at, [2, 2, D])
        yg, at = view(at, [NT, D])
        assert at <= 43744, at
        xs_dram = nc.dram_tensor("xs_dram", [NET * ET, D], F32, kind="Internal").ap()
        ys_dram = nc.dram_tensor("ys_dram", [NET * ET, D], F32, kind="Internal").ap()
        gate = xn[:, :, :]
        qk_parts = nc.dram_tensor("qk_parts", [3, D, NK + B * S], BF16, kind="Internal").ap()

        d_small = sem("d_small")
        d_kv = sem("d_kv")
        d_x = [sem(f"d_x{b}") for b in range(B)]
        consts = sem("consts")
        ident_ok = sem("ident_ok")
        wtok_ok = sem("wtok_ok")
        mm_tok = sem("mm_tok")
        tok_out = sem("tok_out")
        dve_step = sem("dve_step")
        pool_step = sem("pool_step")
        ln_var = sem("ln_var")
        ln_rstd = sem("ln_rstd")
        ln_out = sem("ln_out")
        tp_mm = sem("tp_mm")
        tp_out = sem("tp_out")
        pj_mm = sem("pj_mm")
        pj_out = sem("pj_out")
        pj_split = sem("pj_split")
        d_part = [sem("d_part0"), sem("d_part1")]
        d_kstk = sem("d_kstk")
        d_qstk = [sem(f"d_qstk{b}") for b in range(B)]
        sel_ok = sem("sel_ok")
        v_mm = sem("v_mm")
        v_out = sem("v_out")
        st_mm = sem("st_mm")
        exp_out = sem("exp_out")
        sm_mm = sem("sm_mm")
        max_out = sem("max_out")
        av_mm = sem("av_mm")
        av_out = sem("av_out")
        mx_pad = sem("mx_pad")
        mx_mm = sem("mx_mm")
        mx_row = sem("mx_row")
        d_mrow = sem("d_mrow")
        at_mm = sem("at_mm")
        at_add = sem("at_add")
        rd_ok = sem("rd_ok")
        sum_mm = sem("sum_mm")
        att_ok = sem("att_ok")
        h_pre = sem("h_pre")
        d_out = sem("d_out")
        zero_ok = sem("zero_ok")
        d_zero = sem("d_zero")
        d_rt = sem("d_rt")
        lg_mm = sem("lg_mm")
        lg_out = sem("lg_out")
        hot_ok = sem("hot_ok")
        sh_ok = sem("sh_ok")
        lexp_ok = sem("lexp_ok")
        cnt_mm = sem("cnt_mm")
        pos_ok = sem("pos_ok")
        d_disp = sem("d_disp")
        d_ew = [sem("d_ew0"), sem("d_ew1")]
        et_mm = sem("et_mm")
        et_out = sem("et_out")
        e1_mm = sem("e1_mm")
        e_silu = sem("e_silu")
        e1_out = sem("e1_out")
        e2_mm = sem("e2_mm")
        e2_out = sem("e2_out")
        d_ys = [sem("d_ys0"), sem("d_ys1")]
        d_yg = sem("d_yg")
        fin = sem("fin")
        d_w = sem("d_w")
        abs_ok = sem("abs_ok")
        mean_mm = sem("mean_mm")
        mean_ok = sem("mean_ok")
        w_ok = sem("w_ok")
        f1_mm = sem("f1_mm")
        f1_out = sem("f1_out")
        f2_mm = sem("f2_mm")
        f2_out = sem("f2_out")
        ffn_add = sem("ffn_add")
        d_w3 = sem("d_w3")
        c_mm = sem("c_mm")
        c_out = sem("c_out")
        c_ab = sem("c_ab")
        ss_ok = sem("ss_ok")
        nrm_ok = sem("nrm_ok")
        act_ab = sem("act_ab")
        dve_ab = sem("dve_ab")
        gate_ok = sem("gate_ok")
        kq_ok = sem("kq_ok")
        alpha_ok = sem("alpha_ok")
        gt_mm = sem("gt_mm")
        gt_out = sem("gt_out")
        g_mm = sem("g_mm")
        pick_dve_ok = sem("pick_dve_ok")
        pick_act_ok = sem("pick_act_ok")
        g_out = sem("g_out")
        su_mm = sem("su_mm")
        du_ok = sem("du_ok")
        gd_mm = sem("gd_mm")
        gd_ok = sem("gd_ok")
        dt_mm = sem("dt_mm")
        dt_out = sem("dt_out")
        gu_mm = sem("gu_mm")
        gu_out = sem("gu_out")
        gk_ok = sem("gk_ok")
        gm_ok = sem("gm_ok")
        gf_mm = sem("gf_mm")
        gf_ok = sem("gf_ok")
        tt_mm = sem("tt_mm")
        tt_out = [sem("tt_out_act"), sem("tt_out_dve")]
        vb_ok = sem("vb_ok")
        qg_ok = sem("qg_ok")
        kt_ok = sem("kt_ok")
        uw_mm = sem("uw_mm")
        uw_out = [sem("uw_out_act"), sem("uw_out_dve")]
        wq_mm = sem("wq_mm")
        wq_act = sem("wq_act")
        wq_dve = sem("wq_dve")
        s_ok = [sem("s_ok0"), sem("s_ok1")]
        r_mm = [sem("r_mm0"), sem("r_mm1")]
        xo_ok = [sem("xo_ok0"), sem("xo_ok1")]
        s_mm = [sem("s_mm0"), sem("s_mm1")]
        sg_ok = [sem("sg_ok0"), sem("sg_ok1")]
        cb_act = sem("cb_act")
        comb_ok = sem("comb_ok")
        o_mm = sem("o_mm")
        o_out = sem("o_out")
        rms_ss = sem("rms_ss")
        rms_rt = sem("rms_rt")
        og_ok = sem("og_ok")
        og_mm = sem("og_mm")
        og_out = sem("og_out")
        wo_mm = sem("wo_mm")
        attn_add = sem("attn_add")

        def take_inverse(eng, n):
            half, ig = divmod(n, 4)
            eng.wait_ge(tt_mm, n + 1)
            for par in range(2):
                dst = t_blk[:, 128 * half:128 * half + 128, par, 4 * ig:4 * ig + 4]
                src = ps[:, 4 + n % 2, :].rearrange("p (i c) -> p c i", i=4)
                if eng is nc.vector:
                    ins = eng.tensor_scalar(dst, src, half_mask[:, par:par + 1], None, ALU.mult)
                else:
                    ins = eng.activation(dst, src, ACT.Copy, scale=half_mask[:, par:par + 1])
            ins.then_inc(tt_out[n % 2], 1)

        def take_uw(eng, t):
            hh = 1 if eng is nc.vector else 0
            eng.wait_ge(uw_mm, t + 1)
            if t >= 2:
                eng.wait_ge(wq_mm, t - 1)
            src = ps[:, 2 * (t % 2) + hh, 0:256].rearrange("p (r o x) -> p r o x", r=4, o=2)
            dst_u = u_tok[:, t, :].rearrange("p (r e o x) -> p r e o x", r=4, e=2, o=2)[:, :, hh]
            dst_w = w_neg[:, t % 2, P * hh:P * hh + P].rearrange("p (r o x) -> p r o x", r=4, o=2)
            if hh:
                eng.tensor_copy(dst_u, src[:, :, :, 0:DH])
                ins = eng.tensor_scalar(dst_w, src[:, :, :, DH:], -1.0, None, ALU.mult)
            else:
                eng.copy(dst_u, src[:, :, :, 0:DH])
                ins = eng.activation(dst_w, src[:, :, :, DH:], ACT.Copy, scale=-1.0)
            ins.then_inc(uw_out[hh], 1)

        def half_products(half):
            return ps[:, 2:6, 0:256].rearrange("p r (e i) -> p r e i", e=8)[:, :, :, DH * half:DH * half + DH]

        def out_tile(n):
            ft, b, u = n // 8, n % 8 // 2, n % 2
            return 4 * b + 2 * ft + u
        def expert_tiles(eng, tile):
            tile(0, 0, True)
            tile(1, 1, True)
            with eng.Fori(1, NET // 2) as i:
                tile(i * 2, 0, False)
                tile(i * 2 + 1, 1, False)
            if NET % 2:
                tile(NET - 1, 0, False)

        block = ctx.enter_context(nc.Block())
        NU = 4 + 2 * B

        def turn_bank(stage, j):
            return ((2, 3), (2, 3), (3, 7), (3, 7))[stage][j % 2]

        def unit_cols(u):
            return (u // 2) * S

        @block.sync
        def _(sp):
            sp.dma_start(ws_t, a["tok_ws_t"].rearrange("(c p) n -> p c n", p=P)).then_inc(d_small, 16)
            sp.dma_start(w_bc, a["tok_w_t"].rearrange("(a d) n -> a d n", a=1).broadcast_to([P, TOK_D, D])).then_inc(d_small, 16)
            sp.dma_start(bias_qk, a["bias_qk"]).then_inc(d_small, 16)
            sp.dma_start(bias_v, a["bias_v"].broadcast_to([P, D])).then_inc(d_small, 16)
            for dst, name in ((keys_t, "keys_t"), (wk_t, "wk_t"), (vals_t, "vals_t"), (wv_t, "wv_t"), (wq_t, "wq_t")):
                sp.dma_start(dst, a[name].rearrange("(c p) n -> p c n", p=P)).then_inc(d_kv, 16)
            order_k, order_q = (0, 1, 0, 1, 2, 0), (0, 0, 1, 1, 0, 2)
            for u in range(NU):
                sp.wait_ge(pj_split, u + 1)
                m = u % 2
                sp.dma_start(qk_parts[:, m * P:(m + 1) * P, unit_cols(u):unit_cols(u) + S].rearrange("t p n -> p t n"),
                             part[:, u % 2]).then_inc(d_part[u % 2], 16)
                if u == 3:
                    sp.wait_ge(d_part[0], 32)
                    sp.wait_ge(d_part[1], 32)
                    for r, t in enumerate(order_k):
                        sp.dma_start(kstk[r * DH:(r + 1) * DH], qk_parts[t, :, 0:NK].rearrange("(h d) n -> d h n", d=DH)
                                     ).then_inc(d_kstk, 16)
                if u >= NU - 3 and u % 2:
                    b = (u - (NU - 3)) // 2
                    sp.wait_ge(d_part[0], 16 * (b + 3))
                    sp.wait_ge(d_part[1], 16 * (b + 3))
                    sp.wait_ge(mm_tok, NT)
                    for r, t in enumerate(order_q):
                        sp.dma_start(qstk[r * DH:(r + 1) * DH, b],
                                     qk_parts[t, :, NK + b * S:NK + (b + 1) * S].rearrange("(h d) n -> d h n", d=DH)
                                     ).then_inc(d_qstk[b], 16)
            for m in range(2):
                sp.wait_ge(d_part[m], 16 * (NU // 2))
            sp.wait_ge(pj_mm, NU)
            sp.wait_ge(v_out, KC)
            for dst, src in ((w1, a["w1_t"].rearrange("(c p) n -> p c n", p=P)), (w2, a["w2_t"].rearrange("(c p) n -> p c n", p=P)),
                             (bias_1, a["b1"]), (bias_2, a["b2"].broadcast_to([P, D]))):
                sp.dma_start(dst, src).then_inc(d_w, 16)
            for b in range(B):
                sp.wait_ge(mx_row, b + 1)
                sp.dma_start(qstk[NPART:P, b % 2], mrow[NPART:P].unsqueeze(1).broadcast_to([P - NPART, NH, S])).then_inc(d_mrow, 16)
                if 1 <= b < B - 1:
                    sp.wait_ge(st_mm, 64 * b)
                    for r, t in enumerate(order_q):
                        sp.dma_start(qstk[r * DH:(r + 1) * DH, (b + 1) % 2],
                                     qk_parts[t, :, NK + (b + 1) * S:NK + (b + 2) * S].rearrange("(h d) n -> d h n", d=DH)
                                     ).then_inc(d_qstk[b + 1], 16)
            if stop == 1:
                sp.wait_ge(at_add, 2 * B)
            if stop >= 2:
                sp.wait_ge(ffn_add, NT)
            if stop >= 3:
                for dst, src in ((w_cat, a["w_cat"].rearrange("(c p) n -> p c n", p=P)),
                                 (w_out, a["w_out"].rearrange("(c p) n -> p c n", p=P)),
                                 (dt_bias, a["dt_bias"].broadcast_to([P, NH])), (a_exp, a["a_log"].broadcast_to([P, NH])),
                                 (rms_w, a["rms_w"].broadcast_to([P, DH])), (dconst, a["dconst"])):
                    sp.dma_start(dst, src).then_inc(d_w3, 16)
                sp.wait_ge(attn_add, NT)
            if stop == 4:
                for dst, src in ((rw, a["router_w"].rearrange("(c p) n -> p c n", p=P)), (rb, a["router_b"].broadcast_to([P, NE])),
                                 (tri, a["tri"]), (em8, a["em8"].broadcast_to([P, NE])), (thr, a["thr"].broadcast_to([P, NE])),
                                 (tile_no, a["tile_no"].broadcast_to([P, NET]))):
                    sp.dma_start(dst, src).then_inc(d_rt, 16)
                sp.wait_ge(pos_ok, 1)
                sp.wait_ge(d_disp, 16 * NT)

                def load(t, slot, first):
                    if not first:
                        sp.wait_ge(e2_mm, t - 1)
                    e = sp.value_load(te_i[0:1, ds(t, 1)], min_val=0, max_val=NE - 1)
                    sp.dma_start(xs[:, slot], xs_dram.rearrange("(t r p) n -> p t r n", p=P, r=2)[:, ds(t, 1)].rearrange("p o r n -> p (o r) n")
                                 ).then_inc(d_ew[slot], 16)
                    sp.dma_start(ew1[:, slot], a["ew1"].rearrange("e (c p) n -> p e c n", p=P)[:, ds(e, 1)].rearrange("p o c n -> p (o c) n")
                                 ).then_inc(d_ew[slot], 16)
                    sp.dma_start(ew2[:, slot], a["ew2"].rearrange("e (c p) n -> p e c n", p=P)[:, ds(e, 1)].rearrange("p o c n -> p (o c) n")
                                 ).then_inc(d_ew[slot], 16)

                expert_tiles(sp, load)
                for b in range(B):
                    sp.wait_ge(fin, 4 * b + 4)
                    sp.dma_start(out.rearrange("(b f p u) c -> p b f u c", b=B, f=2, u=2)[:, b],
                                 h_res[:, 4 * b:4 * b + 4, :].rearrange("p (f u) c -> p f u c", u=2)).then_inc(d_out, 16)
            sp.wait_ge(d_out, 16 * B if stop == 4 else 16)

        @block.gpsimd
        def _(pool):
            pool.memset(ident[:, :], 0.0).then_inc(pool_step, 1)
            pool.memset(minus_half[:, :], -0.5).then_inc(consts, 1)
            pool.wait_ge(pool_step, 1)
            pool.affine_select(out=ident[:, :], in_=ident[:, :], compare_op=ALU.not_equal, fill=1.0, base=0,
                               pattern=[[-1, P]], channel_multiplier=1).then_inc(ident_ok, 1)
            pool.wait_ge(ident_ok, 1)
            pool.memset(sel[NPART:P], 0.0).then_inc(pool_step, 1)
            for i, base in enumerate((0, -NH)):
                pool.wait_ge(pool_step, 2 + i)
                pool.affine_select(out=sel[NPART:P], in_=sel[NPART:P], compare_op=ALU.not_equal, fill=-1.0, base=base,
                                   pattern=[[-1, NH]], channel_multiplier=1).then_inc(pool_step, 1)
            pool.wait_ge(pool_step, 4)
            pool.tensor_copy(kstk[NPART:P], sel[NPART:P].unsqueeze(2).broadcast_to([P - NPART, NH, NK])).then_inc(sel_ok, 1)

            def rstd_of(stage, j):
                pool.wait_ge(ln_var, stage * NT + j + 1)
                pool.tensor_tensor(rstd[:, j:j + 1], var_eps[:, j:j + 1], minus_half[:, 0:1], ALU.pow).then_inc(ln_rstd, 1)

            pool.wait_ge(consts, 1)
            pool.wait_ge(sel_ok, 1)
            for j in range(NT):
                rstd_of(0, j)
            pool.wait_ge(mm_tok, NT)
            pool.memset(spread, 0.0).then_inc(pool_step, 1)
            pool.memset(gather, 0.0).then_inc(pool_step, 1)
            pool.wait_ge(pool_step, 6)
            pool.affine_select(out=spread.rearrange("p (c d) -> p c d", c=4), in_=spread.rearrange("p (c d) -> p c d", c=4),
                               compare_op=ALU.not_equal, fill=1.0, base=-DH, pattern=[[-32, 4], [0, 32]],
                               channel_multiplier=1).then_inc(pool_step, 1)
            for i in range(2):
                pool.wait_ge(pool_step, 7 + i)
                g = gather[:, i, 64 * i:64 * i + 64].rearrange("p (c d) -> p c d", c=4)
                pool.affine_select(out=g, in_=g, compare_op=ALU.not_equal, fill=1.0, base=0, pattern=[[-32, 4], [-1, DH]],
                                   channel_multiplier=1).then_inc(pool_step, 1)
            pool.wait_ge(pool_step, 9)
            pool.memset(ones[:, :], 1.0).then_inc(consts, 4)

            psteps = [9]

            def pstep(ins):
                psteps[0] += 1
                ins.then_inc(pool_step, 1)
                pool.wait_ge(pool_step, psteps[0])

            pool.wait_ge(d_w, 64)
            for i, w in enumerate((w1, w2)):
                w = w.rearrange("p c n -> p (c n)")
                pstep(pool.tensor_scalar(w_sign, w, 0.0, None, ALU.is_gt))
                pool.wait_ge(mean_mm, i + 1)
                pstep(pool.tensor_scalar(w_abs, w, 0.0, None, ALU.is_lt))
                pstep(pool.tensor_tensor(w_sign, w_sign, w_abs, ALU.subtract))
                pool.wait_ge(mean_ok, i + 1)
                pstep(pool.tensor_tensor(w_sign, w_sign, w_mean, ALU.mult))
                pstep(pool.tensor_tensor(w_sign, w_sign, w, ALU.subtract))
                pool.tensor_tensor(w, w, w_sign, ALU.add).then_inc(w_ok, 1)
                pool.wait_ge(w_ok, i + 1)
            if stop >= 2:
                for j in range(NT):
                    rstd_of(1, j)
            if stop >= 4:
                pool.memset(zero_row, 0.0).then_inc(zero_ok, 1)
                pool.wait_ge(zero_ok, 1)
                pool.dma_start(xs_dram.rearrange("(t p) n -> p t n", p=P), zero_row.unsqueeze(1).broadcast_to([P, 2 * NET, D])
                               ).then_inc(d_zero, 16)
            if stop >= 3:
                for j in range(NT):
                    rstd_of(2, j)
                pool.wait_ge(d_w3, 96)
                pool.wait_ge(c_out, NT)
                g = gate.rearrange("p j (h d) -> p (j h) d", d=DH)
                pool.tensor_tensor(g, g, rms_w.unsqueeze(1).broadcast_to([P, NT * NH, DH]), ALU.mult).then_inc(gate_ok, 1)

                def heads(v):
                    return v.rearrange("p t (h d) -> p (t h) d", d=DH)

                def by_head(v):
                    return v.unsqueeze(2).broadcast_to([P, NT * NH, DH])

                pool.wait_ge(alpha_ok, 1)
                pool.wait_ge(gate_ok, 1)
                pool.tensor_tensor(heads(v_tok), heads(v_tok), by_head(small[5].rearrange("p t h -> p (t h)")), ALU.mult).then_inc(vb_ok, 1)
                pool.wait_ge(vb_ok, 1)
                pool.wait_ge(gt_mm, NT)
                pool.wait_ge(gd_ok, 1)
                pool.tensor_tensor(heads(kq_tok[:, 1]), heads(kq_tok[:, 1]), by_head(gd[:, 0]), ALU.mult).then_inc(qg_ok, 1)
                pool.wait_ge(qg_ok, 1)
                pool.wait_ge(gk_ok, 1)
                pstep(pool.tensor_tensor(heads(k_even), heads(k_even), by_head(gd[:, 1]), ALU.mult))
                pool.wait_ge(uw_mm, NT)
                pstep(pool.tensor_scalar(k_odd, k_even, half_mask[:, 1:2], None, ALU.mult))
                pool.tensor_scalar(k_even, k_even, half_mask[:, 0:1], None, ALU.mult).then_inc(kt_ok, 1)
                pool.wait_ge(kt_ok, 1)
                pool.wait_ge(gf_ok, 1)
                for n in range(2 * NT - 1):
                    t, par = divmod(n, 2)
                    for g in range(2):
                        pool.wait_ge(s_ok[g], n + 1)
                        if n or g:
                            pool.wait_ge(sg_ok[1 - g], n + g)
                        for b in (2 * g, 2 * g + 1):
                            f = gf[:, :, t % 8].rearrange("p e (c b a) -> p e c b a", c=2, a=2)[:, :, t // 8, b, par]
                            ins = pool.tensor_tensor(s_dec[:, b], state[:, b], f.unsqueeze(1).unsqueeze(3).broadcast_to([P, 2, 2, DH]), ALU.mult)
                        ins.then_inc(sg_ok[g], 1)
            if stop >= 4:
                for j in range(NT):
                    rstd_of(3, j)
                pool.wait_ge(pos_ok, 1)
                pool.wait_ge(d_zero, 16)
                for j in range(NT):
                    pool.indirect_dma_start(out=xs_dram, out_offset=IndirectOffsetOnAxis(ap=pos_i[:, j:j + 1], axis=0),
                                            in_=xn[:, j, :], in_offset=None).then_inc(d_disp, 16)
                pool.wait_ge(d_ys[0], 16 * ((NET + 1) // 2))
                pool.wait_ge(d_ys[1], 16 * (NET // 2))
                for j in range(NT):
                    pool.indirect_dma_start(out=yg[:, j, :], out_offset=None, in_=ys_dram,
                                            in_offset=IndirectOffsetOnAxis(ap=pos_i[:, j:j + 1], axis=0)).then_inc(d_yg, 16)

        @block.scalar
        def _(act):
            for b in range(B):
                act.dma_start(x_t[b],
                              a["x_t"].rearrange("(c p) n -> p c n", p=P)[:, :, b * S:(b + 1) * S]).then_inc(d_x[b], 16)

            def project_out(u):
                act.wait_ge(pj_mm, u + 1)
                if u >= 2:
                    act.wait_ge(pj_split, u - 1)
                which = 0 if u >= 4 else 1
                act.activation(proj[:, u % 2], ps[:, 4 + u % 2, :], ACT.Relu,
                               bias=bias_qk[:, which, u % 2:u % 2 + 1]).then_inc(pj_out, 1)

            def turn_out(stage, j):
                n = stage * NT + j
                act.wait_ge(tp_mm, n + 1)
                act.copy(xnt[:, :, j * P:(j + 1) * P],
                         ps[:, turn_bank(stage, j), 0:FC * P].rearrange("p (c n) -> p c n", c=FC)).then_inc(tp_out, 1)

            act.wait_ge(d_small, 64)
            for u in range(4):
                project_out(u)
            for b in range(B):
                for j in range(4 * b, 4 * b + 4):
                    turn_out(0, j)
                for m in range(2):
                    project_out(4 + 2 * b + m)

            def unit(n, e):
                for g in range(2):
                    act.wait_ge(st_mm, 2 * n + g + 1)
                    if g == 0 and not (isinstance(n, int) and n < 2):
                        act.wait_ge(av_mm, n - 1)
                    act.activation(prob[:, e, 2 * g:2 * g + 2, :], ps[:, 2 * g:2 * g + 2, :], ACT.Exp,
                                   scale=DH ** -0.5).then_inc(exp_out, 1)

            def quad(b, q, m, parity):
                for e in range(8):
                    unit(8 * m + e, e % 2)
                    if e == 1 and not (isinstance(q, int) and q == 0):
                        quad_out_slot(8 * m, m - 1, 1 - parity)

            def quad_out_slot(n, m, slot):
                act.wait_ge(av_mm, n)
                if not (isinstance(m, int) and m < 2):
                    act.wait_ge(at_mm, m - 1)
                act.copy(att[:, slot], ps[:, 6, :]).then_inc(av_out, 1)

            act.wait_ge(d_w, 64)
            for i, w in enumerate((w1, w2)):
                if i:
                    act.wait_ge(w_ok, i)
                act.activation(w_abs, w.rearrange("p c n -> p (c n)"), ACT.Abs).then_inc(abs_ok, 1)
                act.wait_ge(mean_mm, i + 1)
                if i == 0:
                    act.mul(w_mean.rearrange("p (c a n) -> p c a n", c=FC, a=2)[:, 0], ps[:, 6:8, :], 1.0 / D)
                    act.mul(w_mean.rearrange("p (c a n) -> p c a n", c=FC, a=2)[:, 1], ps[:, 6:8, :], 1.0 / D).then_inc(mean_ok, 1)
                else:
                    for c in range(HC):
                        ins = act.mul(w_mean.rearrange("p (c n) -> p c n", c=HC)[:, c], ps[:, 6, 0:D], 1.0 / HID)
                    ins.then_inc(mean_ok, 1)

            for b in range(B):
                act.wait_ge(mx_mm, b + 1)
                if b:
                    act.wait_ge(d_mrow, 16 * b)
                act.copy(mrow[NPART:P], ps[NPART:P, 7, 0:S // 2].bitcast(BF16)).then_inc(mx_row, 1)
                quad(b, 0, 4 * b, 0)
                quad(b, 1, 4 * b + 1, 1)
                with act.Fori(1, 2) as qp:
                    for e in range(2):
                        quad(b, None, qp * 2 + (4 * b + e), e)
                quad_out_slot(32 * b + 32, 4 * b + 3, 1)

            if stop >= 2:
                for b in range(B):
                    for j in range(4 * b, 4 * b + 4):
                        turn_out(1, j)
                    for m in range(HC):
                        act.wait_ge(f1_mm, b * HC + m + 1)
                        if b >= 2 and m == 0:
                            act.wait_ge(f2_mm, 4 * (b - 1))
                        act.activation(hid[:, b % 2, m, :], ps[:, 4 + m % 2, :], ACT.Gelu, bias=bias_1[:, m:m + 1]).then_inc(f1_out, 1)
            if stop >= 3:
                act.wait_ge(d_w3, 96)
                act.wait_ge(ffn_add, NT)
                for j in range(NT):
                    b, ft, u = j // 4, j % 4 // 2, j % 2
                    act.wait_ge(tp_mm, 2 * NT + j + 1)
                    act.copy(xnt4.rearrange("p c (t b s) -> p c t b s", b=B, s=32)[:, :, 8 * ft:8 * ft + 8, b, u::2],
                             ps[:, turn_bank(2, j), 0:FC * P].rearrange("p (c t s) -> p c t s", c=FC, t=8)).then_inc(tp_out, 1)
                for t in range(NT):
                    act.wait_ge(c_mm, t + 1)
                    s0 = 4 * (t % 2)
                    act.copy(kq_tok[:, :, t, :], ps[:, s0, :].rearrange("p (w n) -> p w n", w=2))
                    act.copy(v_tok[:, t, :], ps[:, s0 + 1, 0:D])
                    act.activation(gate[:, t, :], ps[:, s0 + 1, D:2 * D], ACT.Silu).then_inc(c_out, 1)
                act.wait_ge(ss_ok, NT)
                act.activation(rnorm, ssum, ACT.Sqrt).then_inc(nrm_ok, 1)
                z, u, alpha, be = small[0], small[1], small[2], small[3]
                act.wait_ge(dve_ab, 1)
                act.activation(a_exp, a_exp, ACT.Exp).then_inc(act_ab, 1)
                act.activation(u, z, ACT.Abs).then_inc(act_ab, 1)
                act.wait_ge(act_ab, 2)
                act.activation(u, u, ACT.Exp, scale=-1.0).then_inc(act_ab, 1)
                act.activation(be, ab[:, :, NH:2 * NH], ACT.Exp, scale=-1.0).then_inc(act_ab, 1)
                act.wait_ge(dve_ab, 2)
                act.activation(alpha, alpha, ACT.Exp, scale=-1.0).then_inc(alpha_ok, 1)
                for t in range(NT + 1):
                    if t < NT:
                        act.wait_ge(gt_mm, t + 1)
                        if t >= 2:
                            act.wait_ge(g_mm, t - 1)
                        kk = ps[:, t % 2, 0:2 * P].rearrange("p (a n) -> p a n", a=2)
                        for odd in range(2):
                            act.activation(k_one[:, t % 2, odd], kk, ACT.Copy, scale=half_mask[:, odd:odd + 1])
                        act.copy(kq_f[:, t % 2], ps[:, t % 2, :].rearrange("p (w a n) -> p w a n", w=2, a=2)).then_inc(gt_out, 1)
                    if t:
                        act.wait_ge(pick_dve_ok, t)
                        if t >= 3:
                            act.wait_ge(g_out, t - 2)
                        act.activation(pick_act[:, (t - 1) % 2], half_products(1), ACT.Copy, scale=half_mask[:, 1:2]).then_inc(pick_act_ok, 1)
                act.wait_ge(gd_mm, 1)
                act.copy(gd, ps[:, 7, :].rearrange("p (a n) -> p a n", a=2)).then_inc(gd_ok, 1)
                for n in range(0, 8, 2):
                    take_inverse(act, n)
                for t in range(NT + 1):
                    if t < NT:
                        take_uw(act, t)
                    if t:
                        i = t - 1
                        act.wait_ge(wq_mm, i + 1)
                        for par in range(2):
                            src = ps[:, 4 + i % 2, 0:256].rearrange("p (a b x) -> p a b x", a=2, b=B)[:, :, :, DH * par:DH * par + DH]
                            ins = act.copy(wq_t5[:, i, :, par, :, DH * par:DH * par + DH], src)
                        ins.then_inc(wq_act, 1)
                for t in range(NT):
                    act.wait_ge(xo_ok[0], 2 * t + 1)
                    act.wait_ge(xo_ok[1], 2 * t + 1)
                    if t >= 2:
                        act.wait_ge(comb_ok, t - 1)
                    for w in range(2):
                        ins = act.activation(comb_a[:, t % 2, w], xo[:, 2 * t % 4, :], ACT.Copy, scale=half_mask[:, w:w + 1])
                    ins.then_inc(cb_act, 1)
                for t in range(NT):
                    act.wait_ge(o_mm, t + 1)
                    act.copy(o_tok[:, t, :], ps[:, t % 4, 0:D]).then_inc(o_out, 1)
                act.wait_ge(rms_ss, 1)
                act.activation(small[0], small[0], ACT.Sqrt).then_inc(rms_rt, 1)
                for t in range(NT):
                    act.wait_ge(og_mm, t + 1)
                    act.copy(o_f[:, :, :, 32 * t:32 * t + 32],
                             ps[:, 6 + t % 2, 0:FC * P].rearrange("p (c b s) -> p c b s", c=FC, b=B)).then_inc(og_out, 1)
            if stop >= 4:
                for j in range(NT):
                    turn_out(3, j)
                act.wait_ge(sh_ok, 1)
                act.activation(lexp, lexp, ACT.Exp).then_inc(lexp_ok, 1)

                def expert(t, slot, first):
                    act.wait_ge(et_mm, t + 1)
                    if not first:
                        act.wait_ge(e1_mm, (t - 1) * HC)
                    act.copy(xst[:, slot], ps[:, 6, :].rearrange("p (c n) -> p c n", c=FC)).then_inc(et_out, 1)
                    for m in range(HC):
                        act.wait_ge(e1_mm, t * HC + m + 1)
                        if not (first and t == 0 and m < 2):
                            act.wait_ge(e1_out, t * HC + m - 1)
                        act.activation(silu[:, m % 2], ps[:, m % 4, 0:ET], ACT.Silu).then_inc(e_silu, 1)
                    act.wait_ge(e2_out, t + 1)
                    act.dma_start(ys_dram.rearrange("(t r p) n -> p t r n", p=P, r=2)[:, ds(t, 1)].rearrange("p o r n -> p (o r) n"),
                                  ys[:, slot]).then_inc(d_ys[slot], 16)

                expert_tiles(act, expert)

        @block.tensor
        def _(pe):
            pe.wait_ge(d_kv, 80)
            for u in range(4):
                kh, m = divmod(u, 2)
                if u >= 2:
                    pe.wait_ge(pj_out, u - 1)
                for c in range(FC):
                    mm = pe.matmul(ps[:, 4 + u % 2, :], wk_t[:, c, m * P:(m + 1) * P], keys_t[:, c, kh * S:(kh + 1) * S],
                                   start=(c == 0), stop=(c == FC - 1))
                mm.then_inc(pj_mm, 1)
            for kc in range(KC):
                if kc >= 2:
                    pe.wait_ge(v_out, kc - 1)
                for c in range(FC):
                    mm = pe.matmul(ps[:, 6 + kc % 2, 0:D], vals_t[:, c, kc * P:(kc + 1) * P], wv_t[:, c, :],
                                   start=(c == 0), stop=(c == FC - 1))
                mm.then_inc(v_mm, 1)

            def turn(stage, j):
                n = stage * NT + j
                pe.wait_ge(ln_out, n + 1)
                if n >= 2:
                    pe.wait_ge(tp_out, n - 1)
                for c in range(FC):
                    mm = pe.transpose(ps[:, turn_bank(stage, j), c * P:(c + 1) * P], xn[:, j, c * P:(c + 1) * P], ident[:, :])
                mm.then_inc(tp_mm, 1)

            pe.wait_ge(ident_ok, 1)
            for b in range(B + 1):
                if b < B:
                    pe.wait_ge(d_x[b], 16)
                    for j in range(4 * b, 4 * b + 4):
                        if j >= 2:
                            pe.wait_ge(tok_out, j - 1)
                        for c in range(8):
                            if b == 0 and j == 0:
                                pe.wait_ge(wtok_ok, c + 1)
                            mm = pe.matmul(ps[:, j % 2, 0:D], x_t[b][:, c, (j % 4) * P:(j % 4 + 1) * P], w_tok[:, c, :],
                                           start=(c == 0), stop=(c == 7))
                        mm.then_inc(mm_tok, 1)
                if b >= 1:
                    for j in range(4 * b - 4, 4 * b):
                        turn(0, j)
                    pe.wait_ge(tp_out, 4 * b)
                    for m in range(2):
                        u = 4 + 2 * (b - 1) + m
                        pe.wait_ge(pj_out, u - 1)
                        for c in range(FC):
                            mm = pe.matmul(ps[:, 4 + u % 2, :], wq_t[:, c, m * P:(m + 1) * P],
                                           xnt[:, c, (b - 1) * S:b * S], start=(c == 0), stop=(c == FC - 1))
                        mm.then_inc(pj_mm, 1)

            def unit(q, kc, n, slot, nmax, mslot):
                for g in range(2):
                    if n is not None:
                        if n:
                            pe.wait_ge(exp_out, 2 * n + g - 1)
                        for i in range(2):
                            h = 4 * q + 2 * g + i
                            mm = pe.matmul(ps[:, 2 * g + i, :], kstk[:, h, kc * P:(kc + 1) * P], qstk[:, slot, h, :],
                                           start=True, stop=True)
                        mm.then_inc(st_mm, 1)
                    if nmax is not None:
                        h, part_of = divmod(8 * q + kc, 2)
                        qt = 2 * part_of + g
                        for half in range(2):
                            if nmax or g:
                                pe.wait_ge(max_out, 4 * nmax + 2 * g + half - 1)
                            pe.matmul(ps[:, 4 + half, :], qstk[0:NPART, mslot, h, qt * P:(qt + 1) * P],
                                      kstk[0:NPART, h, half * S:(half + 1) * S], start=True, stop=True).then_inc(sm_mm, 1)

            def attend(n):
                m, kc = divmod(n, KC)
                pe.wait_ge(exp_out, 2 * n + 2)
                if kc == 0 and m:
                    pe.wait_ge(av_out, m)
                for c in range(4):
                    mm = pe.matmul(ps[32 * c:32 * c + 32, 6, :], vaug[:, kc, 4 * (m % 4) + c, :], prob[:, n % 2, c, :],
                                   start=(kc == 0), stop=(kc == KC - 1), skip_group_check=True)
                mm.then_inc(av_mm, 1)

            def spread_sums(m):
                pe.wait_ge(av_out, m + 1)
                if m >= 2 and m % 2 == 0:
                    pe.wait_ge(at_add, m // 2)
                if m % 4 == 0:
                    pe.wait_ge(mx_row, m // 4 + 1)
                if m % 2:
                    pe.wait_ge(rd_ok, m)
                pe.matmul(ps[:, 7, :], spread, att[:, m % 2], start=True, stop=True).then_inc(sum_mm, 1)

            def compact(m):
                pe.wait_ge(att_ok, m + 1)
                for i in range(2):
                    mm = pe.matmul(ps[:, 7, :], gather[:, i], att[:, i], start=(i == 0), stop=(i == 1))
                mm.then_inc(at_mm, 2)

            pe.wait_ge(consts, 5)
            for i in range(2):
                pe.wait_ge(abs_ok, i + 1)
                if i:
                    pe.wait_ge(mean_ok, i)
                if i == 0:
                    for half in range(2):
                        for c in range(FC):
                            mm = pe.matmul(ps[:, 6 + half, :], ones[:, :], w_abs[:, c * HID + half * S:c * HID + (half + 1) * S],
                                           start=(c == 0), stop=(c == FC - 1))
                else:
                    for c in range(HC):
                        mm = pe.matmul(ps[:, 6, 0:D], ones[:, :], w_abs[:, c * D:(c + 1) * D], start=(c == 0), stop=(c == HC - 1))
                mm.then_inc(mean_mm, 1)
            pe.wait_ge(mean_ok, 2)
            pe.wait_ge(d_kstk, 96)
            pe.wait_ge(sel_ok, 1)
            pe.wait_ge(v_out, KC)
            pe.wait_ge(pj_out, NU)
            for b in range(-1, B):
                if b + 1 < B:
                    pe.wait_ge(d_qstk[b + 1], 96)
                if b >= 0:
                    pe.wait_ge(d_mrow, 16 * (b + 1))
                for q in range(4):
                    for kc in range(KC):
                        n = 32 * b + 8 * q + kc
                        unit(q, kc, n if b >= 0 else None, b % 2, n + 32 if b + 1 < B else None, (b + 1) % 2)
                        if b >= 0 and n > 32 * b:
                            attend(n - 1)
                        if b >= 0 and kc == 3 and q:
                            spread_sums(4 * b + q - 1)
                        if b >= 0 and kc == 6 and q == 2:
                            compact(4 * b + 1)
                if b >= 0:
                    attend(32 * b + 31)
                    spread_sums(4 * b + 3)
                    compact(4 * b + 3)
                if b + 1 < B:
                    pe.wait_ge(mx_pad, b + 2)
                    if b >= 0:
                        pe.wait_ge(at_add, 2 * b + 2)
                    for qt in range(QT):
                        mm = pe.transpose(ps[:, 7, qt * (P // 2):(qt + 1) * (P // 2)].bitcast(BF16), mpad[:, qt, :], ident_b[:, :])
                    mm.then_inc(mx_mm, 1)

            if stop >= 2:
                pe.wait_ge(w_ok, 2)
                pe.wait_ge(at_add, 2 * B)
                pe.wait_ge(exp_out, 256)

                def hidden(b):
                    for m in range(HC):
                        n = b * HC + m
                        if n >= 2:
                            pe.wait_ge(f1_out, n - 1)
                        for c in range(FC):
                            mm = pe.matmul(ps[:, 4 + m % 2, :], w1[:, c, m * P:(m + 1) * P], xnt[:, c, b * S:(b + 1) * S],
                                           start=(c == 0), stop=(c == FC - 1))
                        mm.then_inc(f1_mm, 1)

                def ffn_out(b):
                    pe.wait_ge(f1_out, HC * (b + 1))
                    for i in range(4):
                        j = 4 * b + i
                        if j >= 2:
                            pe.wait_ge(f2_out, j - 1)
                        for m in range(HC):
                            mm = pe.matmul(ps[:, 6 + j % 2, 0:D], hid[:, b % 2, m, i * P:(i + 1) * P], w2[:, m, :],
                                           start=(m == 0), stop=(m == HC - 1))
                        mm.then_inc(f2_mm, 1)

                for b in range(B + 1):
                    if b < B:
                        for j in range(4 * b, 4 * b + 4):
                            turn(1, j)
                        pe.wait_ge(tp_out, NT + 4 * b + 4)
                        hidden(b)
                    if b:
                        ffn_out(b - 1)
            if stop >= 3:
                pe.wait_ge(d_w3, 96)
                pe.wait_ge(f2_out, NT)
                for j in range(NT):
                    turn(2, j)
                pe.wait_ge(tp_out, 3 * NT)
                for t in range(NT):
                    if t >= 2:
                        pe.wait_ge(c_out, t - 1)
                        pe.wait_ge(c_ab, t - 1)
                    s0 = 4 * (t % 2)
                    for i, (lo, n) in enumerate(((0, 512), (512, 512), (1024, 2 * NH))):
                        for c in range(FC):
                            mm = pe.matmul(ps[:, s0 + i, 0:n], xnt4[:, c, t * P:(t + 1) * P], w_cat[:, c, lo:lo + n],
                                           start=(c == 0), stop=(c == FC - 1))
                    mm.then_inc(c_mm, 1)
                pe.wait_ge(c_out, NT)
                pe.wait_ge(c_ab, NT)
                for t in range(NT + 1):
                    if t < NT:
                        pe.wait_ge(kq_ok, t + 1)
                        if t >= 2:
                            pe.wait_ge(gt_out, t - 1)
                        for w in range(2):
                            for hh in range(2):
                                mm = pe.transpose(ps[:, t % 2, (2 * w + hh) * P:(2 * w + hh + 1) * P],
                                                  kq_tok[:, w, t, hh * P:(hh + 1) * P], ident[:, :])
                        mm.then_inc(gt_mm, 1)
                    if t:
                        i = t - 1
                        pe.wait_ge(gt_out, i + 1)
                        if i:
                            pe.wait_ge(pick_act_ok, i)
                        for h in range(NH):
                            hh, r, odd = h // 8, 32 * (h % 8 // 2), h % 2
                            at = 128 * hh + 64 * odd
                            for b in range(B):
                                mm = pe.matmul(ps[32 * b:32 * b + 32, 2 + r // 32, at:at + 64],
                                               k_one[r:r + 32, i % 2, odd, hh, 32 * b:32 * b + 32],
                                               kq_f[r:r + 32, i % 2, :, hh, 32 * b:32 * b + 32], start=True, stop=True,
                                               skip_group_check=True)
                        mm.then_inc(g_mm, 1)
                pe.wait_ge(alpha_ok, 1)
                for i, (v, half) in enumerate(((2, 0), (2, 1), (5, 0), (5, 1))):
                    mm = pe.transpose(ps[:, 6, i * P:(i + 1) * P], small[v][:, 8 * half:8 * half + 8, :].rearrange("p t h -> p (t h)"), ident[:, :])
                mm.then_inc(su_mm, 1)
                pe.wait_ge(du_ok, 1)
                for half in range(2):
                    pe.transpose(ps[:, 7, half * P:(half + 1) * P], gam_u[:, 8 * half:8 * half + 8, :].rearrange("p u i -> p (u i)"), ident[:, :])
                    mm = pe.transpose(ps[:, 7, (2 + half) * P:(3 + half) * P], decay[:, DH - 1, 8 * half:8 * half + 8, :].rearrange("p u i -> p (u i)"), ident[:, :])
                mm.then_inc(gd_mm, 1)

                def turn_rows(src, n, bank):
                    half, ig = divmod(n, 4)
                    for i in range(4):
                        mm = pe.transpose(ps[:, bank, i * P:(i + 1) * P], src[:, 128 * half:128 * half + 128, 4 * ig + i], ident[:, :])
                    return mm

                for n in range(8):
                    if n >= 2:
                        pe.wait_ge(dt_out, n - 1)
                    turn_rows(decay.rearrange("p i u j -> p (u j) i"), n, n % 2).then_inc(dt_mm, 1)
                pe.wait_ge(g_out, NT)
                for n in range(8):
                    if n >= 2:
                        pe.wait_ge(gu_out, n - 1)
                    turn_rows(gp[:, :, :, 0].rearrange("p t h i -> p (t h) i"), n, 2 + n % 2).then_inc(gu_mm, 1)
                pe.wait_ge(gk_ok, 1)
                for n in range(8):
                    if n >= 2:
                        pe.wait_ge(tt_out[n % 2], n // 2)
                    turn_rows(t_u.rearrange("p i u j -> p (u j) i"), n, 4 + n % 2).then_inc(tt_mm, 1)
                pe.wait_ge(gm_ok, 1)
                pe.wait_ge(gd_ok, 1)
                for hh in range(2):
                    mm = pe.matmul(ps[:, 6, hh * P:(hh + 1) * P], head_sel[:, hh, :], gam_m.rearrange("p c u -> p (c u)"), start=True, stop=True)
                mm.then_inc(gf_mm, 1)
                pe.wait_ge(tt_out[0], 4)
                pe.wait_ge(tt_out[1], 4)
                pe.wait_ge(gf_ok, 1)
                pe.wait_ge(vb_ok, 1)
                pe.wait_ge(qg_ok, 1)
                for t in range(NT + 1):
                    if t < NT:
                        if t >= 2:
                            pe.wait_ge(uw_out[0], t - 1)
                            pe.wait_ge(uw_out[1], t - 1)
                        for h in range(NH):
                            for b in range(B):
                                mm = pe.matmul(ps[32 * b:32 * b + 32, 2 * (t % 2) + h // 8, 32 * (h % 8):32 * (h % 8) + 32],
                                               t_blk[32 * b:32 * b + 32, NH * t + h].rearrange("p a i -> p (a i)"),
                                               vgk[32 * b:32 * b + 32, :, D * t + DH * h:D * t + DH * h + DH], start=True, stop=True,
                                               skip_group_check=True)
                        mm.then_inc(uw_mm, 1)
                    if t:
                        i = t - 1
                        pe.wait_ge(uw_out[0], i + 1)
                        pe.wait_ge(uw_out[1], i + 1)
                        if i >= 2:
                            pe.wait_ge(wq_act, i - 1)
                            pe.wait_ge(wq_dve, i - 1)
                        for hh in range(2):
                            pe.transpose(ps[:, 4 + i % 2, hh * P:(hh + 1) * P], w_neg[:, i % 2, hh * P:(hh + 1) * P], ident[:, :])
                            mm = pe.transpose(ps[:, 6 + i % 2, hh * P:(hh + 1) * P], kq_tok[:, 1, i, hh * P:(hh + 1) * P], ident[:, :])
                        mm.then_inc(wq_mm, 1)
                pe.wait_ge(wq_act, NT)
                pe.wait_ge(wq_dve, NT)
                pe.wait_ge(kt_ok, 1)

                def halves(v):
                    return v.rearrange("p (a e x) -> p a e x", a=2, e=2)

                for n in range(2 * NT):
                    t, par = divmod(n, 2)
                    for g in range(2):
                        pe.wait_ge(s_ok[g], n + 1)
                        for r in range(4):
                            for hh in range(2):
                                for b in (2 * g, 2 * g + 1):
                                    mm = pe.matmul(ps[32 * b:32 * b + 32, r, 32 * hh:32 * hh + 32],
                                                   wq_t5[32 * r:32 * r + 32, t, hh, par, b, :], state[32 * r:32 * r + 32, b, :, hh, :],
                                                   start=True, stop=True, skip_group_check=True)
                        mm.then_inc(r_mm[g], 1)
                    for g in range(2) if n < 2 * NT - 1 else ():
                        pe.wait_ge(xo_ok[g], n + 1)
                        for r in range(4):
                            for hh in range(2):
                                for b in (2 * g, 2 * g + 1):
                                    f, x = P * hh + 32 * r, 64 * r + 32 * hh
                                    mm = pe.matmul(halves(ps[32 * r:32 * r + 32, 4 + b, 0:64])[:, :, hh, :],
                                                   (k_even, k_odd)[par][32 * b:32 * b + 32, t, f:f + 32],
                                                   xo[32 * b:32 * b + 32, n % 4, x:x + 32].rearrange("p (a x) -> p a x", a=2),
                                                   start=True, stop=True, skip_group_check=True)
                        mm.then_inc(s_mm[g], 1)
                pe.wait_ge(xo_ok[0], 2 * NT)
                pe.wait_ge(xo_ok[1], 2 * NT)
                for t in range(NT):
                    pe.wait_ge(comb_ok, t + 1)
                    if t >= 4:
                        pe.wait_ge(o_out, t - 3)
                    for b in range(B):
                        r = slice(32 * b, 32 * b + 32)
                        pe.matmul(ps[r, t % 4, 0:D], swap[r, r], comb_qs[r, t, :].rearrange("p (r e x) -> p e r x", r=4, e=2),
                                  start=True, stop=False, skip_group_check=True)
                    for h in range(NH):
                        x = 64 * (h % 8 // 2) + 32 * (h // 8) + DH * (h % 2)
                        for b in range(B):
                            r = slice(32 * b, 32 * b + 32)
                            mm = pe.matmul(ps[r, t % 4, DH * h:DH * h + DH], p_blk[r, NH * t + h].rearrange("p a i -> p (a i)"),
                                           u_tok[r, t, x:x + DH], start=False, stop=True, skip_group_check=True)
                    mm.then_inc(o_mm, 1)
                for t in range(NT):
                    pe.wait_ge(og_ok, t + 1)
                    if t >= 2:
                        pe.wait_ge(og_out, t - 1)
                    for c in range(FC):
                        mm = pe.transpose(ps[:, 6 + t % 2, c * P:(c + 1) * P], o_tok[:, t, c * P:(c + 1) * P], ident[:, :])
                    mm.then_inc(og_mm, 1)
                    for n in range(8 * (t // 8), 8 * (t // 8) + 8) if t % 8 == 7 else ():
                        if n % 8 == 0:
                            pe.wait_ge(og_out, t + 1)
                        j = out_tile(n)
                        b, ft, u = j // 4, j % 4 // 2, j % 2
                        if n >= 2:
                            pe.wait_ge(attn_add, n - 1)
                        for c in range(FC):
                            mm = pe.matmul(ps[:, 2 + n % 2, 0:D], o_f[:, c, b, D * ft + u:D * ft + D:2], w_out[:, c, :],
                                           start=(c == 0), stop=(c == FC - 1))
                        mm.then_inc(wo_mm, 1)
            if stop >= 4:
                pe.wait_ge(d_rt, 96)
                for j in range(NT):
                    if j == 0:
                        pe.wait_ge(attn_add, NT)
                    turn(3, j)
                    pe.wait_ge(tp_out, 3 * NT + j + 1)
                    for c in range(FC):
                        mm = pe.matmul(ps[:, 0, j * NE:(j + 1) * NE], xnt[:, c, j * P:(j + 1) * P], rw[:, c, :],
                                       start=(c == 0), stop=(c == FC - 1))
                mm.then_inc(lg_mm, 1)
                pe.wait_ge(hot_ok, 1)
                hot = onehot.rearrange("p j e -> p (j e)")
                pe.matmul(ps[:, 1, 0:NT * NE], tri, hot, start=True, stop=True)
                pe.matmul(ps[:, 2, 0:NT * NE], ones[:, :], hot, start=True, stop=True).then_inc(cnt_mm, 1)
                pe.wait_ge(pos_ok, 1)

                def turn_tokens(t, slot, first):
                    pe.wait_ge(d_ew[slot], (t // 2 + 1) * 48 if isinstance(t, int) else t * 24 + (48 if slot == 0 else 24))
                    if not (first and t == 0):
                        pe.wait_ge(et_out, t)
                    for c in range(FC):
                        for r in range(2):
                            mm = pe.transpose(ps[:, 6, c * ET + r * P:c * ET + (r + 1) * P], xs[:, slot, r, c * P:(c + 1) * P], ident[:, :])
                    mm.then_inc(et_mm, 1)

                def expert(t, slot, first):
                    pe.wait_ge(et_out, t + 1)
                    for m in range(HC):
                        if not (first and t == 0 and m < 4):
                            pe.wait_ge(e1_out, t * HC + m - 3)
                        for half in range(2):
                            for c in range(FC):
                                mm = pe.matmul(ps[:, m % 4, half * ET:(half + 1) * ET],
                                               ew1[:, slot, c, half * HID + m * P:half * HID + (m + 1) * P], xst[:, slot, c, :],
                                               start=(c == 0), stop=(c == FC - 1))
                        mm.then_inc(e1_mm, 1)
                    if not (isinstance(t, int) and t == NET - 1):
                        turn_tokens(t + 1, 1 - slot, first)
                    pe.wait_ge(e1_out, t * HC + HC)
                    if not (first and t == 0):
                        pe.wait_ge(e2_out, t)
                    for r in range(2):
                        for m in range(HC):
                            mm = pe.matmul(ps[:, 4 + r, 0:D], eu[:, slot, m, r * P:(r + 1) * P], ew2[:, slot, m, :],
                                           start=(m == 0), stop=(m == HC - 1))
                    mm.then_inc(e2_mm, 1)

                turn_tokens(0, 0, True)
                expert_tiles(pe, expert)

        @block.vector
        def _(dve):
            steps = [0]

            def step(ins):
                steps[0] += 1
                ins.then_inc(dve_step, 1)
                dve.wait_ge(dve_step, steps[0])

            dve.wait_ge(ident_ok, 1)
            dve.tensor_copy(ident_b[:, :], ident[:, :])
            dve.wait_ge(d_small, 64)
            for c in range(8):
                d, ic = divmod(c, FC)
                dve.tensor_tensor(w_tok[:, c, :], ws_t[:, ic, :], w_bc[:, d, :], ALU.mult).then_inc(wtok_ok, 1)
            step(dve.memset(vaug[:, :, :, DH:32], 0.0))
            dve.memset(vaug[:, :, :, DH:DH + 1], 1.0)

            def split(u):
                dve.wait_ge(pj_out, u + 1)
                if u >= 2:
                    dve.wait_ge(d_part[u % 2], 16 * (u // 2))
                f = proj[:, u % 2]
                step(dve.tensor_copy(part[:, u % 2, 0], f))
                step(dve.tensor_tensor(f, f, part[:, u % 2, 0], ALU.subtract))
                step(dve.tensor_copy(part[:, u % 2, 1], f))
                step(dve.tensor_tensor(f, f, part[:, u % 2, 1], ALU.subtract))
                dve.tensor_copy(part[:, u % 2, 2], f).then_inc(pj_split, 1)

            for u in range(4):
                split(u)
            for kc in range(KC):
                dve.wait_ge(v_mm, kc + 1)
                dve.tensor_tensor(vtmp[:, kc % 2], ps[:, 6 + kc % 2, 0:D], bias_v, ALU.add).then_inc(v_out, 1)
                dve.wait_ge(v_out, kc + 1)
                dve.tensor_scalar(vaug[:, kc, :, 0:DH], vtmp[:, kc % 2].rearrange("p (h d) -> p h d", h=NH), 0.0, None,
                                  ALU.max)

            def ln_stats(j):
                step(dve.bn_stats(bn[:, j % 2, :], h_res[:, j, :]))
                step(dve.bn_aggr(mv[:, j, :], bn[:, j % 2, :]))
                dve.tensor_scalar(var_eps[:, j:j + 1], mv[:, j, 1:2], LN_EPS, None, ALU.add).then_inc(ln_var, 1)

            def ln_apply(stage, j):
                dve.wait_ge(ln_rstd, stage * NT + j + 1)
                dve.tensor_scalar(xn[:, j, :], h_res[:, j, :], mv[:, j, 0:1], rstd[:, j:j + 1], ALU.subtract,
                                  ALU.mult).then_inc(ln_out, 1)

            for b in range(B + 1):
                if b < B:
                    for j in range(4 * b, 4 * b + 4):
                        dve.wait_ge(mm_tok, j + 1)
                        dve.tensor_copy(h_res[:, j, :], ps[:, j % 2, 0:D]).then_inc(tok_out, 1)
                        dve.wait_ge(tok_out, j + 1)
                        ln_stats(j)
                        if j >= 1:
                            ln_apply(0, j - 1)
                else:
                    ln_apply(0, NT - 1)
                if b >= 2:
                    for m in range(2):
                        split(4 + 2 * (b - 2) + m)
            for m in range(2):
                split(4 + 2 * (B - 1) + m)
            dve.wait_ge(mm_tok, NT)
            dve.wait_ge(ln_out, NT)
            step(dve.tensor_tensor(h_res[:, :, :], h_res[:, :, :], xn[:, :, :], ALU.add))
            step(dve.memset(mpad, 0.0))

            def maxima(h, nmax):
                for qt in range(QT):
                    for half in range(2):
                        dve.wait_ge(sm_mm, 8 * nmax + 2 * qt + half + 1)
                        dve.tensor_reduce(mx[:, half, qt, ds(h, 1)], ps[:, 4 + half, :], AX.X, ALU.max).then_inc(max_out, 1)

            def normalise(m, slot):
                dve.wait_ge(sum_mm, m + 1)
                if m:
                    dve.wait_ge(att_ok, m)
                dve.reciprocal(rden, ps[:, 7, :]).then_inc(rd_ok, 1)
                dve.wait_ge(rd_ok, m + 1)
                dve.tensor_tensor(att[:, slot], att[:, slot], rden, ALU.mult).then_inc(att_ok, 1)

            def add_attention(b, c):
                dve.wait_ge(at_mm, 4 * b + 2 * c + 2)
                row = h_res[:, 4 * b + 2 * c:4 * b + 2 * c + 2, :].rearrange("p f (s u) -> p f u s", u=2)
                dve.tensor_tensor(row, ps[:, 7, :].rearrange("p (f u s) -> p f u s", f=2, u=2), row, ALU.add
                                  ).then_inc(at_add, 1)

            dve.wait_ge(consts, 5)
            for b in range(-1, B):
                for q in range(4):
                    for i in range(4):
                        if b + 1 < B:
                            maxima(4 * q + i, (b + 1) * NH + 4 * q + i)
                        if b >= 0 and q and i == 2:
                            normalise(4 * b + q - 1, (q - 1) % 2)
                        if b >= 0 and q == 2 and i == 3:
                            add_attention(b, 0)
                if b >= 0:
                    normalise(4 * b + 3, 1)
                    add_attention(b, 1)
                if b + 1 < B:
                    dve.wait_ge(max_out, 8 * NH * (b + 2))
                    step(dve.tensor_tensor(mx1, mx[:, 0], mx[:, 1], ALU.max))
                    if b >= 0:
                        dve.wait_ge(mx_mm, b + 1)
                    step(dve.tensor_copy(mpad[:, :, NPART:NPART + NH], mx1))
                    step(dve.tensor_tensor(mlo, mx1, mpad[:, :, NPART:NPART + NH], ALU.subtract))
                    dve.tensor_copy(mpad[:, :, NPART + NH:P], mlo).then_inc(mx_pad, 1)

            if stop >= 2:
                for j in range(NT + 1):
                    if j < NT:
                        if j == 0:
                            dve.wait_ge(at_add, 2 * B)
                        ln_stats(j)
                    if j:
                        ln_apply(1, j - 1)
                for j in range(NT):
                    dve.wait_ge(f2_mm, j + 1)
                    if j >= 2:
                        dve.wait_ge(ffn_add, j - 1)
                    dve.tensor_tensor(ffn_sum[:, j % 2], ps[:, 6 + j % 2, 0:D], bias_2, ALU.add).then_inc(f2_out, 1)
                    dve.wait_ge(f2_out, j + 1)
                    dve.tensor_tensor(h_res[:, j, :], h_res[:, j, :], ffn_sum[:, j % 2], ALU.add).then_inc(ffn_add, 1)
            if stop >= 3:
                dve.wait_ge(ffn_add, NT)
                for j in range(NT + 1):
                    if j < NT:
                        ln_stats(j)
                    if j:
                        ln_apply(2, j - 1)
                for t in range(NT):
                    dve.wait_ge(c_out, t + 1)
                    dve.tensor_copy(ab[:, t, :], ps[:, 4 * (t % 2) + 2, 0:2 * NH]).then_inc(c_ab, 1)
                    step(dve.tensor_tensor(sq.rearrange("p (w n) -> p w n", w=2), kq_tok[:, :, t, :], kq_tok[:, :, t, :], ALU.mult))
                    dve.tensor_reduce(ssum[:, t, :], sq.rearrange("p (h d) -> p h d", d=DH), AX.X, ALU.add).then_inc(ss_ok, 1)
                    dve.wait_ge(ss_ok, t + 1)
                z, u, alpha, be, gb, beta, s2, q1 = small
                s1 = be
                dve.wait_ge(d_w3, 96)
                dve.wait_ge(c_ab, NT)
                dve.tensor_tensor(z, ab[:, :, 0:NH], dt_bias.unsqueeze(1).broadcast_to([P, NT, NH]), ALU.add).then_inc(dve_ab, 1)
                dve.wait_ge(act_ab, 4)
                step(dve.tensor_scalar(be, be, 1.0, None, ALU.add))
                step(dve.reciprocal(beta, be))
                step(dve.tensor_scalar(s1, u, 2.0, None, ALU.add))
                step(dve.reciprocal(s2, s1))
                step(dve.tensor_tensor(s1, u, s2, ALU.mult))
                step(dve.tensor_tensor(s2, s1, s1, ALU.mult))
                step(dve.tensor_scalar(q1, s2, 1.0 / 15, None, ALU.mult))
                for m in (13, 11, 9, 7, 5, 3):
                    step(dve.scalar_tensor_tensor(out=q1, in0=q1, scalar=1.0 / m, in1=s2, op0=ALU.add, op1=ALU.mult))
                step(dve.scalar_tensor_tensor(out=q1, in0=q1, scalar=1.0, in1=s1, op0=ALU.add, op1=ALU.mult))
                step(dve.tensor_scalar(z, z, 0.0, None, ALU.max))
                step(dve.scalar_tensor_tensor(out=z, in0=q1, scalar=2.0, in1=z, op0=ALU.mult, op1=ALU.add))
                dve.tensor_tensor(alpha, z, a_exp.unsqueeze(1).broadcast_to([P, NT, NH]), ALU.mult).then_inc(dve_ab, 1)
                dve.wait_ge(nrm_ok, 1)
                step(dve.tensor_scalar(rnorm, rnorm, 1e-12, None, ALU.max))
                step(dve.reciprocal(ssum, rnorm))
                step(dve.tensor_scalar(ssum[:, :, NH:], ssum[:, :, NH:], DH ** -0.5, None, ALU.mult))
                for t in range(NT):
                    for w in range(2):
                        kq = kq_tok[:, w, t, :].rearrange("p (h d) -> p h d", d=DH)
                        ins = dve.tensor_tensor(kq, kq, ssum[:, t, w * NH:(w + 1) * NH].unsqueeze(2).broadcast_to([P, NH, DH]), ALU.mult)
                    ins.then_inc(kq_ok, 1)

                def pick(t):
                    dve.wait_ge(g_mm, t + 1)
                    dve.tensor_scalar(pick_dve, half_products(0), half_mask[:, 0:1], None, ALU.mult).then_inc(pick_dve_ok, 1)
                    dve.wait_ge(pick_dve_ok, t + 1)
                    dve.wait_ge(pick_act_ok, t + 1)
                    for hh in range(2):
                        ins = dve.tensor_tensor(gp[:, t, 8 * hh:8 * hh + 8].rearrange("p (r o) w i -> p r (o w i)", o=2),
                                                pick_dve[:, :, 4 * hh:4 * hh + 4].rearrange("p r e i -> p r (e i)"),
                                                pick_act[:, t % 2, :, 4 * hh:4 * hh + 4].rearrange("p r e i -> p r (e i)"), ALU.add)
                    ins.then_inc(g_out, 1)
                    dve.wait_ge(g_out, t + 1)

                for t in range(NT):
                    pick(t)
                dve.wait_ge(su_mm, 1)
                step(dve.tensor_copy(ab_u, ps[:, 6, :].rearrange("p (a u t) -> p a u t", a=2, u=16)))
                step(dve.tensor_copy(decay, eye16.rearrange("p (i j) -> p i j", i=DH).unsqueeze(2).broadcast_to([P, DH, 16, DH])))
                for i in range(1, DH):
                    step(dve.tensor_tensor(decay[:, i, :, 0:i], decay[:, i - 1, :, 0:i], ab_u[:, 0, :, i:i + 1].broadcast_to([P, 16, i]), ALU.mult))
                dve.tensor_tensor(gam_u, decay[:, :, :, 0].rearrange("p i u -> p u i"), ab_u[:, 0, :, 0:1].broadcast_to([P, 16, DH]), ALU.mult
                                  ).then_inc(du_ok, 1)
                dve.wait_ge(du_ok, 1)
                for n in range(8):
                    half, ig = divmod(n, 4)
                    dve.wait_ge(dt_mm, n + 1)
                    for par in range(2):
                        ins = dve.scalar_tensor_tensor(
                            out=p_blk[:, 128 * half:128 * half + 128, par, 4 * ig:4 * ig + 4],
                            in0=ps[:, n % 2, :].rearrange("p (i c) -> p c i", i=4), scalar=half_mask[:, par:par + 1],
                            in1=gp[:, :, :, 1].rearrange("p t h i -> p (t h) i")[:, 128 * half:128 * half + 128, 4 * ig:4 * ig + 4],
                            op0=ALU.mult, op1=ALU.mult)
                    ins.then_inc(dt_out, 1)
                dve.wait_ge(dt_out, 8)
                for n in range(8):
                    half, ig = divmod(n, 4)
                    dve.wait_ge(gu_mm, n + 1)
                    d = decay.rearrange("p i u j -> p i (u j)")[:, 4 * ig:4 * ig + 4, 128 * half:128 * half + 128]
                    dve.scalar_tensor_tensor(out=a_u.rearrange("p i u j -> p i (u j)")[:, 4 * ig:4 * ig + 4, 128 * half:128 * half + 128],
                                             in0=ps[:, 2 + n % 2, :].rearrange("p (i c) -> p i c", i=4), scalar=-1.0, in1=d,
                                             op0=ALU.mult, op1=ALU.mult).then_inc(gu_out, 1)
                dve.wait_ge(gu_out, 8)
                for i in range(1, DH):
                    ins = dve.tensor_tensor(a_u[:, i], a_u[:, i], ab_u[:, 1, :, i:i + 1].broadcast_to([P, 16, DH]), ALU.mult)
                step(ins)
                step(dve.tensor_copy(t_u, eye16.rearrange("p (i j) -> p i j", i=DH).unsqueeze(2).broadcast_to([P, DH, 16, DH])))
                for i in range(1, DH):
                    pr = t_prod[:, 0:16 * i * i].rearrange("p (u c j) -> p u c j", u=16, c=i)
                    step(dve.tensor_tensor(pr, a_u[:, i, :, 0:i].unsqueeze(2).broadcast_to([P, 16, i, i]),
                                           t_u[:, 0:i, :, 0:i].rearrange("p j u c -> p u c j"), ALU.mult))
                    step(dve.tensor_reduce(t_u[:, i, :, 0:i], pr, AX.X, ALU.add))
                dve.wait_ge(gd_ok, 1)
                step(dve.tensor_tensor(gb.rearrange("p t h -> p (t h)"), gd[:, 0], beta.rearrange("p t h -> p (t h)"), ALU.mult))
                dve.tensor_tensor(gk, kq_tok[:, 0].rearrange("p t (h d) -> p (t h) d", d=DH),
                                  gb.rearrange("p t h -> p (t h)").unsqueeze(2).broadcast_to([P, NT * NH, DH]), ALU.mult).then_inc(gk_ok, 1)
                dve.tensor_tensor(gam_m, gam_u[:, :, DH - 1].unsqueeze(1).broadcast_to([P, 8, 16]),
                                  tile_mask.unsqueeze(2).broadcast_to([P, 8, 16]), ALU.mult).then_inc(gm_ok, 1)
                dve.memset(state, 0.0).then_inc(s_ok[0], 1)
                dve.wait_ge(s_ok[0], 1)
                dve.engine_nop().then_inc(s_ok[1], 1)
                for n in range(1, 8, 2):
                    take_inverse(dve, n)
                dve.wait_ge(gf_mm, 1)
                dve.tensor_copy(gf, ps[:, 6, 0:256].rearrange("p (a c u) -> p a c u", a=2, c=8)).then_inc(gf_ok, 1)
                for t in range(NT + 1):
                    if t < NT:
                        take_uw(dve, t)
                    if t:
                        i = t - 1
                        dve.wait_ge(wq_mm, i + 1)
                        for par in range(2):
                            src = ps[:, 6 + i % 2, 0:256].rearrange("p (a b x) -> p a b x", a=2, b=B)[:, :, :, DH * par:DH * par + DH]
                            ins = dve.tensor_copy(wq_t5[:, i, :, par, :, DH * (1 - par):DH * (1 - par) + DH], src)
                        ins.then_inc(wq_dve, 1)
                dve.wait_ge(uw_out[0], NT)
                dve.wait_ge(uw_out[1], NT)

                def combine(t):
                    dve.wait_ge(cb_act, t + 1)
                    for w, dst in enumerate((u_tok, comb_qs)):
                        ins = dve.scalar_tensor_tensor(out=dst[:, t, :], in0=xo[:, (2 * t + 1) % 4, :], scalar=half_mask[:, 1 - w:2 - w],
                                                       in1=comb_a[:, t % 2, w], op0=ALU.mult, op1=ALU.add)
                    ins.then_inc(comb_ok, 1)

                for n in range(2 * NT):
                    t, par = divmod(n, 2)
                    for g in range(2):
                        own = slice(64 * g, 64 * g + 64)
                        dve.wait_ge(r_mm[g], n + 1)
                        if t >= 2:
                            dve.wait_ge(comb_ok, t - 1)
                        dve.scalar_tensor_tensor(out=xo[own, n % 4, :].rearrange("p (r x) -> p r x", r=4),
                                                 in0=u_tok[own, t, :].rearrange("p (r x) -> p r x", r=4),
                                                 scalar=half_mask[own, par:par + 1], in1=ps[own, 0:4, 0:64], op0=ALU.mult, op1=ALU.add
                                                 ).then_inc(xo_ok[g], 1)
                    if n and not par:
                        combine(t - 1)
                    for g in range(2) if n < 2 * NT - 1 else ():
                        bs = slice(2 * g, 2 * g + 2)
                        dve.wait_ge(s_mm[g], n + 1)
                        dve.wait_ge(sg_ok[g], n + 1)
                        for a_half in range(2):
                            ins = dve.scalar_tensor_tensor(
                                out=state[:, bs, a_half].rearrange("p b e x -> p b (e x)"), in0=ps[:, 4 + 2 * g:6 + 2 * g, 32 * a_half:32 * a_half + 32],
                                scalar=half_mask[:, a_half:a_half + 1], in1=s_dec[:, bs, a_half].rearrange("p b e x -> p b (e x)"),
                                op0=ALU.mult, op1=ALU.add)
                        ins.then_inc(s_ok[g], 1)
                dve.wait_ge(xo_ok[0], 2 * NT)
                dve.wait_ge(xo_ok[1], 2 * NT)
                combine(NT - 1)
                ms = small[0]
                for t in range(NT):
                    dve.wait_ge(o_out, t + 1)
                    step(dve.tensor_tensor(sq[:, 0:D], o_tok[:, t, :], o_tok[:, t, :], ALU.mult))
                    step(dve.tensor_reduce(ms[:, t, :], sq[:, 0:D].rearrange("p (h d) -> p h d", d=DH), AX.X, ALU.add))
                dve.tensor_scalar(ms, ms, 1.0 / DH, 1e-6, ALU.mult, ALU.add).then_inc(rms_ss, 1)
                dve.wait_ge(rms_rt, 1)
                step(dve.reciprocal(q1, ms))
                dve.wait_ge(gate_ok, 1)
                for t in range(NT):
                    o = o_tok[:, t, :].rearrange("p (h d) -> p h d", d=DH)
                    step(dve.tensor_tensor(o, o, q1[:, t, :].unsqueeze(2).broadcast_to([P, NH, DH]), ALU.mult))
                    dve.tensor_tensor(o_tok[:, t, :], o_tok[:, t, :], gate[:, t, :], ALU.mult).then_inc(og_ok, 1)
                for n in range(NT):
                    j = out_tile(n)
                    dve.wait_ge(wo_mm, n + 1)
                    dve.tensor_tensor(h_res[:, j, :], ps[:, 2 + n % 2, 0:D], h_res[:, j, :], ALU.add).then_inc(attn_add, 1)
            if stop >= 4:
                dve.wait_ge(attn_add, NT)
                for j in range(NT + 1):
                    if j < NT:
                        ln_stats(j)
                    if j:
                        ln_apply(3, j - 1)

                def over(v, n=NE):
                    return v.unsqueeze(2).broadcast_to([P, NT, n])

                def each(v, n=NT):
                    return v.unsqueeze(1).broadcast_to([P, n, NE])

                dve.wait_ge(lg_mm, 1)
                step(dve.tensor_tensor(lg, ps[:, 0, 0:NT * NE].rearrange("p (j e) -> p j e", e=NE), each(rb), ALU.add))
                step(dve.tensor_reduce(lmax, lg, AX.X, ALU.max))
                dve.tensor_tensor(lexp, lg, over(lmax), ALU.subtract).then_inc(sh_ok, 1)
                step(dve.tensor_tensor(eq, lg, over(lmax), ALU.is_ge))
                step(dve.tensor_tensor(eq, eq, each(em8), ALU.mult))
                step(dve.tensor_reduce(pos, eq, AX.X, ALU.min))
                dve.tensor_tensor(onehot, each(em8), over(pos), ALU.is_equal).then_inc(hot_ok, 1)
                dve.wait_ge(lexp_ok, 1)
                step(dve.tensor_reduce(pmax, lexp, AX.X, ALU.add))
                step(dve.reciprocal(pmax, pmax))
                dve.wait_ge(cnt_mm, 1)
                totals = ps[:, 2, 0:NT * NE].rearrange("p (j e) -> p j e", e=NE)
                step(dve.tensor_copy(cnt[:, 0], totals))
                src, w = 0, 1
                while w < NT:
                    step(dve.tensor_copy(cnt[:, 1 - src, 0:w], cnt[:, src, 0:w]))
                    step(dve.tensor_tensor(cnt[:, 1 - src, w:NT], cnt[:, src, w:NT], cnt[:, src, 0:NT - w], ALU.add))
                    src, w = 1 - src, 2 * w
                step(dve.tensor_tensor(cmp_[:, 0:NE], cnt[:, src, NT - 1].unsqueeze(2).broadcast_to([P, NE, NE]), each(thr, NE), ALU.is_gt))
                step(dve.tensor_reduce(ends[:, 0], cmp_[:, 0:NE], AX.X, ALU.add))
                step(dve.tensor_copy(ends[:, 2], ends[:, 0]))
                at_, w = 0, 1
                while w < NE:
                    step(dve.tensor_copy(ends[:, 1 - at_, 0:w], ends[:, at_, 0:w]))
                    step(dve.tensor_tensor(ends[:, 1 - at_, w:NE], ends[:, at_, w:NE], ends[:, at_, 0:NE - w], ALU.add))
                    at_, w = 1 - at_, 2 * w
                step(dve.tensor_tensor(base, ends[:, at_], ends[:, 2], ALU.subtract))
                step(dve.tensor_scalar(base, base, float(ET), None, ALU.mult))
                step(dve.tensor_tensor(cmp_, each(ends[:, at_], NET), tile_no.unsqueeze(2).broadcast_to([P, NET, NE]), ALU.is_le))
                step(dve.tensor_reduce(te[:, 0:NET], cmp_, AX.X, ALU.add))
                step(dve.tensor_scalar(te_i[:, 0:NET], te[:, 0:NET], float(NE - 1), None, ALU.min))
                step(dve.tensor_tensor(cnt[:, 2], cnt[:, src], totals, ALU.subtract))
                step(dve.tensor_tensor(cnt[:, 2], ps[:, 1, 0:NT * NE].rearrange("p (j e) -> p j e", e=NE), cnt[:, 2], ALU.add))
                step(dve.tensor_tensor(cnt[:, 2], cnt[:, 2], each(base), ALU.add))
                step(dve.tensor_tensor(cnt[:, 2], cnt[:, 2], onehot, ALU.mult))
                step(dve.tensor_reduce(pos, cnt[:, 2], AX.X, ALU.add))
                dve.tensor_copy(pos_i, pos).then_inc(pos_ok, 1)

                def expert(t, slot, first):
                    for m in range(HC):
                        dve.wait_ge(e_silu, t * HC + m + 1)
                        if m == 0 and not first:
                            dve.wait_ge(e2_mm, t - 1)
                        dve.tensor_tensor(eu[:, slot, m, :], ps[:, m % 4, ET:2 * ET], silu[:, m % 2], ALU.mult).then_inc(e1_out, 1)
                    dve.wait_ge(e2_mm, t + 1)
                    if not first:
                        dve.wait_ge(d_ys[slot], t * 8 if slot == 0 else t * 8 - 8)
                    dve.tensor_copy(ys[:, slot], ps[:, 4:6, 0:D]).then_inc(e2_out, 1)

                expert_tiles(dve, expert)
                dve.wait_ge(d_yg, 16 * NT)
                for j in range(NT):
                    dve.scalar_tensor_tensor(out=h_res[:, j, :], in0=yg[:, j, :], scalar=pmax[:, j:j + 1], in1=h_res[:, j, :],
                                             op0=ALU.mult, op1=ALU.add).then_inc(fin, 1)


def delta_constants():
    p, c = np.arange(P)[:, None], np.arange(P)[None]
    half = p % 32 // DH
    cols = [half == np.arange(2)[None], np.tile(np.eye(DH).reshape(1, -1), (P, 1)), half == c[:, :32] // DH,
            (p // 32 == c // 32) & ((p + DH) % 32 == c % 32)]
    cols += [p % NH == 8 * hh + c // DH for hh in range(2)] + [p // NH == np.arange(8)[None]]
    return np.concatenate([np.asarray(x, np.float32) for x in cols], axis=1)


def kernel(**inputs):
    import concourse.bacc as bacc
    from concourse import mybir as _mybir
    from concourse.bass_utils import run_bass_kernel_spmd

    n = {name: np.asarray(v) for name, v in inputs.items()}
    x = n["x"].reshape(B, 2, P, 2, D, TOK_D)
    arrays = {
        "x_t": x.transpose(5, 4, 0, 1, 3, 2).reshape(TOK_D * D, B * S),
        "tok_ws_t": n["L0_tok_weighted_sum"].T,
        "tok_w_t": n["L0_tok_weight"].T,
        "keys_t": n["L0_attn_keys"][0].T,
        "vals_t": n["L0_attn_values"][0].T,
        "wq_t": n["L0_attn_Wq_w"].T,
        "wk_t": n["L0_attn_Wk_w"].T,
        "wv_t": n["L0_attn_Wv_w"].T,
        "bias_qk": np.stack([n["L0_attn_Wq_b"], n["L0_attn_Wk_b"]]).reshape(2, FC, P).transpose(2, 0, 1),
        "bias_v": n["L0_attn_Wv_b"][None],
        "w1_t": n["L0_ffn_w1"].T,
        "w2_t": n["L0_ffn_w2"].T,
        "b1": n["L0_ffn_b1"].reshape(HC, P).T,
        "b2": n["L0_ffn_b2"][None],
        "w_cat": np.concatenate([n["L1_attn_" + w] for w in ("Wk", "Wq", "Wv", "Wgate", "Walpha", "Wbeta")], axis=1),
        "w_out": n["L1_attn_Wout"],
        "dt_bias": n["L1_attn_dt_bias"][None],
        "a_log": n["L1_attn_A_log"][None],
        "rms_w": n["L1_attn_rms_w"][None],
        "dconst": delta_constants(),
        "router_w": n["L1_ffn_router_w"],
        "router_b": n["L1_ffn_router_b"][None],
        "ew1": n["L1_ffn_w1"],
        "ew2": n["L1_ffn_w2"],
        "tri": np.triu(np.ones((P, P), np.float32), 1),
        "em8": np.arange(-NE, 0, dtype=np.float32)[None],
        "thr": np.arange(0, NE * ET, ET, dtype=np.float32)[None],
        "tile_no": np.arange(NET, dtype=np.float32)[None],
    }
    arrays = {f"in_{name}": np.ascontiguousarray(v) for name, v in arrays.items()}
    nc = bacc.Bacc("TRN2", target_bir_lowering=False, num_devices=1)
    aps = {name[3:]: nc.dram_tensor(name, v.shape, _mybir.dt.from_np(v.dtype), kind="ExternalInput").ap()
           for name, v in arrays.items()}
    out = nc.dram_tensor("out", [B * S, D], F32, kind="ExternalOutput").ap()
    build(nc, aps, out, STOP)
    r = run_bass_kernel_spmd(nc, [arrays], core_ids=[0])
    return r.results[0]["out"].reshape(B, S, D)
```

```python
from contextlib import ExitStack

import numpy as np
from concourse import mybir
from concourse.bass import IndirectOffsetOnAxis, ds

F32 = mybir.dt.float32
BF16 = mybir.dt.bfloat16
I32 = mybir.dt.int32
U32 = mybir.dt.uint32
ALU = mybir.AluOpType
ACT = mybir.ActivationFunctionType
AX = mybir.AxisListType

P = 128
B, S, D = 4, 512, 256
NT = B * S // P
FC = D // P
TOK_D = 4
NK, NH, DH = 1024, 16, 16
KC = NK // P
QT = S // P
HC = 8
NE = 8
ET = 256
NET = (B * S + NE * (ET - 1)) // ET
CAT = 4 * D + 2 * NH
NPART = 96
HID = 1024
LN_EPS = 1e-5


STOP = 4


def build(nc, a, out, stop):
    with ExitStack() as ctx:
        def sb(name, shape, dt=F32):
            return ctx.enter_context(nc.sbuf_tensor(name, shape, dt))

        def sem(name):
            return ctx.enter_context(nc.semaphore(name))

        ps = ctx.enter_context(nc.psum_tensor("ps", [P, 8, 512], F32))
        h_res = sb("h_res", [P, NT, D])
        xn = sb("xn", [P, NT, D])
        ident = sb("ident", [P, P])
        ident_b = sb("ident_b", [P, P], BF16)
        bn = sb("bn", [P, 2, 6])
        mv = sb("mv", [P, NT, 2])
        var_eps = sb("var_eps", [P, NT])
        rstd = sb("rstd", [P, NT])
        ones = sb("ones", [P, P])
        minus_half = sb("minus_half", [P, NT * 32])
        arena = sb("arena", [P, 44000])

        def view(at, shape, dt=F32):
            n = int(np.prod(shape))
            words = n if dt in (F32, I32, U32) else n // 2
            v = arena[:, at:at + words]
            if dt != F32:
                v = v.bitcast(dt)
            names = " ".join(f"d{i}" for i in range(len(shape)))
            if len(shape) > 1:
                v = v.rearrange(f"p ({names}) -> p {names}", **{f"d{i}": s for i, s in enumerate(shape)})
            return v, at + words

        at = 0
        xnt, at = view(at, [FC, NT * P])
        kstk, at = view(at, [NH, NK], BF16)
        at_q1 = at + NH * S // 2
        qstk, at = view(at, [2, NH, S], BF16)
        vaug, at = view(at, [KC, NH, 32])
        at_att = at
        x_t = []
        for b in range(B - 1):
            v, at = view(at, [8, S])
            x_t.append(v)
        x_t.append(view(at_q1 - NH * S // 2, [8, S])[0])
        w_tok, at = view(at, [8, D])
        ws_t, w_at = view(0, [FC, D])
        w_bc, _ = view(w_at, [TOK_D, D])
        at_tok = at
        at = at_att
        prob, at = view(at, [2, 4, S])
        att, at = view(at, [2, S])
        rden, at = view(at, [S])
        spread, at = view(at, [P])
        gather, at = view(at, [2, P])
        mx, at = view(at, [2, QT, NH])
        mx1, at = view(at, [QT, NH])
        mlo, at = view(at, [QT, NH])
        mpad, at = view(at, [QT, P], BF16)
        mrow, at = view(at, [S], BF16)
        at_free = at
        assert at <= at_tok
        at = at_tok
        keys_t, k_at = view(at_q1, [FC, NK])
        vals_t, _ = view(k_at, [FC, NK])
        wq_t, at = view(at, [FC, D])
        wk_t, at = view(at, [FC, D])
        wv_t, at = view(at, [FC, D])
        bias_qk, at = view(at, [2, FC])
        bias_v, at = view(at, [D])
        sel, at = view(at, [NH])
        proj, at = view(at, [2, S])
        part, at = view(at, [2, 3, S], BF16)
        vtmp, at = view(at, [2, D])
        assert at <= 44000, at
        at = at_free
        w1, at = view(at, [FC, HID])
        w2, at = view(at, [HC, D])
        w_abs, at = view(at, [HC * D])
        w_mean, at = view(at, [HC * D])
        w_sign, at = view(at, [HC * D])
        bias_1, at = view(at, [HC])
        bias_2, at = view(at, [D])
        assert at <= 44000, at
        hid, _ = view(FC * NT * P, [2, HC, S])
        ffn_sum, _ = view(FC * NT * P + 2 * HC * S, [2, D])

        R = NT * D
        kq_tok, _ = view(0, [2, NT, D])
        v_tok, _ = view(2 * R, [NT, D])
        gp, _ = view(3 * R, [NT, NH, 2, DH])
        a_u, _ = view(6 * R, [DH, 16, DH])
        gk, _ = view(4 * R, [NT * NH, DH])
        comb_qs, _ = view(0, [NT, D])
        t_u, _ = view(3 * R, [2, DH, 8, DH])
        u_tok, _ = view(3 * R, [NT, D])
        vgk, _ = view(2 * R, [2, 2 * R])
        decay, _ = view(5 * R, [DH, 16, DH])
        t_prod = [view(4 * R + half * R // 2, [R // 2])[0] for half in range(2)]
        sq, at = view(6 * R, [2 * D])
        k_f, at = view(at, [2, 2, P])
        kq_one, at = view(at, [2, 2, 2, 2, P])
        pick_dve, at = view(at, [4, 8, DH])
        pick_act, at = view(at, [2, 4, 8, DH])
        t_blk, _ = view(5 * R, [NT * NH, 2, DH])
        wq_t5, _ = view(5 * R, [NT, 2, 2, B, 32])
        o_tok, _ = view(5 * R, [NT, D])
        o_f, _ = view(6 * R, [FC, B, S])
        p_blk, _ = view(7 * R, [NT * NH, 2, DH])
        xnt4, at = view(7 * R, [FC, NT * P])
        w_cat, at = view(at, [FC, CAT])
        k_even, _ = view(4 * R, [NT, D])
        k_odd = v_tok
        at = R
        xo, at = view(at, [4, D])
        comb_a, at = view(at, [2, 2, D])
        w_out, at = view(9 * R, [FC, D])
        small = []
        for _ in range(8):
            v, at = view(at, [NT, NH])
            small.append(v)
        w_neg, _ = view(at, [2, D])
        ab, at = view(at, [NT, 2 * NH])
        ssum, at = view(at, [NT, 2 * NH])
        rnorm, at = view(at, [NT, 2 * NH])
        state, s_at = view(at - NT * 4 * NH, [B, 2, 2, DH])
        s_dec, s_at = view(s_at, [B, 2, 2, DH])
        dt_bias, at = view(at, [NH])
        a_exp, at = view(at, [NH])
        rms_w, at = view(at, [DH])
        ab_u, at = view(at, [2, 16, DH])
        gam_u, at = view(at, [16, DH])
        gd, at = view(at, [2, NT * NH])
        gf, at = view(at, [2, 8, 16])
        gam_m, at = view(at, [8, 16])
        at_dconst = at
        half_mask, at = view(at, [2])
        eye16, at = view(at, [DH * DH])
        head_mask, at = view(at, [32])
        swap, at = view(at, [P])
        head_sel, at = view(at, [2, P])
        tile_mask, at = view(at, [8])
        dconst, at = view(at_dconst, [at - at_dconst])
        assert at <= 43744, at
        zero_row, _ = view(43744, [D])
        at = FC * NT * P
        rw, at = view(at, [FC, NE])
        rb, at = view(at, [NE])
        tri, at = view(at, [P])
        em8, at = view(at, [NE])
        thr, at = view(at, [NE])
        tile_no, at = view(at, [NET])
        lg, at = view(at, [NT, NE])
        lmax, at = view(at, [NT])
        eq, at = view(at, [NT, NE])
        onehot, at = view(at, [NT, NE])
        lexp, at = view(at, [NT, NE])
        pmax, at = view(at, [NT])
        cnt, at = view(at, [3, NT, NE])
        cmp_, at = view(at, [NET, NE])
        ends, at = view(at, [3, NE])
        base, at = view(at, [NE])
        pos, at = view(at, [NT])
        pos_i, at = view(at, [NT], U32)
        te, at = view(at, [NET + 1])
        te_i, at = view(at, [NET + 1], U32)
        ew1, at = view(at, [2, FC, 2 * HID])
        ew2, at = view(at, [2, HC, D])
        xs, at = view(at, [2, 2, D])
        xst, at = view(at, [2, FC, ET])
        silu, at = view(at, [2, ET])
        eu, at = view(at, [2, HC, ET])
        ys, at = view(at, [2, 2, D])
        yg, at = view(at, [NT, D])
        assert at <= 43744, at
        xs_dram = nc.dram_tensor("xs_dram", [NET * ET, D], F32, kind="Internal").ap()
        ys_dram = nc.dram_tensor("ys_dram", [NET * ET, D], F32, kind="Internal").ap()
        gate = xn[:, :, :]
        qk_parts = nc.dram_tensor("qk_parts", [3, D, NK + B * S], BF16, kind="Internal").ap()

        d_small = sem("d_small")
        d_kv = sem("d_kv")
        d_x = [sem(f"d_x{b}") for b in range(B)]
        consts = sem("consts")
        ident_ok = sem("ident_ok")
        wtok_ok = sem("wtok_ok")
        mm_tok = sem("mm_tok")
        tok_out = sem("tok_out")
        dve_step = sem("dve_step")
        pool_step = sem("pool_step")
        ln_var = sem("ln_var")
        ln_rstd = sem("ln_rstd")
        ln_out = sem("ln_out")
        tp_mm = sem("tp_mm")
        tp_out = sem("tp_out")
        pj_mm = sem("pj_mm")
        pj_out = sem("pj_out")
        pj_split = sem("pj_split")
        d_part = [sem("d_part0"), sem("d_part1")]
        d_kstk = sem("d_kstk")
        d_qstk = [sem(f"d_qstk{b}") for b in range(B)]
        sel_ok = sem("sel_ok")
        v_mm = sem("v_mm")
        v_out = sem("v_out")
        st_mm = sem("st_mm")
        exp_out = sem("exp_out")
        sm_mm = sem("sm_mm")
        max_out = sem("max_out")
        av_mm = sem("av_mm")
        av_out = sem("av_out")
        mx_pad = sem("mx_pad")
        mx_mm = sem("mx_mm")
        mx_row = sem("mx_row")
        d_mrow = sem("d_mrow")
        at_mm = sem("at_mm")
        at_add = sem("at_add")
        rd_ok = sem("rd_ok")
        sum_mm = sem("sum_mm")
        att_ok = sem("att_ok")
        h_pre = sem("h_pre")
        d_out = sem("d_out")
        zero_ok = sem("zero_ok")
        d_zero = sem("d_zero")
        d_rt = sem("d_rt")
        lg_mm = sem("lg_mm")
        lg_out = sem("lg_out")
        hot_ok = sem("hot_ok")
        sh_ok = sem("sh_ok")
        lexp_ok = sem("lexp_ok")
        cnt_mm = sem("cnt_mm")
        pos_ok = sem("pos_ok")
        d_disp = sem("d_disp")
        d_ew = [sem("d_ew0"), sem("d_ew1")]
        et_mm = sem("et_mm")
        et_out = sem("et_out")
        e1_mm = sem("e1_mm")
        e_silu = sem("e_silu")
        e1_out = sem("e1_out")
        e2_mm = sem("e2_mm")
        e2_out = sem("e2_out")
        d_ys = [sem("d_ys0"), sem("d_ys1")]
        d_yg = [sem(f"d_yg{b}") for b in range(B)]
        fin = sem("fin")
        d_w = sem("d_w")
        abs_ok = sem("abs_ok")
        mean_mm = sem("mean_mm")
        mean_ok = sem("mean_ok")
        w_ok = sem("w_ok")
        f1_mm = sem("f1_mm")
        f1_out = sem("f1_out")
        f2_mm = sem("f2_mm")
        f2_out = sem("f2_out")
        ffn_add = sem("ffn_add")
        d_w3 = sem("d_w3")
        c_mm = sem("c_mm")
        c_out = sem("c_out")
        c_ab = sem("c_ab")
        ss_ok = sem("ss_ok")
        nrm_ok = sem("nrm_ok")
        act_ab = sem("act_ab")
        dve_ab = sem("dve_ab")
        gate_ok = sem("gate_ok")
        kq_ok = sem("kq_ok")
        alpha_ok = sem("alpha_ok")
        gt_mm = sem("gt_mm")
        gt_out = sem("gt_out")
        g_mm = sem("g_mm")
        pick_dve_ok = sem("pick_dve_ok")
        pick_act_ok = sem("pick_act_ok")
        g_out = sem("g_out")
        su_mm = sem("su_mm")
        du_ok = sem("du_ok")
        gd_mm = sem("gd_mm")
        gd_ok = sem("gd_ok")
        dt_mm = sem("dt_mm")
        dt_out = sem("dt_out")
        gu_mm = sem("gu_mm")
        gu_out = sem("gu_out")
        gk_ok = sem("gk_ok")
        gm_ok = sem("gm_ok")
        gf_mm = sem("gf_mm")
        gf_ok = sem("gf_ok")
        tt_mm = sem("tt_mm")
        tt_out = [sem("tt_out_act"), sem("tt_out_dve")]
        vb_ok = sem("vb_ok")
        qg_ok = sem("qg_ok")
        kd_ok = sem("kd_ok")
        kt_ok = [sem("kt_ok0"), sem("kt_ok1")]
        uw_mm = sem("uw_mm")
        uw_out = [sem("uw_out_act"), sem("uw_out_dve")]
        wq_mm = sem("wq_mm")
        wq_act = sem("wq_act")
        wq_dve = sem("wq_dve")
        s_ok = [sem("s_ok0"), sem("s_ok1")]
        r_mm = [sem("r_mm0"), sem("r_mm1")]
        xo_ok = [sem("xo_ok0"), sem("xo_ok1")]
        s_mm = [sem("s_mm0"), sem("s_mm1")]
        sg_ok = [sem("sg_ok0"), sem("sg_ok1")]
        cb_act = sem("cb_act")
        comb_ok = sem("comb_ok")
        o_mm = sem("o_mm")
        o_out = sem("o_out")
        rms_ss = sem("rms_ss")
        rms_rt = sem("rms_rt")
        og_ok = sem("og_ok")
        og_mm = sem("og_mm")
        og_out = sem("og_out")
        wo_mm = sem("wo_mm")
        attn_add = sem("attn_add")

        def take_inverse(eng, n):
            half, ig = divmod(n, 4)
            eng.wait_ge(tt_mm, n + 1)
            for par in range(2):
                dst = t_blk[:, 128 * half:128 * half + 128, par, 4 * ig:4 * ig + 4]
                src = ps[:, 4 + n % 2, :].rearrange("p (i c) -> p c i", i=4)
                if eng is nc.vector:
                    ins = eng.tensor_scalar(dst, src, half_mask[:, par:par + 1], None, ALU.mult)
                else:
                    ins = eng.activation(dst, src, ACT.Copy, scale=half_mask[:, par:par + 1])
            ins.then_inc(tt_out[n % 2], 1)

        def take_uw(eng, t):
            hh = 1 if eng is nc.vector else 0
            eng.wait_ge(uw_mm, t + 1)
            if t >= 2:
                eng.wait_ge(wq_mm, t - 1)
            src = ps[:, 2 * (t % 2) + hh, 0:256].rearrange("p (r o x) -> p r o x", r=4, o=2)
            dst_u = u_tok[:, t, :].rearrange("p (r e o x) -> p r e o x", r=4, e=2, o=2)[:, :, hh]
            dst_w = w_neg[:, t % 2, P * hh:P * hh + P].rearrange("p (r o x) -> p r o x", r=4, o=2)
            if hh:
                eng.tensor_copy(dst_u, src[:, :, :, 0:DH])
                ins = eng.tensor_scalar(dst_w, src[:, :, :, DH:], -1.0, None, ALU.mult)
            else:
                eng.copy(dst_u, src[:, :, :, 0:DH])
                ins = eng.activation(dst_w, src[:, :, :, DH:], ACT.Copy, scale=-1.0)
            ins.then_inc(uw_out[hh], 1)

        def part_keys(eng, half):
            tiles = slice(NT // 2 * half, NT // 2 * (half + 1))
            eng.wait_ge(kd_ok, 1)
            eng.wait_ge(uw_mm, NT // 2 * (half + 1))
            if eng is nc.vector:
                ins = eng.tensor_scalar(k_even[:, tiles], kq_tok[:, 0, tiles], half_mask[:, 0:1], None, ALU.mult)
            else:
                ins = eng.activation(k_odd[:, tiles], kq_tok[:, 0, tiles], ACT.Copy, scale=half_mask[:, 1:2])
            ins.then_inc(kt_ok[half], 1)

        def half_products(half):
            return ps[:, 2:6, 0:256].rearrange("p r (e i) -> p r e i", e=8)[:, :, :, DH * half:DH * half + DH]

        def out_tile(n):
            ft, b, u = n // 8, n % 8 // 2, n % 2
            return 4 * b + 2 * ft + u
        def wo_bank(n):
            return (2, 4, 5)[n % 3]

        def expert_tiles(eng, tile):
            tile(0, 0, True)
            tile(1, 1, True)
            with eng.Fori(1, NET // 2) as i:
                tile(i * 2, 0, False)
                tile(i * 2 + 1, 1, False)
            if NET % 2:
                tile(NET - 1, 0, False)

        block = ctx.enter_context(nc.Block())
        NU = 4 + 2 * B

        def turn_bank(stage, j):
            return ((2, 3), (2, 3), (3, 7), (3, 7))[stage][j % 2]

        def unit_cols(u):
            return (u // 2) * S

        @block.sync
        def _(sp):
            sp.dma_start(ws_t, a["tok_ws_t"].rearrange("(c p) n -> p c n", p=P)).then_inc(d_small, 16)
            sp.dma_start(w_bc, a["tok_w_t"].rearrange("(a d) n -> a d n", a=1).broadcast_to([P, TOK_D, D])).then_inc(d_small, 16)
            sp.dma_start(bias_qk, a["bias_qk"]).then_inc(d_small, 16)
            sp.dma_start(bias_v, a["bias_v"].broadcast_to([P, D])).then_inc(d_small, 16)
            for dst, name in ((keys_t, "keys_t"), (wk_t, "wk_t"), (vals_t, "vals_t"), (wv_t, "wv_t"), (wq_t, "wq_t")):
                sp.dma_start(dst, a[name].rearrange("(c p) n -> p c n", p=P)).then_inc(d_kv, 16)
            order_k, order_q = (0, 1, 0, 1, 2, 0), (0, 0, 1, 1, 0, 2)
            for u in range(NU):
                sp.wait_ge(pj_split, u + 1)
                m = u % 2
                sp.dma_start(qk_parts[:, m * P:(m + 1) * P, unit_cols(u):unit_cols(u) + S].rearrange("t p n -> p t n"),
                             part[:, u % 2]).then_inc(d_part[u % 2], 16)
                if u == 3:
                    sp.wait_ge(d_part[0], 32)
                    sp.wait_ge(d_part[1], 32)
                    for r, t in enumerate(order_k):
                        sp.dma_start(kstk[r * DH:(r + 1) * DH], qk_parts[t, :, 0:NK].rearrange("(h d) n -> d h n", d=DH)
                                     ).then_inc(d_kstk, 16)
                if u >= NU - 3 and u % 2:
                    b = (u - (NU - 3)) // 2
                    sp.wait_ge(d_part[0], 16 * (b + 3))
                    sp.wait_ge(d_part[1], 16 * (b + 3))
                    sp.wait_ge(mm_tok, NT)
                    for r, t in enumerate(order_q):
                        sp.dma_start(qstk[r * DH:(r + 1) * DH, b],
                                     qk_parts[t, :, NK + b * S:NK + (b + 1) * S].rearrange("(h d) n -> d h n", d=DH)
                                     ).then_inc(d_qstk[b], 16)
            for m in range(2):
                sp.wait_ge(d_part[m], 16 * (NU // 2))
            sp.wait_ge(pj_mm, NU)
            sp.wait_ge(v_out, KC)
            for dst, src in ((w1, a["w1_t"].rearrange("(c p) n -> p c n", p=P)), (w2, a["w2_t"].rearrange("(c p) n -> p c n", p=P)),
                             (bias_1, a["b1"]), (bias_2, a["b2"].broadcast_to([P, D]))):
                sp.dma_start(dst, src).then_inc(d_w, 16)
            for b in range(B):
                if 1 <= b < B - 1:
                    sp.wait_ge(st_mm, 64 * b)
                    for r, t in enumerate(order_q):
                        sp.dma_start(qstk[r * DH:(r + 1) * DH, (b + 1) % 2],
                                     qk_parts[t, :, NK + (b + 1) * S:NK + (b + 2) * S].rearrange("(h d) n -> d h n", d=DH)
                                     ).then_inc(d_qstk[b + 1], 16)
                sp.wait_ge(mx_row, b + 1)
                sp.dma_start(qstk[NPART:P, b % 2], mrow[NPART:P].unsqueeze(1).broadcast_to([P - NPART, NH, S])).then_inc(d_mrow, 16)
            if stop == 1:
                sp.wait_ge(at_add, 2 * B)
            if stop >= 2:
                sp.wait_ge(ffn_add, NT)
            if stop >= 3:
                for dst, src in ((w_cat, a["w_cat"].rearrange("(c p) n -> p c n", p=P)),
                                 (w_out, a["w_out"].rearrange("(c p) n -> p c n", p=P)),
                                 (dt_bias, a["dt_bias"].broadcast_to([P, NH])), (a_exp, a["a_log"].broadcast_to([P, NH])),
                                 (rms_w, a["rms_w"].broadcast_to([P, DH])), (dconst, a["dconst"])):
                    sp.dma_start(dst, src).then_inc(d_w3, 16)
                sp.wait_ge(o_mm, NT)
            if stop == 4:
                for dst, src in ((rw, a["router_w"].rearrange("(c p) n -> p c n", p=P)), (rb, a["router_b"].broadcast_to([P, NE])),
                                 (tri, a["tri"]), (em8, a["em8"].broadcast_to([P, NE])), (thr, a["thr"].broadcast_to([P, NE])),
                                 (tile_no, a["tile_no"].broadcast_to([P, NET]))):
                    sp.dma_start(dst, src).then_inc(d_rt, 16)
                sp.wait_ge(pos_ok, 1)

                def load(t, slot, first):
                    if not first:
                        sp.wait_ge(e2_mm, t - 1)
                    e = sp.value_load(te_i[0:1, ds(t, 1)], min_val=0, max_val=NE - 1)
                    sp.dma_start(ew1[:, slot], a["ew1"].rearrange("e (c p) n -> p e c n", p=P)[:, ds(e, 1)].rearrange("p o c n -> p (o c) n")
                                 ).then_inc(d_ew[slot], 16)
                    sp.dma_start(ew2[:, slot], a["ew2"].rearrange("e (c p) n -> p e c n", p=P)[:, ds(e, 1)].rearrange("p o c n -> p (o c) n")
                                 ).then_inc(d_ew[slot], 16)

                    if first and t == 0:
                        sp.wait_ge(d_disp, 16 * NT)
                    sp.dma_start(xs[:, slot], xs_dram.rearrange("(t r p) n -> p t r n", p=P, r=2)[:, ds(t, 1)].rearrange("p o r n -> p (o r) n")
                                 ).then_inc(d_ew[slot], 16)

                expert_tiles(sp, load)
                for b in range(B):
                    sp.wait_ge(fin, 4 * b + 4)
                    sp.dma_start(out.rearrange("(b f p u) c -> p b f u c", b=B, f=2, u=2)[:, b],
                                 h_res[:, 4 * b:4 * b + 4, :].rearrange("p (f u) c -> p f u c", u=2)).then_inc(d_out, 16)
            sp.wait_ge(d_out, 16 * B if stop == 4 else 16)

        @block.gpsimd
        def _(pool):
            pool.memset(ident[:, :], 0.0).then_inc(pool_step, 1)
            pool.memset(minus_half[:, :], -0.5).then_inc(consts, 1)
            pool.wait_ge(pool_step, 1)
            pool.affine_select(out=ident[:, :], in_=ident[:, :], compare_op=ALU.not_equal, fill=1.0, base=0,
                               pattern=[[-1, P]], channel_multiplier=1).then_inc(ident_ok, 1)
            pool.wait_ge(ident_ok, 1)
            pool.memset(sel[NPART:P], 0.0).then_inc(pool_step, 1)
            for i, base in enumerate((0, -NH)):
                pool.wait_ge(pool_step, 2 + i)
                pool.affine_select(out=sel[NPART:P], in_=sel[NPART:P], compare_op=ALU.not_equal, fill=-1.0, base=base,
                                   pattern=[[-1, NH]], channel_multiplier=1).then_inc(pool_step, 1)
            pool.wait_ge(pool_step, 4)
            pool.tensor_copy(kstk[NPART:P], sel[NPART:P].unsqueeze(2).broadcast_to([P - NPART, NH, NK])).then_inc(sel_ok, 1)

            def rstd_of(stage, k, j=None):
                j = k if j is None else j
                pool.wait_ge(ln_var, stage * NT + k + 1)
                pool.tensor_tensor(rstd[:, j:j + 1], var_eps[:, j:j + 1], minus_half[:, 0:1], ALU.pow).then_inc(ln_rstd, 1)

            pool.wait_ge(consts, 1)
            pool.wait_ge(sel_ok, 1)
            for j in range(NT):
                rstd_of(0, j)
            pool.wait_ge(mm_tok, NT)
            pool.memset(spread, 0.0).then_inc(pool_step, 1)
            pool.memset(gather, 0.0).then_inc(pool_step, 1)
            pool.wait_ge(pool_step, 6)
            pool.affine_select(out=spread.rearrange("p (c d) -> p c d", c=4), in_=spread.rearrange("p (c d) -> p c d", c=4),
                               compare_op=ALU.not_equal, fill=1.0, base=-DH, pattern=[[-32, 4], [0, 32]],
                               channel_multiplier=1).then_inc(pool_step, 1)
            for i in range(2):
                pool.wait_ge(pool_step, 7 + i)
                g = gather[:, i, 64 * i:64 * i + 64].rearrange("p (c d) -> p c d", c=4)
                pool.affine_select(out=g, in_=g, compare_op=ALU.not_equal, fill=1.0, base=0, pattern=[[-32, 4], [-1, DH]],
                                   channel_multiplier=1).then_inc(pool_step, 1)
            pool.wait_ge(pool_step, 9)
            pool.memset(ones[:, :], 1.0).then_inc(consts, 4)

            psteps = [9]

            def pstep(ins):
                psteps[0] += 1
                ins.then_inc(pool_step, 1)
                pool.wait_ge(pool_step, psteps[0])

            pool.wait_ge(d_w, 64)
            for i, w in enumerate((w1, w2)):
                w = w.rearrange("p c n -> p (c n)")
                pstep(pool.tensor_scalar(w_sign, w, 0.0, None, ALU.is_gt))
                pool.wait_ge(mean_mm, i + 1)
                pstep(pool.tensor_scalar(w_abs, w, 0.0, None, ALU.is_lt))
                pstep(pool.tensor_tensor(w_sign, w_sign, w_abs, ALU.subtract))
                pool.wait_ge(mean_ok, i + 1)
                pstep(pool.tensor_tensor(w_sign, w_sign, w_mean, ALU.mult))
                pstep(pool.tensor_tensor(w_sign, w_sign, w, ALU.subtract))
                pool.tensor_tensor(w, w, w_sign, ALU.add).then_inc(w_ok, 1)
                pool.wait_ge(w_ok, i + 1)
            if stop >= 2:
                for j in range(NT):
                    rstd_of(1, j)
            if stop >= 4:
                pool.memset(zero_row, 0.0).then_inc(zero_ok, 1)
                pool.wait_ge(zero_ok, 1)
                pool.dma_start(xs_dram.rearrange("(t p) n -> p t n", p=P), zero_row.unsqueeze(1).broadcast_to([P, 2 * NET, D])
                               ).then_inc(d_zero, 16)
            if stop >= 3:
                for j in range(NT):
                    rstd_of(2, j)
                pool.wait_ge(d_w3, 96)
                pool.wait_ge(c_out, NT)
                g = gate.rearrange("p j (h d) -> p (j h) d", d=DH)
                pool.tensor_tensor(g, g, rms_w.unsqueeze(1).broadcast_to([P, NT * NH, DH]), ALU.mult).then_inc(gate_ok, 1)

                def heads(v):
                    return v.rearrange("p t (h d) -> p (t h) d", d=DH)

                def by_head(v):
                    return v.unsqueeze(2).broadcast_to([P, NT * NH, DH])

                pool.wait_ge(alpha_ok, 1)
                pool.wait_ge(gate_ok, 1)
                pool.tensor_tensor(heads(v_tok), heads(v_tok), by_head(small[5].rearrange("p t h -> p (t h)")), ALU.mult).then_inc(vb_ok, 1)
                pool.wait_ge(vb_ok, 1)
                pool.wait_ge(gt_mm, NT)
                pool.wait_ge(gd_ok, 1)
                pool.tensor_tensor(heads(kq_tok[:, 1]), heads(kq_tok[:, 1]), by_head(gd[:, 0]), ALU.mult).then_inc(qg_ok, 1)
                pool.wait_ge(qg_ok, 1)
                pool.wait_ge(gk_ok, 2)
                pool.tensor_tensor(heads(kq_tok[:, 0]), heads(kq_tok[:, 0]), by_head(gd[:, 1]), ALU.mult).then_inc(kd_ok, 1)
                pool.wait_ge(gf_ok, 1)
                for n in range(2 * NT - 1):
                    t, par = divmod(n, 2)
                    for g in range(2):
                        pool.wait_ge(s_ok[g], n + 1)
                        if n or g:
                            pool.wait_ge(sg_ok[1 - g], n + g)
                        for b in (2 * g, 2 * g + 1):
                            f = gf[:, :, t % 8].rearrange("p e (c b a) -> p e c b a", c=2, a=2)[:, :, t // 8, b, par]
                            ins = pool.tensor_tensor(s_dec[:, b], state[:, b], f.unsqueeze(1).unsqueeze(3).broadcast_to([P, 2, 2, DH]), ALU.mult)
                        ins.then_inc(sg_ok[g], 1)
            if stop >= 4:
                for j in range(NT):
                    rstd_of(3, j, out_tile(j))
                pool.wait_ge(pos_ok, 1)
                pool.wait_ge(d_zero, 16)
                for j in range(NT):
                    pool.indirect_dma_start(out=xs_dram, out_offset=IndirectOffsetOnAxis(ap=pos_i[:, j:j + 1], axis=0),
                                            in_=xn[:, j, :], in_offset=None).then_inc(d_disp, 16)
                pool.wait_ge(d_ys[0], 16 * ((NET + 1) // 2))
                pool.wait_ge(d_ys[1], 16 * (NET // 2))
                for j in range(NT):
                    pool.indirect_dma_start(out=yg[:, j, :], out_offset=None, in_=ys_dram,
                                            in_offset=IndirectOffsetOnAxis(ap=pos_i[:, j:j + 1], axis=0)).then_inc(d_yg[j // 4], 16)

        @block.scalar
        def _(act):
            act.wait_ge(d_kv, 80)
            for b in range(B):
                act.dma_start(x_t[b],
                              a["x_t"].rearrange("(c p) n -> p c n", p=P)[:, :, b * S:(b + 1) * S]).then_inc(d_x[b], 16)

            def project_out(u):
                act.wait_ge(pj_mm, u + 1)
                if u >= 2:
                    act.wait_ge(pj_split, u - 1)
                which = 0 if u >= 4 else 1
                act.activation(proj[:, u % 2], ps[:, 4 + u % 2, :], ACT.Relu,
                               bias=bias_qk[:, which, u % 2:u % 2 + 1]).then_inc(pj_out, 1)

            def turn_out(stage, k, j=None):
                n, j = stage * NT + k, k if j is None else j
                act.wait_ge(tp_mm, n + 1)
                act.copy(xnt[:, :, j * P:(j + 1) * P],
                         ps[:, turn_bank(stage, k), 0:FC * P].rearrange("p (c n) -> p c n", c=FC)).then_inc(tp_out, 1)

            act.wait_ge(d_small, 64)
            for u in range(4):
                project_out(u)
            for b in range(B):
                for j in range(4 * b, 4 * b + 4):
                    turn_out(0, j)
                for m in range(2):
                    project_out(4 + 2 * b + m)

            def unit(n, e):
                for g in range(2):
                    act.wait_ge(st_mm, 2 * n + g + 1)
                    if g == 0 and not (isinstance(n, int) and n < 2):
                        act.wait_ge(av_mm, n - 1)
                    act.activation(prob[:, e, 2 * g:2 * g + 2, :], ps[:, 2 * g:2 * g + 2, :], ACT.Exp,
                                   scale=DH ** -0.5).then_inc(exp_out, 1)

            def quad(b, q, m, parity):
                for e in range(8):
                    unit(8 * m + e, e % 2)
                    if e == 0 and not (isinstance(q, int) and q == 0):
                        quad_out_slot(8 * m, m - 1, 1 - parity)

            def quad_out_slot(n, m, slot):
                act.wait_ge(av_mm, n)
                if not (isinstance(m, int) and m < 2):
                    act.wait_ge(at_mm, m - 1)
                act.copy(att[:, slot], ps[:, 6, :]).then_inc(av_out, 1)

            act.wait_ge(d_w, 64)
            for i, w in enumerate((w1, w2)):
                if i:
                    act.wait_ge(w_ok, i)
                act.activation(w_abs, w.rearrange("p c n -> p (c n)"), ACT.Abs).then_inc(abs_ok, 1)
                act.wait_ge(mean_mm, i + 1)
                if i == 0:
                    act.mul(w_mean.rearrange("p (c a n) -> p c a n", c=FC, a=2)[:, 0], ps[:, 6:8, :], 1.0 / D)
                    act.mul(w_mean.rearrange("p (c a n) -> p c a n", c=FC, a=2)[:, 1], ps[:, 6:8, :], 1.0 / D).then_inc(mean_ok, 1)
                else:
                    for c in range(HC):
                        ins = act.mul(w_mean.rearrange("p (c n) -> p c n", c=HC)[:, c], ps[:, 6, 0:D], 1.0 / HID)
                    ins.then_inc(mean_ok, 1)

            for b in range(B):
                act.wait_ge(mx_mm, b + 1)
                if b:
                    act.wait_ge(d_mrow, 16 * b)
                act.copy(mrow[NPART:P], ps[NPART:P, 7, 0:S // 2].bitcast(BF16)).then_inc(mx_row, 1)
                quad(b, 0, 4 * b, 0)
                quad(b, 1, 4 * b + 1, 1)
                with act.Fori(1, 2) as qp:
                    for e in range(2):
                        quad(b, None, qp * 2 + (4 * b + e), e)
                quad_out_slot(32 * b + 32, 4 * b + 3, 1)

            if stop >= 2:
                for b in range(B):
                    for j in range(4 * b, 4 * b + 4):
                        turn_out(1, j)
                    for m in range(HC):
                        act.wait_ge(f1_mm, b * HC + m + 1)
                        if b >= 2 and m == 0:
                            act.wait_ge(f2_mm, 4 * (b - 1))
                        act.activation(hid[:, b % 2, m, :], ps[:, 4 + m % 2, :], ACT.Gelu, bias=bias_1[:, m:m + 1]).then_inc(f1_out, 1)
            if stop >= 3:
                act.wait_ge(d_w3, 96)
                act.wait_ge(ffn_add, NT)
                for j in range(NT):
                    b, ft, u = j // 4, j % 4 // 2, j % 2
                    act.wait_ge(tp_mm, 2 * NT + j + 1)
                    act.copy(xnt4.rearrange("p c (t b s) -> p c t b s", b=B, s=32)[:, :, 8 * ft:8 * ft + 8, b, u::2],
                             ps[:, turn_bank(2, j), 0:FC * P].rearrange("p (c t s) -> p c t s", c=FC, t=8)).then_inc(tp_out, 1)
                for t in range(NT):
                    act.wait_ge(c_mm, t + 1)
                    s0 = 4 * (t % 2)
                    act.copy(kq_tok[:, :, t, :], ps[:, s0, :].rearrange("p (w n) -> p w n", w=2))
                    act.copy(v_tok[:, t, :], ps[:, s0 + 1, 0:D])
                    act.activation(gate[:, t, :], ps[:, s0 + 1, D:2 * D], ACT.Silu).then_inc(c_out, 1)
                    if t in (9, NT - 1):
                        half = t // (NT - 1)
                        tiles = slice(NT // 2 * half, NT // 2 * (half + 1))
                        act.wait_ge(ss_ok, NT // 2 * (half + 1))
                        act.activation(rnorm[:, tiles], ssum[:, tiles], ACT.Sqrt).then_inc(nrm_ok, 1)
                z, u, alpha, be = small[0], small[1], small[2], small[3]
                act.wait_ge(dve_ab, 1)
                act.activation(a_exp, a_exp, ACT.Exp).then_inc(act_ab, 1)
                act.activation(u, z, ACT.Abs).then_inc(act_ab, 1)
                act.wait_ge(act_ab, 2)
                act.activation(u, u, ACT.Exp, scale=-1.0).then_inc(act_ab, 1)
                act.activation(be, ab[:, :, NH:2 * NH], ACT.Exp, scale=-1.0).then_inc(act_ab, 1)
                for t in range(NT + 1):
                    if t < NT:
                        act.wait_ge(gt_mm, t + 1)
                        if t >= 2:
                            act.wait_ge(g_mm, t - 1)
                        for odd in range(2):
                            act.activation(kq_one[:, t % 2, odd].rearrange("p w a n -> p (w a n)"), ps[:, t % 2, :], ACT.Copy,
                                           scale=half_mask[:, odd:odd + 1])
                        act.copy(k_f[:, t % 2].rearrange("p a n -> p (a n)"), ps[:, t % 2, 0:2 * P]).then_inc(gt_out, 1)
                    if t == 1:
                        act.wait_ge(dve_ab, 2)
                        act.activation(alpha, alpha, ACT.Exp, scale=-1.0).then_inc(alpha_ok, 1)
                    if t:
                        act.wait_ge(pick_dve_ok, t)
                        if t >= 3:
                            act.wait_ge(g_out, t - 2)
                        act.activation(pick_act[:, (t - 1) % 2], half_products(1), ACT.Copy, scale=half_mask[:, 1:2]).then_inc(pick_act_ok, 1)
                act.wait_ge(gd_mm, 1)
                act.copy(gd, ps[:, 7, :].rearrange("p (a n) -> p a n", a=2)).then_inc(gd_ok, 1)
                for t in range(NT + 1):
                    if t % (NT // 2) == 0 and t < NT:
                        for n in (t // 2, t // 2 + 2):
                            take_inverse(act, n)
                    if t < NT:
                        take_uw(act, t)
                    if t == 3 * NT // 4:
                        part_keys(act, 0)
                    if t:
                        i = t - 1
                        act.wait_ge(wq_mm, i + 1)
                        for par in range(2):
                            src = ps[:, 4 + i % 2, 0:256].rearrange("p (a b x) -> p a b x", a=2, b=B)[:, :, :, DH * par:DH * par + DH]
                            ins = act.copy(wq_t5[:, i, :, par, :, DH * par:DH * par + DH], src)
                        ins.then_inc(wq_act, 1)
                part_keys(act, 1)
                for t in range(NT):
                    act.wait_ge(xo_ok[0], 2 * t + 1)
                    act.wait_ge(xo_ok[1], 2 * t + 1)
                    if t >= 2:
                        act.wait_ge(comb_ok, t - 1)
                    for w in range(2):
                        ins = act.activation(comb_a[:, t % 2, w], xo[:, 2 * t % 4, :], ACT.Copy, scale=half_mask[:, w:w + 1])
                    ins.then_inc(cb_act, 1)
                for t in range(NT):
                    act.wait_ge(o_mm, t + 1)
                    act.copy(o_tok[:, t, :], ps[:, t % 4, 0:D]).then_inc(o_out, 1)
                    if t % 8 == 7:
                        act.wait_ge(rms_ss, t // 8 + 1)
                        act.activation(small[0][:, t - 7:t + 1], small[0][:, t - 7:t + 1], ACT.Sqrt).then_inc(rms_rt, 1)
                for t in range(NT):
                    act.wait_ge(og_mm, t + 1)
                    act.copy(o_f[:, :, :, 32 * t:32 * t + 32],
                             ps[:, 6 + t % 2, 0:FC * P].rearrange("p (c b s) -> p c b s", c=FC, b=B)).then_inc(og_out, 1)
            if stop >= 4:
                for k in range(NT):
                    turn_out(3, k, out_tile(k))
                act.wait_ge(sh_ok, 1)
                act.activation(lexp, lexp, ACT.Exp).then_inc(lexp_ok, 1)

                def take_tokens(t, slot):
                    act.wait_ge(et_mm, t + 1)
                    if not (isinstance(t, int) and t < 2):
                        act.wait_ge(e1_mm, (t - 1) * HC)
                    act.copy(xst[:, slot], ps[:, 6, :].rearrange("p (c n) -> p c n", c=FC)).then_inc(et_out, 1)

                def expert(t, slot, first):
                    for m in range(HC):
                        act.wait_ge(e1_mm, t * HC + m + 1)
                        if not (first and t == 0 and m < 2):
                            act.wait_ge(e1_out, t * HC + m - 1)
                        act.activation(silu[:, m % 2], ps[:, m % 4, 0:ET], ACT.Silu).then_inc(e_silu, 1)
                    if not (isinstance(t, int) and t == NET - 1):
                        take_tokens(t + 1, 1 - slot)
                    act.wait_ge(e2_out, t + 1)
                    act.dma_start(ys_dram.rearrange("(t r p) n -> p t r n", p=P, r=2)[:, ds(t, 1)].rearrange("p o r n -> p (o r) n"),
                                  ys[:, slot]).then_inc(d_ys[slot], 16)

                take_tokens(0, 0)
                expert_tiles(act, expert)

        @block.tensor
        def _(pe):
            pe.wait_ge(d_kv, 80)
            for u in range(4):
                kh, m = divmod(u, 2)
                if u >= 2:
                    pe.wait_ge(pj_out, u - 1)
                for c in range(FC):
                    mm = pe.matmul(ps[:, 4 + u % 2, :], wk_t[:, c, m * P:(m + 1) * P], keys_t[:, c, kh * S:(kh + 1) * S],
                                   start=(c == 0), stop=(c == FC - 1))
                mm.then_inc(pj_mm, 1)
            for kc in range(KC):
                if kc >= 2:
                    pe.wait_ge(v_out, kc - 1)
                for c in range(FC):
                    mm = pe.matmul(ps[:, 6 + kc % 2, 0:D], vals_t[:, c, kc * P:(kc + 1) * P], wv_t[:, c, :],
                                   start=(c == 0), stop=(c == FC - 1))
                mm.then_inc(v_mm, 1)

            def turn(stage, k, j=None):
                n, j = stage * NT + k, k if j is None else j
                pe.wait_ge(ln_out, n + 1)
                if n >= 2:
                    pe.wait_ge(tp_out, n - 1)
                for c in range(FC):
                    mm = pe.transpose(ps[:, turn_bank(stage, k), c * P:(c + 1) * P], xn[:, j, c * P:(c + 1) * P], ident[:, :])
                mm.then_inc(tp_mm, 1)

            pe.wait_ge(ident_ok, 1)
            for b in range(B + 1):
                if b < B:
                    pe.wait_ge(d_x[b], 16)
                    for j in range(4 * b, 4 * b + 4):
                        if j >= 2:
                            pe.wait_ge(tok_out, j - 1)
                        for c in range(8):
                            if b == 0 and j == 0:
                                pe.wait_ge(wtok_ok, c + 1)
                            mm = pe.matmul(ps[:, j % 2, 0:D], x_t[b][:, c, (j % 4) * P:(j % 4 + 1) * P], w_tok[:, c, :],
                                           start=(c == 0), stop=(c == 7))
                        mm.then_inc(mm_tok, 1)
                if b >= 1:
                    for j in range(4 * b - 4, 4 * b):
                        turn(0, j)
                    pe.wait_ge(tp_out, 4 * b)
                    for m in range(2):
                        u = 4 + 2 * (b - 1) + m
                        pe.wait_ge(pj_out, u - 1)
                        for c in range(FC):
                            mm = pe.matmul(ps[:, 4 + u % 2, :], wq_t[:, c, m * P:(m + 1) * P],
                                           xnt[:, c, (b - 1) * S:b * S], start=(c == 0), stop=(c == FC - 1))
                        mm.then_inc(pj_mm, 1)

            def unit(q, kc, n, slot, nmax, mslot, before):
                def for_maxima(g, half):
                    if nmax is not None:
                        h, part_of = divmod(8 * q + kc, 2)
                        qt = 2 * part_of + g
                        if nmax or g:
                            pe.wait_ge(max_out, 4 * nmax + 2 * g + half - 1)
                        pe.matmul(ps[:, 4 + half, :], qstk[0:NPART, mslot, h, qt * P:(qt + 1) * P],
                                  kstk[0:NPART, h, half * S:(half + 1) * S], start=True, stop=True).then_inc(sm_mm, 1)

                for g in range(2):
                    for_maxima(g, 0)
                    if n is not None:
                        if n:
                            pe.wait_ge(exp_out, 2 * n + g - 1)
                        for i in range(2):
                            h = 4 * q + 2 * g + i
                            mm = pe.matmul(ps[:, 2 * g + i, :], kstk[:, h, kc * P:(kc + 1) * P], qstk[:, slot, h, :],
                                           start=True, stop=True)
                        mm.then_inc(st_mm, 1)
                    for_maxima(g, 1)
                    if g == 0 and before is not None:
                        attend(before)

            def attend(n):
                m, kc = divmod(n, KC)
                pe.wait_ge(exp_out, 2 * n + 2)
                if kc == 0 and m:
                    pe.wait_ge(av_out, m)
                for c in range(4):
                    mm = pe.matmul(ps[32 * c:32 * c + 32, 6, :], vaug[:, kc, 4 * (m % 4) + c, :], prob[:, n % 2, c, :],
                                   start=(kc == 0), stop=(kc == KC - 1), skip_group_check=True)
                mm.then_inc(av_mm, 1)

            def spread_sums(m):
                pe.wait_ge(av_out, m + 1)
                if m >= 2 and m % 2 == 0:
                    pe.wait_ge(at_add, m // 2)
                if m == 0:
                    pe.wait_ge(mx_row, 1)
                elif m % 4 == 3 and m // 4 + 1 < B:
                    pe.wait_ge(mx_row, m // 4 + 2)
                if m % 2:
                    pe.wait_ge(rd_ok, m)
                pe.matmul(ps[:, 7, :], spread, att[:, m % 2], start=True, stop=True).then_inc(sum_mm, 1)

            def compact(m):
                pe.wait_ge(att_ok, m + 1)
                for i in range(2):
                    mm = pe.matmul(ps[:, 7, :], gather[:, i], att[:, i], start=(i == 0), stop=(i == 1))
                mm.then_inc(at_mm, 2)

            def weight_sums(i):
                pe.wait_ge(abs_ok, i + 1)
                if i:
                    pe.wait_ge(mean_ok, i)
                if i == 0:
                    for half in range(2):
                        for c in range(FC):
                            mm = pe.matmul(ps[:, 6 + half, :], ones[:, :], w_abs[:, c * HID + half * S:c * HID + (half + 1) * S],
                                           start=(c == 0), stop=(c == FC - 1))
                else:
                    for c in range(HC):
                        mm = pe.matmul(ps[:, 6, 0:D], ones[:, :], w_abs[:, c * D:(c + 1) * D], start=(c == 0), stop=(c == HC - 1))
                mm.then_inc(mean_mm, 1)

            pe.wait_ge(consts, 5)
            pe.wait_ge(d_kstk, 96)
            pe.wait_ge(sel_ok, 1)
            pe.wait_ge(v_out, KC)
            pe.wait_ge(pj_out, NU)
            for b in range(-1, B):
                if b + 1 < B:
                    pe.wait_ge(d_qstk[b + 1], 96)
                if b >= 0:
                    pe.wait_ge(d_mrow, 16 * (b + 1))
                for q in range(4):
                    for kc in range(KC):
                        n = 32 * b + 8 * q + kc
                        unit(q, kc, n if b >= 0 else None, b % 2, n + 32 if b + 1 < B else None, (b + 1) % 2,
                             n - 1 if b >= 0 and n > 32 * b else None)
                        if b < 0 and (q, kc) in ((1, 4), (3, 4)):
                            weight_sums(q // 2)
                        if b >= 0 and kc == 3 and q:
                            spread_sums(4 * b + q - 1)
                        if b >= 0 and kc == 6 and q == 2:
                            compact(4 * b + 1)
                if b >= 0:
                    attend(32 * b + 31)
                if b + 1 < B:
                    pe.wait_ge(mx_pad, b + 2)
                    if b < 0:
                        pe.wait_ge(mean_ok, 2)
                    else:
                        pe.wait_ge(rd_ok, 4 * b + 3)
                    for qt in range(QT):
                        mm = pe.transpose(ps[:, 7, qt * (P // 2):(qt + 1) * (P // 2)].bitcast(BF16), mpad[:, qt, :], ident_b[:, :])
                    mm.then_inc(mx_mm, 1)
                if b >= 0:
                    spread_sums(4 * b + 3)
                    compact(4 * b + 3)

            if stop >= 2:
                pe.wait_ge(w_ok, 2)
                pe.wait_ge(at_add, 2 * B)
                pe.wait_ge(exp_out, 256)

                def hidden(b):
                    for m in range(HC):
                        n = b * HC + m
                        if n >= 2:
                            pe.wait_ge(f1_out, n - 1)
                        for c in range(FC):
                            mm = pe.matmul(ps[:, 4 + m % 2, :], w1[:, c, m * P:(m + 1) * P], xnt[:, c, b * S:(b + 1) * S],
                                           start=(c == 0), stop=(c == FC - 1))
                        mm.then_inc(f1_mm, 1)

                def ffn_out(b):
                    pe.wait_ge(f1_out, HC * (b + 1))
                    for i in range(4):
                        j = 4 * b + i
                        if j >= 2:
                            pe.wait_ge(f2_out, j - 1)
                        for m in range(HC):
                            mm = pe.matmul(ps[:, 6 + j % 2, 0:D], hid[:, b % 2, m, i * P:(i + 1) * P], w2[:, m, :],
                                           start=(m == 0), stop=(m == HC - 1))
                        mm.then_inc(f2_mm, 1)

                for b in range(B + 1):
                    if b < B:
                        for j in range(4 * b, 4 * b + 4):
                            turn(1, j)
                        pe.wait_ge(tp_out, NT + 4 * b + 4)
                        hidden(b)
                    if b:
                        ffn_out(b - 1)
            if stop >= 3:
                pe.wait_ge(d_w3, 96)
                pe.wait_ge(f2_out, NT)
                for j in range(NT):
                    turn(2, j)
                pe.wait_ge(tp_out, 3 * NT)
                for t in range(NT):
                    if t >= 2:
                        pe.wait_ge(c_out, t - 1)
                        pe.wait_ge(c_ab, t - 1)
                    s0 = 4 * (t % 2)
                    for i, (lo, n) in enumerate(((0, 512), (512, 512), (1024, 2 * NH))):
                        for c in range(FC):
                            mm = pe.matmul(ps[:, s0 + i, 0:n], xnt4[:, c, t * P:(t + 1) * P], w_cat[:, c, lo:lo + n],
                                           start=(c == 0), stop=(c == FC - 1))
                    mm.then_inc(c_mm, 1)
                pe.wait_ge(c_out, NT)
                pe.wait_ge(c_ab, NT)
                for t in range(NT + 1):
                    if t == 2:
                        pe.wait_ge(alpha_ok, 1)
                        for i, (v, half) in enumerate(((2, 0), (2, 1), (5, 0), (5, 1))):
                            mm = pe.transpose(ps[:, 6, i * P:(i + 1) * P], small[v][:, 8 * half:8 * half + 8, :].rearrange("p t h -> p (t h)"), ident[:, :])
                        mm.then_inc(su_mm, 1)
                    if t < NT:
                        pe.wait_ge(kq_ok, t + 1)
                        if t >= 2:
                            pe.wait_ge(gt_out, t - 1)
                        for w in range(2):
                            for hh in range(2):
                                mm = pe.transpose(ps[:, t % 2, (2 * w + hh) * P:(2 * w + hh + 1) * P],
                                                  kq_tok[:, w, t, hh * P:(hh + 1) * P], ident[:, :])
                        mm.then_inc(gt_mm, 1)
                    if t:
                        i = t - 1
                        pe.wait_ge(gt_out, i + 1)
                        if i:
                            pe.wait_ge(pick_act_ok, i)
                        for hh in range(2):
                            for r in range(4):
                                for b in range(B):
                                    rows = slice(32 * r, 32 * r + 32)
                                    mm = pe.matmul(ps[32 * b:32 * b + 32, 2 + r, 128 * hh:128 * hh + 128],
                                                   k_f[rows, i % 2, hh, 32 * b:32 * b + 32],
                                                   kq_one[rows, i % 2, :, :, hh, 32 * b:32 * b + 32].rearrange("p o w i -> p (o w) i"),
                                                   start=True, stop=True, skip_group_check=True)
                        mm.then_inc(g_mm, 1)
                pe.wait_ge(du_ok, 1)
                for half in range(2):
                    pe.transpose(ps[:, 7, half * P:(half + 1) * P], gam_u[:, 8 * half:8 * half + 8, :].rearrange("p u i -> p (u i)"), ident[:, :])
                    mm = pe.transpose(ps[:, 7, (2 + half) * P:(3 + half) * P], decay[:, DH - 1, 8 * half:8 * half + 8, :].rearrange("p u i -> p (u i)"), ident[:, :])
                mm.then_inc(gd_mm, 1)

                def by_half(v):
                    return v[:, 0:128], v[:, 128:256]

                def turn_rows(src, n, bank):
                    ig = n % 4
                    for i in range(4):
                        mm = pe.transpose(ps[:, bank, i * P:(i + 1) * P], src[n // 4][:, :, 4 * ig + i], ident[:, :])
                    return mm

                for n in range(8):
                    if n >= 2:
                        pe.wait_ge(dt_out, n - 1)
                    turn_rows(by_half(decay.rearrange("p i u j -> p (u j) i")), n, n % 2).then_inc(dt_mm, 1)
                pe.wait_ge(g_out, NT)
                for n in range(8):
                    if n >= 2:
                        pe.wait_ge(gu_out, n - 1)
                    turn_rows(by_half(gp[:, :, :, 0].rearrange("p t h i -> p (t h) i")), n, 2 + n % 2).then_inc(gu_mm, 1)

                def turn_inverse(half):
                    pe.wait_ge(gk_ok, half + 1)
                    for n in range(4 * half, 4 * half + 4):
                        if n % 4 >= 2:
                            pe.wait_ge(tt_out[n % 2], n // 2)
                        turn_rows([t_u[:, i].rearrange("p i u j -> p (u j) i") for i in range(2)], n, 4 + n % 2).then_inc(tt_mm, 1)
                    for i in range(2):
                        pe.wait_ge(tt_out[i], 2 * half + 2)

                turn_inverse(0)
                pe.wait_ge(gm_ok, 1)
                pe.wait_ge(gd_ok, 1)
                for hh in range(2):
                    mm = pe.matmul(ps[:, 6, hh * P:(hh + 1) * P], head_sel[:, hh, :], gam_m.rearrange("p c u -> p (c u)"), start=True, stop=True)
                mm.then_inc(gf_mm, 1)
                pe.wait_ge(gf_ok, 1)
                pe.wait_ge(vb_ok, 1)
                pe.wait_ge(qg_ok, 1)
                for t in range(NT + 1):
                    if t == NT // 2:
                        pe.wait_ge(wq_act, t - 1)
                        turn_inverse(1)
                    if t < NT:
                        if t >= 2:
                            pe.wait_ge(uw_out[0], t - 1)
                            pe.wait_ge(uw_out[1], t - 1)
                        for h in range(NH):
                            for b in range(B):
                                mm = pe.matmul(ps[32 * b:32 * b + 32, 2 * (t % 2) + h // 8, 32 * (h % 8):32 * (h % 8) + 32],
                                               t_blk[32 * b:32 * b + 32, NH * t + h].rearrange("p a i -> p (a i)"),
                                               vgk[32 * b:32 * b + 32, :, D * t + DH * h:D * t + DH * h + DH], start=True, stop=True,
                                               skip_group_check=True)
                        mm.then_inc(uw_mm, 1)
                    if t:
                        i = t - 1
                        pe.wait_ge(uw_out[0], i + 1)
                        pe.wait_ge(uw_out[1], i + 1)
                        if i >= 2:
                            pe.wait_ge(wq_act, i - 1)
                            pe.wait_ge(wq_dve, i - 1)
                        for hh in range(2):
                            pe.transpose(ps[:, 4 + i % 2, hh * P:(hh + 1) * P], w_neg[:, i % 2, hh * P:(hh + 1) * P], ident[:, :])
                            mm = pe.transpose(ps[:, 6 + i % 2, hh * P:(hh + 1) * P], kq_tok[:, 1, i, hh * P:(hh + 1) * P], ident[:, :])
                        mm.then_inc(wq_mm, 1)
                pe.wait_ge(wq_act, NT)
                pe.wait_ge(wq_dve, NT)

                def halves(v):
                    return v.rearrange("p (a e x) -> p a e x", a=2, e=2)

                for n in range(2 * NT):
                    t, par = divmod(n, 2)
                    for g in range(2):
                        pe.wait_ge(s_ok[g], n + 1)
                        for r in range(4):
                            for hh in range(2):
                                for b in (2 * g, 2 * g + 1):
                                    mm = pe.matmul(ps[32 * b:32 * b + 32, r, 32 * hh:32 * hh + 32],
                                                   wq_t5[32 * r:32 * r + 32, t, hh, par, b, :], state[32 * r:32 * r + 32, b, :, hh, :],
                                                   start=True, stop=True, skip_group_check=True)
                        mm.then_inc(r_mm[g], 1)
                    for g in range(2) if n < 2 * NT - 1 else ():
                        pe.wait_ge(xo_ok[g], n + 1)
                        if par == 0 and t % (NT // 2) == 0 and g == 0:
                            pe.wait_ge(kt_ok[t // (NT // 2)], 2)
                        for r in range(4):
                            for hh in range(2):
                                for b in (2 * g, 2 * g + 1):
                                    f, x = P * hh + 32 * r, 64 * r + 32 * hh
                                    mm = pe.matmul(halves(ps[32 * r:32 * r + 32, 4 + b, 0:64])[:, :, hh, :],
                                                   (k_even, k_odd)[par][32 * b:32 * b + 32, t, f:f + 32],
                                                   xo[32 * b:32 * b + 32, n % 4, x:x + 32].rearrange("p (a x) -> p a x", a=2),
                                                   start=True, stop=True, skip_group_check=True)
                        mm.then_inc(s_mm[g], 1)
                pe.wait_ge(xo_ok[0], 2 * NT)
                pe.wait_ge(xo_ok[1], 2 * NT)
                for t in range(NT):
                    pe.wait_ge(comb_ok, t + 1)
                    if t >= 4:
                        pe.wait_ge(o_out, t - 3)
                    for b in range(B):
                        r = slice(32 * b, 32 * b + 32)
                        pe.matmul(ps[r, t % 4, 0:D], swap[r, r], comb_qs[r, t, :].rearrange("p (r e x) -> p e r x", r=4, e=2),
                                  start=True, stop=False, skip_group_check=True)
                    for h in range(NH):
                        x = 64 * (h % 8 // 2) + 32 * (h // 8) + DH * (h % 2)
                        for b in range(B):
                            r = slice(32 * b, 32 * b + 32)
                            mm = pe.matmul(ps[r, t % 4, DH * h:DH * h + DH], p_blk[r, NH * t + h].rearrange("p a i -> p (a i)"),
                                           u_tok[r, t, x:x + DH], start=False, stop=True, skip_group_check=True)
                    mm.then_inc(o_mm, 1)

                def route(k):
                    if k < NT:
                        turn(3, k, out_tile(k))
                    if k == 0:
                        pe.wait_ge(d_rt, 96)
                        return
                    pe.wait_ge(tp_out, 3 * NT + k)
                    j = out_tile(k - 1)
                    for c in range(FC):
                        mm = pe.matmul(ps[:, 0, j * NE:(j + 1) * NE], xnt[:, c, j * P:(j + 1) * P], rw[:, c, :],
                                       start=(c == 0), stop=(c == FC - 1))
                    return mm

                for t in range(NT):
                    pe.wait_ge(og_ok, t + 1)
                    if t >= 2:
                        pe.wait_ge(og_out, t - 1)
                    for c in range(FC):
                        mm = pe.transpose(ps[:, 6 + t % 2, c * P:(c + 1) * P], o_tok[:, t, c * P:(c + 1) * P], ident[:, :])
                    mm.then_inc(og_mm, 1)
                    for n in range(8 * (t // 8), 8 * (t // 8) + 8) if t % 8 == 7 else ():
                        if n % 8 == 0:
                            pe.wait_ge(og_out, t + 1)
                        j = out_tile(n)
                        b, ft, u = j // 4, j % 4 // 2, j % 2
                        if n >= 3:
                            pe.wait_ge(attn_add, n - 2)
                        for c in range(FC):
                            mm = pe.matmul(ps[:, wo_bank(n), 0:D], o_f[:, c, b, D * ft + u:D * ft + D:2], w_out[:, c, :],
                                           start=(c == 0), stop=(c == FC - 1))
                        mm.then_inc(wo_mm, 1)
                        if n >= NT // 2:
                            route(n - NT // 2)
            if stop >= 4:
                for k in range(NT // 2, NT + 1):
                    mm = route(k)
                mm.then_inc(lg_mm, 1)
                pe.wait_ge(hot_ok, 1)
                hot = onehot.rearrange("p j e -> p (j e)")
                pe.matmul(ps[:, 1, 0:NT * NE], tri, hot, start=True, stop=True)
                pe.matmul(ps[:, 2, 0:NT * NE], ones[:, :], hot, start=True, stop=True).then_inc(cnt_mm, 1)
                pe.wait_ge(pos_ok, 1)

                def turn_tokens(t, slot, first):
                    pe.wait_ge(d_ew[slot], (t // 2 + 1) * 48 if isinstance(t, int) else t * 24 + (48 if slot == 0 else 24))
                    if not (first and t == 0):
                        pe.wait_ge(et_out, t)
                    for c in range(FC):
                        for r in range(2):
                            mm = pe.transpose(ps[:, 6, c * ET + r * P:c * ET + (r + 1) * P], xs[:, slot, r, c * P:(c + 1) * P], ident[:, :])
                    mm.then_inc(et_mm, 1)

                def expert(t, slot, first):
                    pe.wait_ge(et_out, t + 1)
                    for m in range(HC):
                        if not (first and t == 0 and m < 4):
                            pe.wait_ge(e1_out, t * HC + m - 3)
                        for half in range(2):
                            for c in range(FC):
                                mm = pe.matmul(ps[:, m % 4, half * ET:(half + 1) * ET],
                                               ew1[:, slot, c, half * HID + m * P:half * HID + (m + 1) * P], xst[:, slot, c, :],
                                               start=(c == 0), stop=(c == FC - 1))
                        mm.then_inc(e1_mm, 1)
                    if not (isinstance(t, int) and t == NET - 1):
                        turn_tokens(t + 1, 1 - slot, first)
                    if not (first and t == 0):
                        pe.wait_ge(e2_out, t)
                    for r in range(2):
                        for m in range(HC):
                            if r == 0:
                                pe.wait_ge(e1_out, t * HC + m + 1)
                            mm = pe.matmul(ps[:, 4 + r, 0:D], eu[:, slot, m, r * P:(r + 1) * P], ew2[:, slot, m, :],
                                           start=(m == 0), stop=(m == HC - 1))
                    mm.then_inc(e2_mm, 1)

                turn_tokens(0, 0, True)
                expert_tiles(pe, expert)

        @block.vector
        def _(dve):
            steps = [0]

            def step(ins):
                steps[0] += 1
                ins.then_inc(dve_step, 1)
                dve.wait_ge(dve_step, steps[0])

            dve.wait_ge(ident_ok, 1)
            dve.tensor_copy(ident_b[:, :], ident[:, :])
            dve.wait_ge(d_small, 64)
            for c in range(8):
                d, ic = divmod(c, FC)
                dve.tensor_tensor(w_tok[:, c, :], ws_t[:, ic, :], w_bc[:, d, :], ALU.mult).then_inc(wtok_ok, 1)
            step(dve.memset(vaug[:, :, :, DH:32], 0.0))
            dve.memset(vaug[:, :, :, DH:DH + 1], 1.0)

            def split(u):
                dve.wait_ge(pj_out, u + 1)
                if u >= 2:
                    dve.wait_ge(d_part[u % 2], 16 * (u // 2))
                f = proj[:, u % 2]
                step(dve.tensor_copy(part[:, u % 2, 0], f))
                step(dve.tensor_tensor(f, f, part[:, u % 2, 0], ALU.subtract))
                step(dve.tensor_copy(part[:, u % 2, 1], f))
                step(dve.tensor_tensor(f, f, part[:, u % 2, 1], ALU.subtract))
                dve.tensor_copy(part[:, u % 2, 2], f).then_inc(pj_split, 1)

            split(0)
            split(1)
            for kc in range(KC):
                dve.wait_ge(v_mm, kc + 1)
                dve.tensor_tensor(vtmp[:, kc % 2], ps[:, 6 + kc % 2, 0:D], bias_v, ALU.add).then_inc(v_out, 1)
                dve.wait_ge(v_out, kc + 1)
                dve.tensor_scalar(vaug[:, kc, :, 0:DH], vtmp[:, kc % 2].rearrange("p (h d) -> p h d", h=NH), 0.0, None,
                                  ALU.max)

            split(2)
            split(3)

            def ln_stats(j):
                step(dve.bn_stats(bn[:, j % 2, :], h_res[:, j, :]))
                step(dve.bn_aggr(mv[:, j, :], bn[:, j % 2, :]))
                dve.tensor_scalar(var_eps[:, j:j + 1], mv[:, j, 1:2], LN_EPS, None, ALU.add).then_inc(ln_var, 1)

            def ln_apply(stage, k, j=None):
                j = k if j is None else j
                dve.wait_ge(ln_rstd, stage * NT + k + 1)
                dve.tensor_scalar(xn[:, j, :], h_res[:, j, :], mv[:, j, 0:1], rstd[:, j:j + 1], ALU.subtract,
                                  ALU.mult).then_inc(ln_out, 1)

            for b in range(B + 1):
                if b < B:
                    for j in range(4 * b, 4 * b + 4):
                        dve.wait_ge(mm_tok, j + 1)
                        dve.tensor_copy(h_res[:, j, :], ps[:, j % 2, 0:D]).then_inc(tok_out, 1)
                        dve.wait_ge(tok_out, j + 1)
                        ln_stats(j)
                        if j >= 1:
                            ln_apply(0, j - 1)
                else:
                    ln_apply(0, NT - 1)
                if b >= 2:
                    for m in range(2):
                        split(4 + 2 * (b - 2) + m)
            for m in range(2):
                split(4 + 2 * (B - 1) + m)
            dve.wait_ge(mm_tok, NT)
            dve.wait_ge(ln_out, NT)
            step(dve.tensor_tensor(h_res[:, :, :], h_res[:, :, :], xn[:, :, :], ALU.add))
            step(dve.memset(mpad, 0.0))

            def inverse_sums(m, qt):
                if qt == 0:
                    dve.wait_ge(sum_mm, m + 1)
                    if m:
                        dve.wait_ge(att_ok, m)
                ins = dve.reciprocal(rden[:, qt * P:(qt + 1) * P], ps[:, 7, qt * P:(qt + 1) * P])
                if qt == QT - 1:
                    ins.then_inc(rd_ok, 1)

            def maxima(h, nmax, m):
                for qt in range(QT):
                    for half in range(2):
                        dve.wait_ge(sm_mm, 8 * nmax + 2 * qt + half + 1)
                        dve.tensor_reduce(mx[:, half, qt, ds(h, 1)], ps[:, 4 + half, :], AX.X, ALU.max).then_inc(max_out, 1)
                    if m is not None:
                        inverse_sums(m, qt)

            def normalise(m, slot, inverted):
                for qt in range(QT) if not inverted else ():
                    inverse_sums(m, qt)
                dve.wait_ge(rd_ok, m + 1)
                dve.tensor_tensor(att[:, slot], att[:, slot], rden, ALU.mult).then_inc(att_ok, 1)

            def add_attention(b, c):
                dve.wait_ge(at_mm, 4 * b + 2 * c + 2)
                row = h_res[:, 4 * b + 2 * c:4 * b + 2 * c + 2, :].rearrange("p f (s u) -> p f u s", u=2)
                dve.tensor_tensor(row, ps[:, 7, :].rearrange("p (f u s) -> p f u s", f=2, u=2), row, ALU.add
                                  ).then_inc(at_add, 1)

            dve.wait_ge(consts, 5)
            for b in range(-1, B):
                for q in range(4):
                    for i in range(4):
                        last_quad = 4 * b + q - 1 if b >= 0 and q and i == 2 else None
                        if b + 1 < B:
                            maxima(4 * q + i, (b + 1) * NH + 4 * q + i, last_quad)
                        if last_quad is not None:
                            normalise(last_quad, (q - 1) % 2, b + 1 < B)
                        if b >= 0 and q == 2 and i == 3:
                            add_attention(b, 0)
                        if b == B - 1 and q < 3:
                            j = 4 * q + i
                            dve.wait_ge(at_add, 2 * b)
                            ln_stats(j)
                            if j:
                                ln_apply(1, j - 1)
                if b + 1 < B:
                    dve.wait_ge(max_out, 8 * NH * (b + 2))
                    step(dve.tensor_tensor(mx1, mx[:, 0], mx[:, 1], ALU.max))
                    if b >= 0:
                        dve.wait_ge(mx_mm, b + 1)
                    step(dve.tensor_copy(mpad[:, :, NPART:NPART + NH], mx1))
                    step(dve.tensor_tensor(mlo, mx1, mpad[:, :, NPART:NPART + NH], ALU.subtract))
                    dve.tensor_copy(mpad[:, :, NPART + NH:P], mlo).then_inc(mx_pad, 1)
                if b >= 0:
                    normalise(4 * b + 3, 1, False)
                    add_attention(b, 1)
                    dve.wait_ge(at_add, 2 * b + 2)

            if stop >= 2:
                for j in range(NT - 4, NT + 1):
                    if j < NT:
                        ln_stats(j)
                    ln_apply(1, j - 1)
                for j in range(NT):
                    dve.wait_ge(f2_mm, j + 1)
                    if j >= 2:
                        dve.wait_ge(ffn_add, j - 1)
                    dve.tensor_tensor(ffn_sum[:, j % 2], ps[:, 6 + j % 2, 0:D], bias_2, ALU.add).then_inc(f2_out, 1)
                    dve.wait_ge(f2_out, j + 1)
                    dve.tensor_tensor(h_res[:, j, :], h_res[:, j, :], ffn_sum[:, j % 2], ALU.add).then_inc(ffn_add, 1)
                    dve.wait_ge(ffn_add, j + 1)
                    ln_stats(j)
                    if j:
                        ln_apply(2, j - 1)
                ln_apply(2, NT - 1)
            if stop >= 3:

                def inverse_norms(half):
                    tiles = slice(NT // 2 * half, NT // 2 * (half + 1))
                    dve.wait_ge(nrm_ok, half + 1)
                    step(dve.tensor_scalar(rnorm[:, tiles], rnorm[:, tiles], 1e-12, None, ALU.max))
                    step(dve.reciprocal(ssum[:, tiles], rnorm[:, tiles]))
                    step(dve.tensor_scalar(ssum[:, tiles, NH:], ssum[:, tiles, NH:], DH ** -0.5, None, ALU.mult))

                def unit_length(t):
                    for w in range(2):
                        kq = kq_tok[:, w, t, :].rearrange("p (h d) -> p h d", d=DH)
                        ins = dve.tensor_tensor(kq, kq, ssum[:, t, w * NH:(w + 1) * NH].unsqueeze(2).broadcast_to([P, NH, DH]), ALU.mult)
                    ins.then_inc(kq_ok, 1)

                for t in range(NT):
                    dve.wait_ge(c_out, t + 1)
                    dve.tensor_copy(ab[:, t, :], ps[:, 4 * (t % 2) + 2, 0:2 * NH]).then_inc(c_ab, 1)
                    step(dve.tensor_tensor(sq.rearrange("p (w n) -> p w n", w=2), kq_tok[:, :, t, :], kq_tok[:, :, t, :], ALU.mult))
                    dve.tensor_reduce(ssum[:, t, :], sq.rearrange("p (h d) -> p h d", d=DH), AX.X, ALU.add).then_inc(ss_ok, 1)
                    dve.wait_ge(ss_ok, t + 1)
                    if t == 11:
                        inverse_norms(0)
                    if t >= 12:
                        unit_length(t - 12)
                z, u, alpha, be, gb, beta, s2, q1 = small
                s1 = be
                dve.wait_ge(d_w3, 96)
                dve.wait_ge(c_ab, NT)
                dve.tensor_tensor(z, ab[:, :, 0:NH], dt_bias.unsqueeze(1).broadcast_to([P, NT, NH]), ALU.add).then_inc(dve_ab, 1)
                dve.wait_ge(act_ab, 4)
                step(dve.tensor_scalar(be, be, 1.0, None, ALU.add))
                step(dve.reciprocal(beta, be))
                step(dve.tensor_scalar(s1, u, 2.0, None, ALU.add))
                step(dve.reciprocal(s2, s1))
                step(dve.tensor_tensor(s1, u, s2, ALU.mult))
                step(dve.tensor_tensor(s2, s1, s1, ALU.mult))
                step(dve.tensor_scalar(q1, s2, 1.0 / 15, None, ALU.mult))
                for m in (13, 11, 9, 7, 5, 3):
                    step(dve.scalar_tensor_tensor(out=q1, in0=q1, scalar=1.0 / m, in1=s2, op0=ALU.add, op1=ALU.mult))
                step(dve.scalar_tensor_tensor(out=q1, in0=q1, scalar=1.0, in1=s1, op0=ALU.add, op1=ALU.mult))
                step(dve.tensor_scalar(z, z, 0.0, None, ALU.max))
                step(dve.scalar_tensor_tensor(out=z, in0=q1, scalar=2.0, in1=z, op0=ALU.mult, op1=ALU.add))
                dve.tensor_tensor(alpha, z, a_exp.unsqueeze(1).broadcast_to([P, NT, NH]), ALU.mult).then_inc(dve_ab, 1)

                def pick(t):
                    dve.wait_ge(g_mm, t + 1)
                    dve.tensor_scalar(pick_dve, half_products(0), half_mask[:, 0:1], None, ALU.mult).then_inc(pick_dve_ok, 1)
                    dve.wait_ge(pick_dve_ok, t + 1)
                    dve.wait_ge(pick_act_ok, t + 1)
                    for hh in range(2):
                        ins = dve.tensor_tensor(gp[:, t, 8 * hh:8 * hh + 8].rearrange("p (r o) w i -> p r (o w i)", o=2),
                                                pick_dve[:, :, 4 * hh:4 * hh + 4].rearrange("p r e i -> p r (e i)"),
                                                pick_act[:, t % 2, :, 4 * hh:4 * hh + 4].rearrange("p r e i -> p r (e i)"), ALU.add)
                    ins.then_inc(g_out, 1)
                    dve.wait_ge(g_out, t + 1)


                def decay_row(i):
                    step(dve.tensor_tensor(decay[:, i, :, 0:i], decay[:, i - 1, :, 0:i], ab_u[:, 0, :, i:i + 1].broadcast_to([P, 16, i]), ALU.mult))

                for t in range(NT):
                    pick(t)
                    if t == 2:
                        inverse_norms(1)
                    if t + 4 < NT:
                        unit_length(t + 4)
                    if t == 1:
                        dve.wait_ge(su_mm, 1)
                        step(dve.tensor_copy(ab_u, ps[:, 6, :].rearrange("p (a u t) -> p a u t", a=2, u=16)))
                        step(dve.tensor_copy(decay, eye16.rearrange("p (i j) -> p i j", i=DH).unsqueeze(2).broadcast_to([P, DH, 16, DH])))
                    if t >= 2:
                        decay_row(t - 1)
                decay_row(DH - 1)
                dve.tensor_tensor(gam_u, decay[:, :, :, 0].rearrange("p i u -> p u i"), ab_u[:, 0, :, 0:1].broadcast_to([P, 16, DH]), ALU.mult
                                  ).then_inc(du_ok, 1)
                dve.wait_ge(du_ok, 1)
                for n in range(8):
                    half, ig = divmod(n, 4)
                    dve.wait_ge(dt_mm, n + 1)
                    for par in range(2):
                        ins = dve.scalar_tensor_tensor(
                            out=p_blk[:, 128 * half:128 * half + 128, par, 4 * ig:4 * ig + 4],
                            in0=ps[:, n % 2, :].rearrange("p (i c) -> p c i", i=4), scalar=half_mask[:, par:par + 1],
                            in1=gp[:, :, :, 1].rearrange("p t h i -> p (t h) i")[:, 128 * half:128 * half + 128, 4 * ig:4 * ig + 4],
                            op0=ALU.mult, op1=ALU.mult)
                    ins.then_inc(dt_out, 1)
                dve.wait_ge(dt_out, 8)
                for n in range(8):
                    half, ig = divmod(n, 4)
                    dve.wait_ge(gu_mm, n + 1)
                    d = decay.rearrange("p i u j -> p i (u j)")[:, 4 * ig:4 * ig + 4, 128 * half:128 * half + 128]
                    dve.scalar_tensor_tensor(out=a_u.rearrange("p i u j -> p i (u j)")[:, 4 * ig:4 * ig + 4, 128 * half:128 * half + 128],
                                             in0=ps[:, 2 + n % 2, :].rearrange("p (i c) -> p i c", i=4), scalar=-1.0, in1=d,
                                             op0=ALU.mult, op1=ALU.mult).then_inc(gu_out, 1)
                dve.wait_ge(gu_out, 8)
                for i in range(1, DH):
                    ins = dve.tensor_tensor(a_u[:, i], a_u[:, i], ab_u[:, 1, :, i:i + 1].broadcast_to([P, 16, DH]), ALU.mult)
                step(ins)
                for half in range(2):
                    step(dve.tensor_copy(t_u[:, half], eye16.rearrange("p (i j) -> p i j", i=DH).unsqueeze(2).broadcast_to([P, DH, 8, DH])))

                def inverse_row(half, i):
                    pr = t_prod[half][:, 0:8 * i * i].rearrange("p (u c j) -> p u c j", u=8, c=i)
                    step(dve.tensor_tensor(pr, a_u[:, i, 8 * half:8 * half + 8, 0:i].unsqueeze(2).broadcast_to([P, 8, i, i]),
                                           t_u[:, half, 0:i, :, 0:i].rearrange("p j u c -> p u c j"), ALU.mult))
                    step(dve.tensor_reduce(t_u[:, half, i, :, 0:i], pr, AX.X, ALU.add))

                def decayed_keys(half):
                    rows = slice(NT * NH // 2 * half, NT * NH // 2 * (half + 1))
                    dve.tensor_tensor(gk[:, rows], kq_tok[:, 0].rearrange("p t (h d) -> p (t h) d", d=DH)[:, rows],
                                      gb.rearrange("p t h -> p (t h)")[:, rows].unsqueeze(2).broadcast_to([P, NT * NH // 2, DH]), ALU.mult
                                      ).then_inc(gk_ok, 1)

                for i in range(1, DH):
                    inverse_row(0, i)
                dve.wait_ge(gd_ok, 1)
                step(dve.tensor_tensor(gb.rearrange("p t h -> p (t h)"), gd[:, 0], beta.rearrange("p t h -> p (t h)"), ALU.mult))
                decayed_keys(0)
                dve.tensor_tensor(gam_m, gam_u[:, :, DH - 1].unsqueeze(1).broadcast_to([P, 8, 16]),
                                  tile_mask.unsqueeze(2).broadcast_to([P, 8, 16]), ALU.mult).then_inc(gm_ok, 1)
                dve.memset(state, 0.0).then_inc(s_ok[0], 1)
                dve.wait_ge(s_ok[0], 1)
                dve.engine_nop().then_inc(s_ok[1], 1)
                for n in (1, 3):
                    take_inverse(dve, n)
                dve.wait_ge(gf_mm, 1)
                dve.tensor_copy(gf, ps[:, 6, 0:256].rearrange("p (a c u) -> p a c u", a=2, c=8)).then_inc(gf_ok, 1)
                for t in range(NT + 1):
                    if t == NT // 2:
                        decayed_keys(1)
                        for n in (5, 7):
                            take_inverse(dve, n)
                    if t < NT:
                        take_uw(dve, t)
                    if t == 3 * NT // 4:
                        part_keys(dve, 0)
                    if t:
                        i = t - 1
                        dve.wait_ge(wq_mm, i + 1)
                        for par in range(2):
                            src = ps[:, 6 + i % 2, 0:256].rearrange("p (a b x) -> p a b x", a=2, b=B)[:, :, :, DH * par:DH * par + DH]
                            ins = dve.tensor_copy(wq_t5[:, i, :, par, :, DH * (1 - par):DH * (1 - par) + DH], src)
                        ins.then_inc(wq_dve, 1)
                    if t < NT // 2:
                        for i in (range(1, 8), (8, 9))[t] if t < 2 else (8 + t,):
                            inverse_row(1, i)
                part_keys(dve, 1)
                dve.wait_ge(uw_out[0], NT)
                dve.wait_ge(uw_out[1], NT)

                def combine(t):
                    dve.wait_ge(cb_act, t + 1)
                    for w, dst in enumerate((u_tok, comb_qs)):
                        ins = dve.scalar_tensor_tensor(out=dst[:, t, :], in0=xo[:, (2 * t + 1) % 4, :], scalar=half_mask[:, 1 - w:2 - w],
                                                       in1=comb_a[:, t % 2, w], op0=ALU.mult, op1=ALU.add)
                    ins.then_inc(comb_ok, 1)

                for n in range(2 * NT):
                    t, par = divmod(n, 2)
                    for g in range(2):
                        own = slice(64 * g, 64 * g + 64)
                        dve.wait_ge(r_mm[g], n + 1)
                        if t >= 2:
                            dve.wait_ge(comb_ok, t - 1)
                        dve.scalar_tensor_tensor(out=xo[own, n % 4, :].rearrange("p (r x) -> p r x", r=4),
                                                 in0=u_tok[own, t, :].rearrange("p (r x) -> p r x", r=4),
                                                 scalar=half_mask[own, par:par + 1], in1=ps[own, 0:4, 0:64], op0=ALU.mult, op1=ALU.add
                                                 ).then_inc(xo_ok[g], 1)
                    if n and not par:
                        combine(t - 1)
                    for g in range(2) if n < 2 * NT - 1 else ():
                        bs = slice(2 * g, 2 * g + 2)
                        dve.wait_ge(s_mm[g], n + 1)
                        dve.wait_ge(sg_ok[g], n + 1)
                        for a_half in range(2):
                            ins = dve.scalar_tensor_tensor(
                                out=state[:, bs, a_half].rearrange("p b e x -> p b (e x)"), in0=ps[:, 4 + 2 * g:6 + 2 * g, 32 * a_half:32 * a_half + 32],
                                scalar=half_mask[:, a_half:a_half + 1], in1=s_dec[:, bs, a_half].rearrange("p b e x -> p b (e x)"),
                                op0=ALU.mult, op1=ALU.add)
                        ins.then_inc(s_ok[g], 1)
                dve.wait_ge(xo_ok[0], 2 * NT)
                dve.wait_ge(xo_ok[1], 2 * NT)
                combine(NT - 1)
                ms = small[0]
                for half in range(2):
                    tiles = range(NT // 2 * half, NT // 2 * (half + 1))
                    part_ms, part_r = ms[:, tiles[0]:tiles[-1] + 1], q1[:, tiles[0]:tiles[-1] + 1]
                    for t in tiles:
                        dve.wait_ge(o_out, t + 1)
                        step(dve.tensor_tensor(sq[:, 0:D], o_tok[:, t, :], o_tok[:, t, :], ALU.mult))
                        step(dve.tensor_reduce(ms[:, t, :], sq[:, 0:D].rearrange("p (h d) -> p h d", d=DH), AX.X, ALU.add))
                    dve.tensor_scalar(part_ms, part_ms, 1.0 / DH, 1e-6, ALU.mult, ALU.add).then_inc(rms_ss, 1)
                    dve.wait_ge(rms_rt, half + 1)
                    step(dve.reciprocal(part_r, part_ms))
                    dve.wait_ge(gate_ok, 1)
                    for t in tiles:
                        o = o_tok[:, t, :].rearrange("p (h d) -> p h d", d=DH)
                        step(dve.tensor_tensor(o, o, q1[:, t, :].unsqueeze(2).broadcast_to([P, NH, DH]), ALU.mult))
                        dve.tensor_tensor(o_tok[:, t, :], o_tok[:, t, :], gate[:, t, :], ALU.mult).then_inc(og_ok, 1)
                for n in range(NT):
                    j = out_tile(n)
                    dve.wait_ge(wo_mm, n + 1)
                    dve.tensor_tensor(h_res[:, j, :], ps[:, wo_bank(n), 0:D], h_res[:, j, :], ALU.add).then_inc(attn_add, 1)
                    dve.wait_ge(attn_add, n + 1)
                    ln_stats(j)
                    if n:
                        ln_apply(3, n - 1, out_tile(n - 1))
                ln_apply(3, NT - 1, out_tile(NT - 1))
            if stop >= 4:

                def over(v, n=NE):
                    return v.unsqueeze(2).broadcast_to([P, NT, n])

                def each(v, n=NT):
                    return v.unsqueeze(1).broadcast_to([P, n, NE])

                dve.wait_ge(lg_mm, 1)
                step(dve.tensor_tensor(lg, ps[:, 0, 0:NT * NE].rearrange("p (j e) -> p j e", e=NE), each(rb), ALU.add))
                step(dve.tensor_reduce(lmax, lg, AX.X, ALU.max))
                dve.tensor_tensor(lexp, lg, over(lmax), ALU.subtract).then_inc(sh_ok, 1)
                step(dve.tensor_tensor(eq, lg, over(lmax), ALU.is_ge))
                step(dve.tensor_tensor(eq, eq, each(em8), ALU.mult))
                step(dve.tensor_reduce(pos, eq, AX.X, ALU.min))
                dve.tensor_tensor(onehot, each(em8), over(pos), ALU.is_equal).then_inc(hot_ok, 1)
                dve.wait_ge(lexp_ok, 1)
                step(dve.tensor_reduce(pmax, lexp, AX.X, ALU.add))
                step(dve.reciprocal(pmax, pmax))
                dve.wait_ge(cnt_mm, 1)
                totals = ps[:, 2, 0:NT * NE].rearrange("p (j e) -> p j e", e=NE)
                step(dve.tensor_copy(cnt[:, 0], totals))
                src, w = 0, 1
                while w < NT:
                    step(dve.tensor_copy(cnt[:, 1 - src, 0:w], cnt[:, src, 0:w]))
                    step(dve.tensor_tensor(cnt[:, 1 - src, w:NT], cnt[:, src, w:NT], cnt[:, src, 0:NT - w], ALU.add))
                    src, w = 1 - src, 2 * w
                step(dve.tensor_tensor(cmp_[:, 0:NE], cnt[:, src, NT - 1].unsqueeze(2).broadcast_to([P, NE, NE]), each(thr, NE), ALU.is_gt))
                step(dve.tensor_reduce(ends[:, 0], cmp_[:, 0:NE], AX.X, ALU.add))
                step(dve.tensor_copy(ends[:, 2], ends[:, 0]))
                at_, w = 0, 1
                while w < NE:
                    step(dve.tensor_copy(ends[:, 1 - at_, 0:w], ends[:, at_, 0:w]))
                    step(dve.tensor_tensor(ends[:, 1 - at_, w:NE], ends[:, at_, w:NE], ends[:, at_, 0:NE - w], ALU.add))
                    at_, w = 1 - at_, 2 * w
                step(dve.tensor_tensor(base, ends[:, at_], ends[:, 2], ALU.subtract))
                step(dve.tensor_scalar(base, base, float(ET), None, ALU.mult))
                step(dve.tensor_tensor(cmp_, each(ends[:, at_], NET), tile_no.unsqueeze(2).broadcast_to([P, NET, NE]), ALU.is_le))
                step(dve.tensor_reduce(te[:, 0:NET], cmp_, AX.X, ALU.add))
                step(dve.tensor_scalar(te_i[:, 0:NET], te[:, 0:NET], float(NE - 1), None, ALU.min))
                step(dve.tensor_tensor(cnt[:, 2], cnt[:, src], totals, ALU.subtract))
                step(dve.tensor_tensor(cnt[:, 2], ps[:, 1, 0:NT * NE].rearrange("p (j e) -> p j e", e=NE), cnt[:, 2], ALU.add))
                step(dve.tensor_tensor(cnt[:, 2], cnt[:, 2], each(base), ALU.add))
                step(dve.tensor_tensor(cnt[:, 2], cnt[:, 2], onehot, ALU.mult))
                step(dve.tensor_reduce(pos, cnt[:, 2], AX.X, ALU.add))
                dve.tensor_copy(pos_i, pos).then_inc(pos_ok, 1)

                def expert(t, slot, first):
                    for m in range(HC):
                        dve.wait_ge(e_silu, t * HC + m + 1)
                        if m == 0 and not first:
                            dve.wait_ge(e2_mm, t - 1)
                        dve.tensor_tensor(eu[:, slot, m, :], ps[:, m % 4, ET:2 * ET], silu[:, m % 2], ALU.mult).then_inc(e1_out, 1)
                    dve.wait_ge(e2_mm, t + 1)
                    if not first:
                        dve.wait_ge(d_ys[slot], t * 8 if slot == 0 else t * 8 - 8)
                    dve.tensor_copy(ys[:, slot], ps[:, 4:6, 0:D]).then_inc(e2_out, 1)

                expert_tiles(dve, expert)
                for j in range(NT):
                    if j % 4 == 0:
                        dve.wait_ge(d_yg[j // 4], 64)
                    dve.scalar_tensor_tensor(out=h_res[:, j, :], in0=yg[:, j, :], scalar=pmax[:, j:j + 1], in1=h_res[:, j, :],
                                             op0=ALU.mult, op1=ALU.add).then_inc(fin, 1)


def delta_constants():
    p, c = np.arange(P)[:, None], np.arange(P)[None]
    half = p % 32 // DH
    cols = [half == np.arange(2)[None], np.tile(np.eye(DH).reshape(1, -1), (P, 1)), half == c[:, :32] // DH,
            (p // 32 == c // 32) & ((p + DH) % 32 == c % 32)]
    cols += [p % NH == 8 * hh + c // DH for hh in range(2)] + [p // NH == np.arange(8)[None]]
    return np.concatenate([np.asarray(x, np.float32) for x in cols], axis=1)


def kernel(**inputs):
    import concourse.bacc as bacc
    from concourse import mybir as _mybir
    from concourse.bass_utils import run_bass_kernel_spmd

    n = {name: np.asarray(v) for name, v in inputs.items()}
    x = n["x"].reshape(B, 2, P, 2, D, TOK_D)
    arrays = {
        "x_t": x.transpose(5, 4, 0, 1, 3, 2).reshape(TOK_D * D, B * S),
        "tok_ws_t": n["L0_tok_weighted_sum"].T,
        "tok_w_t": n["L0_tok_weight"].T,
        "keys_t": n["L0_attn_keys"][0].T,
        "vals_t": n["L0_attn_values"][0].T,
        "wq_t": n["L0_attn_Wq_w"].T,
        "wk_t": n["L0_attn_Wk_w"].T,
        "wv_t": n["L0_attn_Wv_w"].T,
        "bias_qk": np.stack([n["L0_attn_Wq_b"], n["L0_attn_Wk_b"]]).reshape(2, FC, P).transpose(2, 0, 1),
        "bias_v": n["L0_attn_Wv_b"][None],
        "w1_t": n["L0_ffn_w1"].T,
        "w2_t": n["L0_ffn_w2"].T,
        "b1": n["L0_ffn_b1"].reshape(HC, P).T,
        "b2": n["L0_ffn_b2"][None],
        "w_cat": np.concatenate([n["L1_attn_" + w] for w in ("Wk", "Wq", "Wv", "Wgate", "Walpha", "Wbeta")], axis=1),
        "w_out": n["L1_attn_Wout"],
        "dt_bias": n["L1_attn_dt_bias"][None],
        "a_log": n["L1_attn_A_log"][None],
        "rms_w": n["L1_attn_rms_w"][None],
        "dconst": delta_constants(),
        "router_w": n["L1_ffn_router_w"],
        "router_b": n["L1_ffn_router_b"][None],
        "ew1": n["L1_ffn_w1"],
        "ew2": n["L1_ffn_w2"],
        "tri": np.triu(np.ones((P, P), np.float32), 1),
        "em8": np.arange(-NE, 0, dtype=np.float32)[None],
        "thr": np.arange(0, NE * ET, ET, dtype=np.float32)[None],
        "tile_no": np.arange(NET, dtype=np.float32)[None],
    }
    arrays = {f"in_{name}": np.ascontiguousarray(v) for name, v in arrays.items()}
    nc = bacc.Bacc("TRN2", target_bir_lowering=False, num_devices=1)
    aps = {name[3:]: nc.dram_tensor(name, v.shape, _mybir.dt.from_np(v.dtype), kind="ExternalInput").ap()
           for name, v in arrays.items()}
    out = nc.dram_tensor("out", [B * S, D], F32, kind="ExternalOutput").ap()
    build(nc, aps, out, STOP)
    r = run_bass_kernel_spmd(nc, [arrays], core_ids=[0])
    return r.results[0]["out"].reshape(B, S, D)
```
